# Optimizing a Trainium2 kernel written in Bass

```python
import numpy as np
import jax
import jax.numpy as jnp

def _softmax(x, axis=-1):
    return jax.nn.softmax(x, axis=axis)

def _gelu(x):
    return jax.nn.gelu(x, approximate=True)

def _silu(x):
    return jax.nn.silu(x)

def _sigmoid(x):
    return jax.nn.sigmoid(x)

def _layernorm(x, axis=-1, eps=1e-05):
    m = jnp.mean(x, axis=axis, keepdims=True)
    v = jnp.var(x, axis=axis, keepdims=True)
    return (x - m) / jnp.sqrt(v + eps)

def _scatter_add(tgt, idx, src, axis=0):
    return tgt.at[idx].add(src)

def _segment_sum(src, seg, n):
    return jax.ops.segment_sum(src, seg, n)
kernel_name = 'mk_gnn_preln_d4_gnn_r32_72e28a'

def setup_inputs(seed: int=0):
    np.random.seed(seed)
    _w = jnp.asarray

    def _rec_inputs():
        import jax
        import jax.numpy as jnp
        _gk = jax.random.key(seed)
        x = -0.0008691 + 1 * jax.random.normal(jax.random.fold_in(_gk, 1), (50000, 128), jnp.float32)
        src = jax.random.randint(jax.random.fold_in(_gk, 2), (50000,), 0, 50000, jnp.int32)
        dst = jax.random.randint(jax.random.fold_in(_gk, 3), (50000,), 0, 50000, jnp.int32)
        _o = jnp.argsort(dst, stable=True)
        src = src[_o]
        dst = dst[_o]
        return (x, src, dst)
    x, src, dst = _rec_inputs()

    def _L0_gnn_setup():
        import jax, jax.numpy as jnp
        import numpy as np
        N_NODES = 10000
        N_EDGES = 20000
        D = 128
        key = jax.random.key(seed)
        ks = jax.random.split(key, 8)
        x = jax.random.normal(ks[0], (N_NODES, D), dtype=jnp.float32)
        edge_index = jax.random.randint(ks[1], (2, N_EDGES), 0, N_NODES, dtype=jnp.int64)
        scale = 1.0 / np.sqrt(D)
        W0 = jax.random.normal(ks[2], (D, D), dtype=jnp.float32) * scale
        b0 = jax.random.normal(ks[3], (D,), dtype=jnp.float32) * scale
        W1 = jax.random.normal(ks[4], (D, D), dtype=jnp.float32) * scale
        b1 = jax.random.normal(ks[5], (D,), dtype=jnp.float32) * scale
        W2 = jax.random.normal(ks[6], (D, D), dtype=jnp.float32) * scale
        b2 = jax.random.normal(ks[7], (D,), dtype=jnp.float32) * scale
        return {'x': x, 'edge_index': edge_index, 'W0': W0, 'b0': b0, 'W1': W1, 'b1': b1, 'W2': W2, 'b2': b2}
    _L0_gnn_all = _L0_gnn_setup()
    _L0_gnn_in = {k: v for k, v in _L0_gnn_all.items() if k in ('W0', 'b0', 'W1', 'b1', 'W2', 'b2')}
    del _L0_gnn_all

    def _L1_gnn_setup():
        import jax, jax.numpy as jnp
        import numpy as np
        N_NODES = 3125
        N_EDGES = 20000
        D_FEAT = 128
        key = jax.random.key(seed)
        k1, k2, k3, k4 = jax.random.split(key, 4)
        x = jax.random.normal(k1, (N_NODES, D_FEAT), dtype=jnp.float32)
        edge_index = jax.random.randint(k2, (2, N_EDGES), 0, N_NODES, dtype=jnp.int64)
        W = jax.random.normal(k3, (D_FEAT, D_FEAT), dtype=jnp.float32) / np.sqrt(D_FEAT)
        W_self = jax.random.normal(k4, (D_FEAT, D_FEAT), dtype=jnp.float32) / np.sqrt(D_FEAT)
        return {'x': x, 'edge_index': edge_index, 'W': W, 'W_self': W_self}
    _L1_gnn_all = _L1_gnn_setup()
    _L1_gnn_in = {k: v for k, v in _L1_gnn_all.items() if k in ('W', 'W_self')}
    del _L1_gnn_all

    def _L2_gnn_setup():
        import jax, jax.numpy as jnp
        import numpy as np
        import math
        DIM = 128
        HEADS = 8
        HC = DIM // HEADS
        N = 50000
        E = 25000
        LEAKY_SLOPE = 0.2

        def _seg_softmax(logits, seg, n):
            m = jax.ops.segment_max(logits, seg, num_segments=n)
            m = jnp.where(jnp.isfinite(m), m, 0.0)
            e = jnp.exp(logits - m[seg])
            s = jax.ops.segment_sum(e, seg, num_segments=n)
            return e / jnp.maximum(s[seg], 1e-16)
        key = jax.random.key(seed)
        ks = jax.random.split(key, 20)
        sc = 1.0 / math.sqrt(DIM)
        inp = {'x': jax.random.normal(ks[0], (N, DIM), jnp.float32), 'edge_index': jax.random.randint(ks[1], (2, E), 0, N, jnp.int64), 'gat_w': jax.random.normal(ks[2], (DIM, DIM), jnp.float32) * sc, 'gat_att_src': jax.random.normal(ks[3], (HEADS, HC), jnp.float32) * sc, 'gat_att_dst': jax.random.normal(ks[4], (HEADS, HC), jnp.float32) * sc, 'gat_b': jnp.zeros((DIM,), jnp.float32), 'sage_wl': jax.random.normal(ks[5], (DIM, DIM), jnp.float32) * sc, 'sage_bl': jnp.zeros((DIM,), jnp.float32), 'sage_wr': jax.random.normal(ks[6], (DIM, DIM), jnp.float32) * sc, 'tr_wq': jax.random.normal(ks[7], (DIM, DIM), jnp.float32) * sc, 'tr_bq': jnp.zeros((DIM,), jnp.float32), 'tr_wk': jax.random.normal(ks[8], (DIM, DIM), jnp.float32) * sc, 'tr_bk': jnp.zeros((DIM,), jnp.float32), 'tr_wv': jax.random.normal(ks[9], (DIM, DIM), jnp.float32) * sc, 'tr_bv': jnp.zeros((DIM,), jnp.float32), 'tr_wskip': jax.random.normal(ks[10], (DIM, DIM), jnp.float32) * sc, 'tr_bskip': jnp.zeros((DIM,), jnp.float32), 'fus_w': jax.random.normal(ks[11], (3 * DIM, DIM), jnp.float32) * (1.0 / math.sqrt(3 * DIM)), 'fus_b': jnp.zeros((DIM,), jnp.float32), 'ln_g': jnp.ones((DIM,), jnp.float32), 'ln_b': jnp.zeros((DIM,), jnp.float32)}
        return inp
    _L2_gnn_all = _L2_gnn_setup()
    _L2_gnn_in = {k: v for k, v in _L2_gnn_all.items() if k in ('gat_w', 'gat_att_src', 'gat_att_dst', 'gat_b', 'sage_wl', 'sage_bl', 'sage_wr', 'tr_wq', 'tr_bq', 'tr_wk', 'tr_bk', 'tr_wv', 'tr_bv', 'tr_wskip', 'tr_bskip', 'fus_w', 'fus_b', 'ln_g', 'ln_b')}
    del _L2_gnn_all

    def _L3_gnn_setup():
        import jax, jax.numpy as jnp
        import numpy as np
        N = 3125
        E = 50000
        D_IN = 128
        D_H = 128
        D_OUT = 128
        key = jax.random.key(seed)
        ks = jax.random.split(key, 11)
        x = jax.random.normal(ks[0], (N, D_IN), dtype=jnp.float32)
        edge_index = jax.random.randint(ks[1], (2, E), 0, N, dtype=jnp.int32)
        s_in = 1.0 / np.sqrt(D_IN)
        s_h = 1.0 / np.sqrt(D_H)
        return {'x': x, 'edge_index': edge_index, 'W_neigh1': jax.random.uniform(ks[2], (D_H, D_IN), jnp.float32, -s_in, s_in), 'b_neigh1': jax.random.uniform(ks[3], (D_H,), jnp.float32, -s_in, s_in), 'W_self1': jax.random.uniform(ks[4], (D_H, D_IN), jnp.float32, -s_in, s_in), 'b_self1': jax.random.uniform(ks[5], (D_H,), jnp.float32, -s_in, s_in), 'W_neigh2': jax.random.uniform(ks[6], (D_OUT, D_H), jnp.float32, -s_h, s_h), 'b_neigh2': jax.random.uniform(ks[7], (D_OUT,), jnp.float32, -s_h, s_h), 'W_self2': jax.random.uniform(ks[8], (D_OUT, D_H), jnp.float32, -s_h, s_h), 'b_self2': jax.random.uniform(ks[9], (D_OUT,), jnp.float32, -s_h, s_h)}
    _L3_gnn_all = _L3_gnn_setup()
    _L3_gnn_in = {k: v for k, v in _L3_gnn_all.items() if k in ('W_neigh1', 'b_neigh1', 'W_self1', 'b_self1', 'W_neigh2', 'b_neigh2', 'W_self2', 'b_self2')}
    del _L3_gnn_all
    return {'x': x, 'src': src, 'dst': dst, 'L0_gnn_W0': _L0_gnn_in['W0'], 'L0_gnn_b0': _L0_gnn_in['b0'], 'L0_gnn_W1': _L0_gnn_in['W1'], 'L0_gnn_b1': _L0_gnn_in['b1'], 'L0_gnn_W2': _L0_gnn_in['W2'], 'L0_gnn_b2': _L0_gnn_in['b2'], 'L1_gnn_W': _L1_gnn_in['W'], 'L1_gnn_W_self': _L1_gnn_in['W_self'], 'L2_gnn_gat_w': _L2_gnn_in['gat_w'], 'L2_gnn_gat_att_src': _L2_gnn_in['gat_att_src'], 'L2_gnn_gat_att_dst': _L2_gnn_in['gat_att_dst'], 'L2_gnn_gat_b': _L2_gnn_in['gat_b'], 'L2_gnn_sage_wl': _L2_gnn_in['sage_wl'], 'L2_gnn_sage_bl': _L2_gnn_in['sage_bl'], 'L2_gnn_sage_wr': _L2_gnn_in['sage_wr'], 'L2_gnn_tr_wq': _L2_gnn_in['tr_wq'], 'L2_gnn_tr_bq': _L2_gnn_in['tr_bq'], 'L2_gnn_tr_wk': _L2_gnn_in['tr_wk'], 'L2_gnn_tr_bk': _L2_gnn_in['tr_bk'], 'L2_gnn_tr_wv': _L2_gnn_in['tr_wv'], 'L2_gnn_tr_bv': _L2_gnn_in['tr_bv'], 'L2_gnn_tr_wskip': _L2_gnn_in['tr_wskip'], 'L2_gnn_tr_bskip': _L2_gnn_in['tr_bskip'], 'L2_gnn_fus_w': _L2_gnn_in['fus_w'], 'L2_gnn_fus_b': _L2_gnn_in['fus_b'], 'L2_gnn_ln_g': _L2_gnn_in['ln_g'], 'L2_gnn_ln_b': _L2_gnn_in['ln_b'], 'L3_gnn_W_neigh1': _L3_gnn_in['W_neigh1'], 'L3_gnn_b_neigh1': _L3_gnn_in['b_neigh1'], 'L3_gnn_W_self1': _L3_gnn_in['W_self1'], 'L3_gnn_b_self1': _L3_gnn_in['b_self1'], 'L3_gnn_W_neigh2': _L3_gnn_in['W_neigh2'], 'L3_gnn_b_neigh2': _L3_gnn_in['b_neigh2'], 'L3_gnn_W_self2': _L3_gnn_in['W_self2'], 'L3_gnn_b_self2': _L3_gnn_in['b_self2']}

def reference(x, src, dst, L0_gnn_W0, L0_gnn_b0, L0_gnn_W1, L0_gnn_b1, L0_gnn_W2, L0_gnn_b2, L1_gnn_W, L1_gnn_W_self, L2_gnn_gat_w, L2_gnn_gat_att_src, L2_gnn_gat_att_dst, L2_gnn_gat_b, L2_gnn_sage_wl, L2_gnn_sage_bl, L2_gnn_sage_wr, L2_gnn_tr_wq, L2_gnn_tr_bq, L2_gnn_tr_wk, L2_gnn_tr_bk, L2_gnn_tr_wv, L2_gnn_tr_bv, L2_gnn_tr_wskip, L2_gnn_tr_bskip, L2_gnn_fus_w, L2_gnn_fus_b, L2_gnn_ln_g, L2_gnn_ln_b, L3_gnn_W_neigh1, L3_gnn_b_neigh1, L3_gnn_W_self1, L3_gnn_b_self1, L3_gnn_W_neigh2, L3_gnn_b_neigh2, L3_gnn_W_self2, L3_gnn_b_self2):
    import jax
    import jax.numpy as jnp

    def _L0_gnn_ref(x, edge_index, W0, b0, W1, b1, W2, b2):
        import jax, jax.numpy as jnp
        import numpy as np
        N_NODES = 10000
        N_EDGES = 20000
        D = 128
        n = x.shape[0]
        sl = jnp.arange(n, dtype=edge_index.dtype)
        ei = jnp.concatenate([edge_index, jnp.stack([sl, sl])], axis=1)
        row, col = (ei[0], ei[1])
        deg = jax.ops.segment_sum(jnp.ones(row.shape[0], x.dtype), col, num_segments=n)
        dinv = jnp.where(deg > 0, deg ** (-0.5), 0.0)
        norm = (dinv[row] * dinv[col])[:, None]
        for W, b in ((W0, b0), (W1, b1), (W2, b2)):
            h = jax.nn.relu(x @ W + b)
            msg = norm * h[row]
            x = jax.ops.segment_sum(msg, col, num_segments=n)
        return x

    def _L1_gnn_ref(x, edge_index, W, W_self):
        import jax, jax.numpy as jnp
        import numpy as np
        N_NODES = 3125
        N_EDGES = 20000
        D_FEAT = 128
        src = edge_index[0]
        tgt = edge_index[1]
        messages = jnp.take(x, src, axis=0) @ W
        aggr_out = jax.ops.segment_sum(messages, tgt, num_segments=x.shape[0])
        return aggr_out + x @ W_self

    def _L2_gnn_ref(x, edge_index, gat_w, gat_att_src, gat_att_dst, gat_b, sage_wl, sage_bl, sage_wr, tr_wq, tr_bq, tr_wk, tr_bk, tr_wv, tr_bv, tr_wskip, tr_bskip, fus_w, fus_b, ln_g, ln_b):
        import jax, jax.numpy as jnp
        import numpy as np
        import math
        DIM = 128
        HEADS = 8
        HC = DIM // HEADS
        N = 50000
        E = 25000
        LEAKY_SLOPE = 0.2

        def _seg_softmax(logits, seg, n):
            m = jax.ops.segment_max(logits, seg, num_segments=n)
            m = jnp.where(jnp.isfinite(m), m, 0.0)
            e = jnp.exp(logits - m[seg])
            s = jax.ops.segment_sum(e, seg, num_segments=n)
            return e / jnp.maximum(s[seg], 1e-16)
        n = x.shape[0]
        src, dst = (edge_index[0], edge_index[1])
        loop = jnp.arange(n, dtype=src.dtype)
        s2 = jnp.concatenate([src, loop])
        d2 = jnp.concatenate([dst, loop])
        h = (x @ gat_w).reshape(n, HEADS, HC)
        a_src = (h * gat_att_src).sum(-1)
        a_dst = (h * gat_att_dst).sum(-1)
        logits = jax.nn.leaky_relu(a_src[s2] + a_dst[d2], LEAKY_SLOPE)
        alpha = _seg_softmax(logits, d2, n)
        gat_out = jax.ops.segment_sum(alpha[:, :, None] * h[s2], d2, num_segments=n).reshape(n, DIM) + gat_b
        ones = jnp.ones(src.shape, x.dtype)
        deg = jax.ops.segment_sum(ones, dst, num_segments=n)
        nbr = jax.ops.segment_sum(x[src], dst, num_segments=n) / jnp.maximum(deg, 1.0)[:, None]
        sage_out = nbr @ sage_wl + sage_bl + x @ sage_wr
        sage_out = sage_out / jnp.maximum(jnp.linalg.norm(sage_out, axis=-1, keepdims=True), 1e-12)
        q = (x @ tr_wq + tr_bq).reshape(n, HEADS, HC)
        k = (x @ tr_wk + tr_bk).reshape(n, HEADS, HC)
        v = (x @ tr_wv + tr_bv).reshape(n, HEADS, HC)
        t_logits = (q[dst] * k[src]).sum(-1) / math.sqrt(HC)
        t_alpha = _seg_softmax(t_logits, dst, n)
        tr_out = jax.ops.segment_sum(t_alpha[:, :, None] * v[src], dst, num_segments=n).reshape(n, DIM)
        tr_out = tr_out + x @ tr_wskip + tr_bskip
        concat = jnp.concatenate([gat_out, sage_out, tr_out], axis=-1)
        out = concat @ fus_w + fus_b
        mu = out.mean(-1, keepdims=True)
        var = ((out - mu) ** 2).mean(-1, keepdims=True)
        return (out - mu) / jnp.sqrt(var + 1e-05) * ln_g + ln_b

    def _L3_gnn_ref(x, edge_index, W_neigh1, b_neigh1, W_self1, b_self1, W_neigh2, b_neigh2, W_self2, b_self2):
        import jax, jax.numpy as jnp
        import numpy as np
        N = 3125
        E = 50000
        D_IN = 128
        D_H = 128
        D_OUT = 128
        src, dst = (edge_index[0], edge_index[1])
        n = x.shape[0]
        deg = jax.ops.segment_sum(jnp.ones(src.shape[0], x.dtype), dst, num_segments=n)
        inv_deg = 1.0 / jnp.maximum(deg, 1.0)

        def agg(h):
            return jax.ops.segment_sum(h[src], dst, num_segments=n) * inv_deg[:, None]
        h1 = agg(x) @ W_neigh1.T + b_neigh1 + x @ W_self1.T + b_self1
        h1 = jax.nn.relu(h1)
        h2 = agg(h1) @ W_neigh2.T + b_neigh2 + h1 @ W_self2.T + b_self2
        return h2
    edge_index = jnp.stack([src, dst])
    h = jnp.maximum(_layernorm(x, axis=-1), 0.0)
    x = x + _L0_gnn_ref(h, edge_index, L0_gnn_W0, L0_gnn_b0, L0_gnn_W1, L0_gnn_b1, L0_gnn_W2, L0_gnn_b2)
    h = jnp.maximum(_layernorm(x, axis=-1), 0.0)
    x = x + _L1_gnn_ref(h, edge_index, L1_gnn_W, L1_gnn_W_self)
    h = jnp.maximum(_layernorm(x, axis=-1), 0.0)
    x = x + _L2_gnn_ref(h, edge_index, L2_gnn_gat_w, L2_gnn_gat_att_src, L2_gnn_gat_att_dst, L2_gnn_gat_b, L2_gnn_sage_wl, L2_gnn_sage_bl, L2_gnn_sage_wr, L2_gnn_tr_wq, L2_gnn_tr_bq, L2_gnn_tr_wk, L2_gnn_tr_bk, L2_gnn_tr_wv, L2_gnn_tr_bv, L2_gnn_tr_wskip, L2_gnn_tr_bskip, L2_gnn_fus_w, L2_gnn_fus_b, L2_gnn_ln_g, L2_gnn_ln_b)
    h = jnp.maximum(_layernorm(x, axis=-1), 0.0)
    x = x + _L3_gnn_ref(h, edge_index, L3_gnn_W_neigh1, L3_gnn_b_neigh1, L3_gnn_W_self1, L3_gnn_b_self1, L3_gnn_W_neigh2, L3_gnn_b_neigh2, L3_gnn_W_self2, L3_gnn_b_self2)
    return x

_drawn_inputs = setup_inputs


def setup_inputs(seed=0):
    import zlib

    import numpy as np

    out = dict(_drawn_inputs(seed))
    spreads = {'L2_gnn_gat_b': (0.0, 0.1),
     'L2_gnn_sage_bl': (0.0, 0.8),
     'L2_gnn_tr_bq': (0.0, 2.0),
     'L2_gnn_tr_bk': (0.0, 2.0),
     'L2_gnn_tr_bv': (0.0, 0.1),
     'L2_gnn_tr_bskip': (0.0, 0.1),
     'L2_gnn_fus_b': (0.0, 0.1),
     'L2_gnn_ln_g': (1.0, 0.2),
     'L2_gnn_ln_b': (0.0, 0.1)}
    factors = {'L2_gnn_gat_att_src': 3.434,
     'L2_gnn_gat_att_dst': 21.4,
     'L3_gnn_b_neigh1': 4.019,
     'L3_gnn_b_self1': 3.531,
     'L2_gnn_sage_wl': 3.102}
    for name, (base, spread) in spreads.items():
        noise = np.random.default_rng([zlib.crc32(name.encode()), seed]).standard_normal(out[name].shape)
        drawn = base * np.exp(spread * noise) if base else spread * noise
        out[name] = jnp.asarray(drawn.astype(out[name].dtype))
    for name, factor in factors.items():
        out[name] = (out[name] * factor).astype(out[name].dtype)
    return out
```

```python
from contextlib import ExitStack, contextmanager

import numpy as np

import concourse.bass as bass
from concourse import mybir

P = 128
D = 128
N = 50000
E = 50000
HEADS = 8
HC = D // HEADS
QUAD = 4
BODY = 4
COLS = 400
TURNS = COLS // (QUAD * BODY)
NQ = COLS // QUAD
STEP = QUAD * BODY
ROWS = P * COLS
QA = D + 2 * HEADS
SW = 3 * D + 4 * HEADS
R_, X_, M_, S_ = 0, 2 * D, 3 * D, 3 * D + 2 * HEADS
PROJ = 3 * D + HEADS
NEG = -1.0e30
EPS = 1e-5

MATS = ["W0", "W1", "W2", "L1_W", "L1_Wself", "gat_w", "gat_wT", "sage_wl", "sage_wr", "wq", "wqT", "wk",
        "wv", "wskipT", "F1", "F2", "F3", "Wn1T", "Ws1T", "Wn2T", "Ws2T", "gat_b_col", "bskip_col",
        "bv_col", "bq_col"]
VECS = ["b0", "b1", "b2", "sage_bl", "bq", "fus_b", "ln_g", "ln_b", "bn1", "bs1", "bn2", "bs2"]

PHASES = [("in", None), ("edge", "g0"), ("gcn", 1), ("edge", "g1"), ("gcn", 2), ("edge", "g2"), ("gcn_out", None),
          ("edge", "h1"), ("conv", None), ("attend", "h2"), ("fuse", None), ("edge", "h3"), ("sage1", None),
          ("edge", "h4"), ("sage2", None)]

COUNTS = {
    "idx": dict(edge=1, gcn=1, gcn_out=1, conv=1, attend=1, fuse=1, sage1=1, sage2=1),
    "idx2": dict(attend=1),
    "summed": dict(edge=4),
    "agg_steps": dict(gcn=1, gcn_out=2),
    "norm_steps": {"in": 4, "gcn_out": 4, "conv": 4, "fuse": 4}, "norm_steps2": dict(fuse=4),
    "stats2": dict(fuse=1), "rstd2": dict(fuse=1), "shift2": dict(fuse=1), "rstd_steps2": dict(fuse=1),
    "front_steps0": dict(attend=7), "front_steps1": dict(attend=7),
    "back_steps0": dict(attend=10), "back_steps1": dict(attend=9),
    "self_steps": dict(fuse=3), "blend_steps": dict(fuse=7), "fuse_steps": dict(fuse=4), "x3_steps": dict(fuse=2),
    "rstd_steps": {"in": 1, "gcn_out": 1, "conv": 1, "fuse": 1}, "sage_log": dict(fuse=1),
    "agg_ready": dict(gcn=1, fuse=1, sage1=1, sage2=1),
    "transposed": {"in": 1, "gcn": 1, "conv": 1, "attend": 1, "fuse": 1, "sage1": 1, "sage2": 1},
    "own_transposed": dict(conv=1, fuse=1, sage1=1, sage2=1),
    "xt_ready": {"in": 1, "gcn": 1, "conv": 1, "attend": 1, "fuse": 1, "sage1": 1, "sage2": 1},
    "xu_ready": dict(conv=1, fuse=1, sage1=1, sage2=1),
    "product": {"in": 1, "gcn": 1, "conv": 1, "fuse": 1, "sage1": 1, "sage2": 1},
    "biased": {"in": 1, "gcn": 1, "sage1": 1, "sage2": 1},
    "out_ready": {"in": 1, "gcn": 1, "sage1": 1, "sage2": 1},
    "x_ready": dict(gcn_out=1, conv=1, fuse=1),
    "stats": {"in": 1, "gcn_out": 1, "conv": 1, "fuse": 1},
    "rstd": {"in": 1, "gcn_out": 1, "conv": 1, "fuse": 1},
    "shift": {"in": 1, "gcn_out": 1, "conv": 1, "fuse": 1},
    "h_ready": {"in": 1, "gcn_out": 1, "conv": 1, "fuse": 1},
    "h_transposed": dict(conv=1),
    "ht_ready": dict(conv=1),
    "qa_product": dict(conv=1),
    "qa_ready": dict(conv=1),
    "proj0": dict(attend=1), "proj1": dict(attend=1),
    "gaps0": dict(attend=1), "gaps1": dict(attend=1),
    "exps0": dict(attend=1), "exps1": dict(attend=1),
    "proj_used0": dict(attend=1), "proj_used1": dict(attend=1),
    "state_ready": dict(attend=1),
    "self_product": dict(fuse=1), "self_used": dict(fuse=1),
    "self_gaps": dict(fuse=1), "self_exps": dict(fuse=1),
    "sage_biased": dict(fuse=1), "sage_squares": dict(fuse=4), "sage_floor": dict(fuse=1), "sage_norm": dict(fuse=1),
    "gat_ready": dict(fuse=1), "tr_ready": dict(fuse=1), "sage_ready": dict(fuse=1),
    "parts_transposed": dict(fuse=3), "parts_ready": dict(fuse=3),
    "fused": dict(fuse=1), "fused_used": dict(fuse=1), "normed": dict(fuse=1),
}
GATHERS = dict(edge=64, gcn=64, gcn_out=64, conv=64, attend=128, fuse=64, sage1=64, sage2=64)
LOADS = {"in": 16, "gcn": 16, "gcn_out": 32, "conv": 32, "fuse": 32, "sage1": 16, "sage2": 32}
STORES = {"in": 16, "edge": 16, "gcn": 16, "gcn_out": 32, "conv": 48, "attend": 16, "fuse": 32, "sage1": 16,
          "sage2": 16}
CREDIT = 10 * BODY


def before(name, f):
    c = COUNTS[name]
    extra = BODY if name in ("idx", "idx2") else 0
    return CREDIT + sum(c[k] * (NQ + 0) + extra for k, _ in PHASES[:f] if k in c)


def before_slot(table, f):
    return (16 if table is STORES else 0) + TURNS * sum(table.get(k, 0) for k, _ in PHASES[:f])


def gnn_kernel(nc, a, out):
    f32, f16, i32 = mybir.dt.float32, mybir.dt.float16, mybir.dt.int32
    ALU, ACT, AX = mybir.AluOpType, mybir.ActivationFunctionType, mybir.AxisListType
    ctx = ExitStack()

    def sb(name, shape, dt=f32):
        return ctx.enter_context(nc.sbuf_tensor(name, shape, dt))

    def sem(name):
        return ctx.enter_context(nc.semaphore(name))

    def dram(name, rows, width):
        return nc.dram_tensor(name, (rows, width), f32).ap()

    with ctx:
        tab = {n: dram("tab_" + n, ROWS, D) for n in ("g0", "g1", "g2", "h1", "h2", "h3", "h4")}
        tab_qa = dram("tab_qa", ROWS, QA)
        res = {n: dram("res_" + n, ROWS, D) for n in ("x1", "x2", "x3")}
        sums = dram("sums", ROWS + P, D)
        states = dram("states", ROWS + P, SW)

        def cols(t):
            return t[0:ROWS, :].rearrange("(p c) f -> p c f", c=COLS)

        mats = sb("mats", [P, len(MATS), D])
        vecs = sb("vecs", [P, len(VECS), D])
        ident = sb("ident", [P, P])
        upper = sb("upper", [P, P])
        lower = sb("lower", [P, P])
        hmask = sb("hmask", [P, HEADS])
        attc = sb("attc", [P, 3])
        ones = sb("ones", [P, P])
        zero16 = sb("zero16", [P, P], f16)
        iota = sb("iota", [P, COLS], f16)
        emptyrow = sb("emptyrow", [P, 1])
        firstrow = sb("firstrow", [P, 1])
        eps = sb("eps", [P, 1])
        src_i = sb("src_i", [P, COLS + STEP], i32)
        dst_i = sb("dst_i", [P, COLS + STEP], i32)
        last_i = sb("last_i", [P, COLS + STEP], i32)
        dst = sb("dst", [P, COLS])
        same = sb("same", [P, COLS])
        gapneg = sb("gapneg", [P, COLS])
        dinv = sb("dinv", [P, COLS])
        invdeg = sb("invdeg", [P, COLS])
        has = sb("has", [P, COLS])
        stage = sb("stage", [P, STEP], i32)
        stage2 = sb("stage2", [P, STEP], i32)
        carry_mask = sb("carry_mask", [P, P])
        carry_maskT = sb("carry_maskT", [P, P])
        first_end = sb("first_end", [P, 1], i32)
        carry = sb("carry", [P, D])

        G = sb("G", [P, STEP, D])
        L1 = sb("L1", [P, STEP, D])
        L2 = sb("L2", [P, STEP, D])
        O1 = sb("O1", [P, STEP, D])
        O2 = sb("O2", [P, STEP, D])
        ST = sb("ST", [P, STEP, SW])
        QG = sb("QG", [P, STEP, QA])
        XT = sb("XT", [P, 2, QUAD * D])
        XU = sb("XU", [P, BODY, QUAD * D])
        XV = sb("XV", [P, 3, QUAD * D])
        bst = sb("bst", [P, 2, QUAD, 6])
        mv = sb("mv", [P, 2, QUAD, 2])
        rs = sb("rs", [P, 2, 2, QUAD])
        nm = sb("nm", [P, 2, QUAD])
        bst2 = sb("bst2", [P, 2, QUAD, 6])
        mv2 = sb("mv2", [P, 2, QUAD, 2])
        rs2 = sb("rs2", [P, 2, 2, QUAD])
        nm2 = sb("nm2", [P, 2, QUAD])
        WE = sb("WE", [P, PROJ])
        WQA = sb("WQA", [P, QA])
        BQA = sb("BQA", [P, QA])
        WSELF = sb("WSELF", [P, D + HEADS])
        WS3 = sb("WS3", [P, D])
        c0 = sb("c0", [P, D])
        c1 = sb("c1", [P, D])
        bsum = sb("bsum", [P, 2, D])
        blk = sb("blk", [P, 4, HEADS])
        oh_hi = sb("oh_hi", [P, 16, P], f16)
        oh_lo = sb("oh_lo", [P, 16, COLS], f16)
        prod = sb("prod", [P, 2, 2, D])
        red = sb("red", [P, 2, 2, HEADS])
        asum = sb("asum", [P, 2, 2, HEADS])
        lg = sb("lg", [P, 2, 2, 2 * HEADS])
        gaps = sb("gaps", [P, 2, 2, 4 * HEADS])
        exps = sb("exps", [P, 2, 2, 4 * HEADS])
        tmp = sb("tmp", [P, 2, 2 * D])
        sage = sb("sage", [P, 2, QUAD, D])
        hself = sb("hself", [P, QUAD, D])
        yv = sb("yv", [P, 2, QUAD, D])
        zn = sb("zn", [P, 2, QUAD, D])
        sq = sb("sq", [P, D])
        ss = sb("ss", [P, 2, 3, QUAD])
        sgap = sb("sgap", [P, 2, QUAD, 2 * HEADS])
        sexp = sb("sexp", [P, 2, QUAD, 2 * HEADS])
        slog = sb("slog", [P, QUAD, HEADS])
        sm = sb("sm", [P, QUAD, HEADS])
        zz = sb("zz", [P, QUAD, 2 * HEADS])
        lnb = sb("lnb", [P, 1])

        t_f = [L1[:, :, :].rearrange("p c f -> p (c f)")[:, k * COLS:(k + 1) * COLS] for k in range(5)]
        t_i = QG[:, :, :].rearrange("p c f -> p (c f)")[:, 0:COLS].bitcast(i32)
        cm = L1[:, :, :].rearrange("p c f -> p (c f)")[:, 0:2 * HEADS * P].rearrange("p (h q) -> p h q", h=2 * HEADS)
        cmT = L2[:, :, :].rearrange("p c f -> p (c f)")[:, 0:2 * HEADS * P].rearrange("p (h q) -> p h q", h=2 * HEADS)
        rsv = O1[:, :, :].rearrange("p c f -> p (c f)")[:, 0:2 * HEADS * (HC + 1)].rearrange(
            "p (h e) -> p h e", h=2 * HEADS)
        fixrow = O2[:, :, :].rearrange("p c f -> p (c f)")[:, 0:SW]
        fixtmp = O2[:, :, :].rearrange("p c f -> p (c f)")[:, 512:512 + SW]
        mc = O2[:, :, :].rearrange("p c f -> p (c f)")[:, 1024:1024 + 6 * 16].rearrange("p (k h) -> p k h", k=6)

        bank = ctx.enter_context(nc.psum_tensor("bank", [P, 8, 512], f32))

        S = {n: sem(n) for n in COUNTS}
        gathered = [sem(f"gathered{b}") for b in range(BODY)]
        loaded = [sem(f"loaded{b}") for b in range(BODY)]
        stored = [sem(f"stored{b}") for b in range(BODY)]
        s_const = sem("constants")
        s_pool = sem("pool_setup")
        s_poolw = sem("pool_waited")
        s_dvew = sem("vector_waited")
        s_spw = sem("sync_waited")
        s_zero = sem("zero_rows")
        s_onehot = sem("onehot")
        s_hist = sem("histogram")
        s_prep = sem("setup_product")
        s_prepd = sem("setup_vector")
        s_dve = sem("vector_step")
        s_act = sem("scalar_step")
        s_carry_p = sem("carry_product")
        s_carry_v = sem("carry_vector")
        s_carry_d = sem("carry_stored")
        s_fixg = sem("fix_gathered")
        s_acarry = sem("carry_weights")
        s_cgap = sem("carry_gaps")
        BLK, DEG, TOTALS, DIAG, SETUP_END = 4, 20, 25, 32, 54

        def mat(name):
            return mats[:, MATS.index(name), :]

        def vec(name):
            return vecs[:, VECS.index(name), :]

        def over_quad(row):
            return row.unsqueeze(1).to_broadcast([P, QUAD, row.shape[-1]])

        def quad(t, b):
            return t[:, QUAD * b:QUAD * (b + 1), :]

        def per_col(t, i, b):
            return t[:, bass.ds(STEP * i + QUAD * b, QUAD)].unsqueeze(2).to_broadcast([P, QUAD, D])

        def reach(name, f, i, b, part=1):
            c = COUNTS[name][PHASES[f][0]]
            return before(name, f) + (i * BODY + b) * c + part

        def freed(name, f, i, b, ring):
            c = COUNTS[name][PHASES[f][0]]
            return before(name, f) + (i * BODY + b - ring + 1) * c

        def slot_done(table, f, i):
            return before_slot(table, f) + table[PHASES[f][0]] * (i + 1)

        def run(eng, f, stages):
            deepest = max(lag for _, lag in stages)
            order = sorted(stages, key=lambda s: -s[1])
            for s in range(BODY):
                for fn, lag in order:
                    if s >= lag:
                        fn(0, s - lag)
            with eng.Fori(1, TURNS) as i:
                for s in range(BODY):
                    for fn, lag in order:
                        fn(i + (s - lag) // BODY, (s - lag) % BODY)
            for s in range(deepest):
                for fn, lag in order:
                    if s < lag:
                        fn(TURNS + (s - lag) // BODY, (s - lag) % BODY)

        consts = [(mats, "mats"), (vecs, "vecs"), (ident, "ident"), (upper, "upper"), (lower, "lower"),
                  (hmask, "hmask"), (attc, "attc"), (iota, "iota"), (emptyrow, "emptyrow"), (firstrow, "firstrow")]

        def kind(f):
            return PHASES[f][0]

        def prior_tiles(b, k):
            return (QUAD * b + k - 1) % STEP

        block = ctx.enter_context(nc.Block())

        @block.sync
        def _(sp):
            for s in S.values():
                sp.sem_inc(s, CREDIT)
            for t, name in consts:
                sp.dma_start(t[:], a[name]).then_inc(s_const, 16)
            sp.dma_start(src_i[:, 0:COLS], a["src"]).then_inc(s_const, 16)
            sp.dma_start(dst_i[:, 0:COLS], a["dst"]).then_inc(s_const, 16)
            sp.wait_ge(s_zero, 1)
            half = P // 2
            for n in range(2):
                at, of = slice(ROWS + n * half, ROWS + (n + 1) * half), slice(n * half, (n + 1) * half)
                sp.dma_start(sums[at, :], G[of, 0, :]).then_inc(stored[n], 16)
                sp.dma_start(states[at, :], ST[of, 0, :]).then_inc(stored[2 + n], 16)

            for f in range(len(PHASES)):
                k, what = PHASES[f]
                for b in range(BODY):
                    if f:
                        sp.wait_ge(stored[b], before_slot(STORES, f))
                if k == "fuse":
                    sp.wait_ge(s_carry_d, 16 * sum(kk in ("edge", "attend") for kk, _ in PHASES[:f]))
                loads = {"in": [(L2, a["x"])], "gcn": [(L1, tab[f"g{what - 1}"] if k == "gcn" else None)],
                         "gcn_out": [(L1, tab["g2"]), (L2, a["x"])], "conv": [(L1, tab["h1"]), (L2, res["x1"])],
                         "fuse": [(L1, tab["h2"]), (L2, res["x2"])], "sage1": [(L1, tab["h3"])],
                         "sage2": [(L1, tab["h4"]), (L2, res["x3"])]}.get(k, [])
                readers = {"in": ["h_ready"], "gcn": ["agg_ready"], "gcn_out": ["x_ready"],
                           "conv": ["own_transposed", "x_ready"], "fuse": ["own_transposed", "x_ready"],
                           "sage1": ["own_transposed"], "sage2": ["own_transposed", "out_ready"]}.get(k, [])
                stores = {"in": [(O1, tab["g0"])], "edge": [(G, sums)], "gcn": [(O1, tab.get(f"g{what}"))],
                          "gcn_out": [(O2, res["x1"]), (O1, tab["h1"])],
                          "conv": [(O2, res["x2"]), (O1, tab["h2"]), (QG, tab_qa)], "attend": [(ST, states)],
                          "fuse": [(O2, res["x3"]), (O1, tab["h3"])], "sage1": [(O1, tab["h4"])],
                          "sage2": [(O1, out)]}[k]
                makers = {"in": ["out_ready"], "edge": [], "gcn": ["out_ready"], "gcn_out": ["x_ready", "h_ready"],
                          "conv": ["x_ready", "h_ready", "qa_ready"], "attend": ["state_ready"],
                          "fuse": ["x_ready", "h_ready"], "sage1": ["out_ready"], "sage2": ["out_ready"]}[k]

                def load(i, b):
                    for r in readers:
                        sp.wait_ge(S[r], freed(r, f, i, b, BODY))
                        sp.sem_inc(s_spw, 1)
                    for t, d in loads:
                        sp.dma_start(quad(t, b), cols(d)[:, bass.ds(STEP * i + QUAD * b, QUAD), :])\
                          .then_inc(loaded[b], 16)

                def store(i, b):
                    for m in makers:
                        sp.wait_ge(S[m], reach(m, f, i, b))
                        sp.sem_inc(s_spw, 1)
                    if k == "edge":
                        sp.wait_ge(S["summed"], reach("summed", f, i, b, QUAD))
                        sp.sem_inc(s_spw, 1)
                    for t, d in stores:
                        sp.dma_start(cols(d)[:, bass.ds(STEP * i + QUAD * b, QUAD), :], quad(t, b))\
                          .then_inc(stored[b], 16)

                lag = {"edge": 1, "attend": 2, "conv": 4, "fuse": 4}.get(k, 3)
                run(sp, f, ([(load, 0)] if loads else []) + [(store, lag)])
            for b in range(BODY):
                sp.wait_ge(stored[b], before_slot(STORES, len(PHASES)))

        @block.gpsimd
        def _(pool):
            for t, val in ((ones, 1.0), (eps, EPS), (zero16, 0.0), (lnb, 10.0 * float(np.log(2.0)))):
                pool.memset(t[:], val).then_inc(s_pool, 1)
            pool.memset(src_i[:, COLS:], 0).then_inc(s_pool, 1)
            pool.memset(dst_i[:, COLS:], 0).then_inc(s_pool, 1)
            pool.memset(last_i[:, COLS:], 0).then_inc(s_pool, 1)
            pool.wait_ge(s_prepd, DEG)
            pool.wait_ge(s_pool, 7)
            pool.memset(t_f[4], -0.5).then_inc(s_pool, 1)
            pool.wait_ge(s_pool, 8)
            pool.tensor_tensor(dinv[:, :], t_f[1], t_f[4], ALU.pow).then_inc(s_pool, 1)

            def gather(dest, table, index):
                return pool.indirect_dma_start(
                    out=dest, out_offset=None, in_=table, in_offset=bass.IndirectOffsetOnAxis(ap=index, axis=0))

            waits = 0
            carries = 0
            for f in range(len(PHASES)):
                k, what = PHASES[f]
                if k == "in":
                    continue
                for b in range(BODY):
                    pool.wait_ge(stored[b], before_slot(STORES, f))
                if k not in ("edge", "attend"):
                    pool.wait_ge(s_carry_d, 16 * carries)
                readers = {"edge": ["summed"], "gcn": ["transposed"], "gcn_out": ["x_ready"],
                           "conv": ["transposed"], "attend": ["state_ready"], "fuse": ["parts_transposed", "blend_steps"],
                           "sage1": ["transposed"], "sage2": ["transposed"]}[k]

                def step(i, b):
                    pool.wait_ge(S["idx"], reach("idx", f, i, b))
                    if k == "attend":
                        pool.wait_ge(S["idx2"], reach("idx2", f, i, b))
                    for r in readers:
                        ring = BODY - 1 if k == "edge" else BODY
                        pool.wait_ge(S[r], freed(r, f, i, b, ring))
                    if k == "edge":
                        pool.wait_ge(stored[b], slot_done(STORES, f, i - 1))
                    pool.sem_inc(s_poolw, 1)
                    for c in range(QUAD):
                        t = QUAD * b + c
                        if k in ("edge", "attend"):
                            gather(G[:, t, :], tab[what], stage[:, t:t + 1]).then_inc(gathered[b], 16)
                        elif k == "fuse":
                            gather(ST[:, t, :], states, stage[:, t:t + 1]).then_inc(gathered[b], 16)
                        else:
                            gather(G[:, t, :], sums, stage[:, t:t + 1]).then_inc(gathered[b], 16)
                        if k == "attend":
                            gather(QG[:, t, :], tab_qa, stage2[:, t:t + 1]).then_inc(gathered[b], 16)

                run(pool, f, [(step, 0)])
                if k == "edge":
                    carries += 1
                    for b in range(BODY):
                        pool.wait_ge(stored[b], before_slot(STORES, f + 1))
                    pool.wait_ge(s_carry_v, carries)
                    pool.indirect_dma_start(
                        out=sums, out_offset=bass.IndirectOffsetOnAxis(ap=first_end[:, 0:1], axis=0),
                        in_=carry[:, :], in_offset=None, compute_op=ALU.add).then_inc(s_carry_d, 16)
                if k == "attend":
                    carries += 1
                    for b in range(BODY):
                        pool.wait_ge(stored[b], before_slot(STORES, f + 1))
                    gather(fixrow, states, first_end[:, 0:1]).then_inc(s_fixg, 16)
                    pool.wait_ge(s_carry_v, carries)
                    pool.indirect_dma_start(
                        out=states, out_offset=bass.IndirectOffsetOnAxis(ap=first_end[:, 0:1], axis=0),
                        in_=fixrow, in_offset=None).then_inc(s_carry_d, 16)

        @block.tensor
        def _(pe):
            prep = [0]

            def product(out_, lhsT, rhs, start=True, stop=True):
                return nc.tensor.matmul(out_, lhsT, rhs, start=start, stop=stop)

            pe.wait_ge(s_const, 16 * (len(consts) + 2))
            pe.wait_ge(s_pool, 4)
            product(bank[:, 0, 0:COLS], zero16[:, :], iota[:, 0:COLS], True, False).then_inc(s_hist, 1)
            with pe.Fori(0, COLS // 16) as i:
                for c in range(16):
                    pe.wait_ge(s_onehot, i * 32 + 2 * c + 2)
                    product(bank[:, 0, 0:COLS], oh_hi[:, c, :], oh_lo[:, c, :], False, False).then_inc(s_hist, 1)
            product(bank[:, 0, 0:COLS], zero16[:, :], iota[:, 0:COLS], False, True).then_inc(s_hist, 1)

            def prep_product(*args):
                product(*args).then_inc(s_prep, 1)

            pe.wait_ge(s_prepd, BLK)
            prep_product(bank[:, 1, 0:HEADS], mat("gat_wT"), blk[:, 0, :])
            prep_product(bank[:, 1, 16:16 + HEADS], mat("gat_wT"), blk[:, 1, :])
            prep_product(bank[:, 1, 32:32 + HEADS], mat("gat_wT"), blk[:, 2, :])
            prep_product(bank[:, 1, 48:48 + HEADS], mat("wqT"), blk[:, 3, :])
            prep_product(bank[:, 1, 64:64 + HEADS], mat("bq_col"), blk[:, 3, :])
            prep_product(bank[:, 2, 0:D], mat("wskipT"), mat("F3"))
            product(bank[:, 3, 0:D], mat("gat_b_col"), mat("F1"), True, False)
            prep_product(bank[:, 3, 0:D], mat("bskip_col"), mat("F3"), False, True)
            prep_product(bank[:, 4, 0:D], mat("bv_col"), mat("F3"))
            pe.wait_ge(s_prepd, TOTALS)
            prep_product(bank[:, 5, 0:1], upper[:, :], t_f[2][:, COLS - 1:COLS])
            pe.wait_ge(s_prepd, DIAG)
            prep_product(bank[:, 6, 0:P], ones[:, :], XT[:, 0, 0:P])
            prep_product(bank[:, 6, P:2 * P], ones[:, :], XT[:, 0, P:2 * P])
            pe.wait_ge(s_prepd, SETUP_END)

            carries = 0
            for f in range(len(PHASES)):
                k, what = PHASES[f]

                if k == "edge":
                    carries += 1
                    pe.wait_ge(S["summed"], reach("summed", f, TURNS - 1, BODY - 1, QUAD))
                    product(bank[:, 0, 0:D], carry_mask[:, :], G[:, STEP - 1, :]).then_inc(s_carry_p, 1)
                    pe.wait_ge(s_carry_v, carries)
                    continue

                def transposes(dest, tile, signal):
                    for c in range(QUAD):
                        ins = nc.tensor.transpose(dest[:, c * D:(c + 1) * D], tile(c), ident[:, :])
                    ins.then_inc(signal, 1)

                def first(i, b):
                    p = b % 2
                    if k == "in":
                        pe.wait_ge(S["h_ready"], reach("h_ready", f, i, b))
                    elif "agg_ready" in COUNTS and k in COUNTS["agg_ready"]:
                        pe.wait_ge(S["agg_ready"], reach("agg_ready", f, i, b))
                    else:
                        pe.wait_ge(gathered[b], slot_done(GATHERS, f, i))
                    pe.wait_ge(S["xt_ready"], freed("xt_ready", f, i, b, 1 if k == "fuse" else 2))
                    source = {"in": lambda c: O2[:, QUAD * b + c, :],
                              "fuse": lambda c: ST[:, QUAD * b + c, X_:X_ + D]}.get(k, lambda c: G[:, QUAD * b + c, :])
                    transposes(bank[:, 0 if k == "fuse" else p, :], source, S["transposed"])
                    if k in ("conv", "sage1", "sage2", "fuse"):
                        pe.wait_ge(loaded[b], slot_done(LOADS, f, i))
                        pe.wait_ge(S["xu_ready"], freed("xu_ready", f, i, b, 1 if k == "fuse" else 2))
                        transposes(bank[:, 1 if k == "fuse" else 2 + p, :], lambda c: L1[:, QUAD * b + c, :],
                                   S["own_transposed"])

                def second(i, b):
                    p = b % 2
                    pe.wait_ge(S["xt_ready"], reach("xt_ready", f, i, b))
                    two = k in ("conv", "sage1", "sage2")
                    if two:
                        pe.wait_ge(S["xu_ready"], reach("xu_ready", f, i, b))
                    user = "x_ready" if k == "conv" else "biased"
                    pe.wait_ge(S[user], freed(user, f, i, b, 1 if k == "conv" else 2))
                    w1, w2 = {"in": ("W0", None), "gcn": (f"W{what}", None), "conv": ("L1_W", "L1_Wself"),
                              "sage1": ("Wn1T", "Ws1T"), "sage2": ("Wn2T", "Ws2T")}[k]
                    o = bank[:, 4 if k == "conv" else 4 + p, :]
                    for c in range(QUAD):
                        w = slice(c * D, (c + 1) * D)
                        ins = product(o[:, w], XT[:, p, w], mat(w1), True, not two)
                        if two:
                            ins = product(o[:, w], XU[:, b, w], mat(w2), False, True)
                    ins.then_inc(S["product"], 1)

                def h_transpose(i, b):
                    pe.wait_ge(S["h_ready"], reach("h_ready", f, i, b))
                    pe.wait_ge(S["ht_ready"], freed("ht_ready", f, i, b, 1))
                    transposes(bank[:, 5, :], lambda c: O1[:, QUAD * b + c, :], S["h_transposed"])

                def h_product(i, b):
                    pe.wait_ge(S["ht_ready"], reach("ht_ready", f, i, b))
                    pe.wait_ge(S["qa_ready"], freed("qa_ready", f, i, b, 1))
                    for c in range(QUAD):
                        ins = product(bank[:, 6 + c // 2, 256 * (c % 2):256 * (c % 2) + QA],
                                      XV[:, b % 2, c * D:(c + 1) * D], WQA[:, :])
                    ins.then_inc(S["qa_product"], 1)

                def project(i, b):
                    pe.wait_ge(S["xt_ready"], reach("xt_ready", f, i, b))
                    for h in range(2):
                        used = f"proj_used{h}"
                        pe.wait_ge(S[used], freed(used, f, i, b, 1))
                        for c in (2 * h, 2 * h + 1):
                            ins = product(bank[:, 2 + c, 0:PROJ], XT[:, b % 2, c * D:(c + 1) * D], WE[:, :])
                        ins.then_inc(S[f"proj{h}"], 1)

                def self_and_sage(i, b):
                    pe.wait_ge(S["xt_ready"], reach("xt_ready", f, i, b))
                    pe.wait_ge(S["xu_ready"], reach("xu_ready", f, i, b))
                    pe.wait_ge(S["self_used"], freed("self_used", f, i, b, 1))
                    for c in range(QUAD):
                        ins = product(bank[:, 2 + c // 2, 256 * (c % 2):256 * (c % 2) + D + HEADS],
                                      XU[:, b, c * D:(c + 1) * D], WSELF[:, :])
                    ins.then_inc(S["self_product"], 1)
                    pe.wait_ge(S["sage_biased"], freed("sage_biased", f, i, b, 1))
                    for c in range(QUAD):
                        w = slice(c * D, (c + 1) * D)
                        product(bank[:, 4, w], XT[:, b % 2, w], mat("sage_wl"), True, False)
                        ins = product(bank[:, 4, w], XU[:, b, w], mat("sage_wr"), False, True)
                    ins.then_inc(S["product"], 1)

                def parts(i, b):
                    for n, (ready, tile) in enumerate((
                            ("gat_ready", lambda c: ST[:, QUAD * b + c, 0:D]),
                            ("tr_ready", lambda c: ST[:, QUAD * b + c, D:2 * D]),
                            ("sage_ready", lambda c: sage[:, b % 2, c, :]))):
                        pe.wait_ge(S[ready], reach(ready, f, i, b))
                        if n == 2:
                            pe.wait_ge(S["parts_ready"], reach("parts_ready", f, i, b, 1))
                        else:
                            pe.wait_ge(S["parts_ready"], freed("parts_ready", f, i, b, 1))
                        transposes(bank[:, 5 + n % 2, :], tile, S["parts_transposed"])

                def fuse_product(i, b):
                    pe.wait_ge(S["parts_ready"], reach("parts_ready", f, i, b, 3))
                    pe.wait_ge(S["fused_used"], freed("fused_used", f, i, b, 1))
                    for c in range(QUAD):
                        w = slice(c * D, (c + 1) * D)
                        product(bank[:, 7, w], XU[:, b, w], WS3[:, :], True, False)
                        product(bank[:, 7, w], XV[:, 0, w], mat("F1"), False, False)
                        product(bank[:, 7, w], XV[:, 1, w], mat("F3"), False, False)
                        ins = product(bank[:, 7, w], XV[:, 2, w], mat("F2"), False, True)
                    ins.then_inc(S["fused"], 1)

                if k == "in":
                    run(pe, f, [(first, 1), (second, 2)])
                elif k in ("gcn", "sage1", "sage2"):
                    run(pe, f, [(first, 0), (second, 1)])
                elif k == "conv":
                    run(pe, f, [(first, 0), (second, 1), (h_transpose, 2), (h_product, 3)])
                elif k == "attend":
                    run(pe, f, [(first, 0), (project, 1)])
                    carries += 1
                    pe.wait_ge(s_acarry, 1)
                    for n in range(4):
                        ins = product(bank[:, n, :], ones[:, :],
                                      cm[:, 4 * n:4 * n + 4, :].rearrange("p h q -> p (h q)"))
                    ins.then_inc(s_carry_p, 1)
                    pe.wait_ge(s_acarry, 2)
                    for n in range(2 * HEADS):
                        ins = nc.tensor.transpose(bank[:, n // 4, (n % 4) * P:(n % 4 + 1) * P], cm[:, n, :], ident[:, :])
                    ins.then_inc(s_carry_p, 1)
                    pe.wait_ge(s_acarry, 3)
                    for n in range(2 * HEADS):
                        product(bank[:, 4, n * (HC + 1):(n + 1) * (HC + 1)], cmT[:, n, :], rsv[:, n, :])
                    product(bank[:, 5, 0:D], carry_mask[:, :], ST[:, STEP - 1, X_:X_ + D]).then_inc(s_carry_p, 1)
                    pe.wait_ge(s_carry_v, carries)
                elif k == "fuse":
                    run(pe, f, [(first, 0), (self_and_sage, 1), (parts, 2), (fuse_product, 3)])

        @block.scalar
        def _(act):
            act.preload_act_table_set("natural_log_exp_and_others")
            act.wait_ge(s_pool, 4)

            for f in range(len(PHASES)):
                k, what = PHASES[f]

                def copy(dest, source, waits, signal):
                    for w in waits:
                        act.wait_ge(*w)
                    nc.scalar.activation(dest, source, ACT.Copy).then_inc(signal, 1)

                def copies(i, b):
                    p = b % 2
                    user = {"attend": "proj1"}.get(k, "product")
                    copy(XT[:, p, :], bank[:, 0 if k == "fuse" else p, :],
                         [(S["transposed"], reach("transposed", f, i, b)), (S[user], freed(user, f, i, b, 2))],
                         S["xt_ready"])
                    if k in ("conv", "sage1", "sage2", "fuse"):
                        user = {"fuse": "fused"}.get(k, "product")
                        copy(XU[:, b, :], bank[:, 1 if k == "fuse" else 2 + p, :],
                             [(S["own_transposed"], reach("own_transposed", f, i, b)),
                              (S[user], freed(user, f, i, b, BODY))], S["xu_ready"])

                def rstd_of(mvt, rst, n=""):
                    def go(i, b):
                        p = b % 2
                        act.wait_ge(S["stats" + n], reach("stats" + n, f, i, b))
                        nc.scalar.activation(rst[:, p, 0, :], mvt[:, p, :, 1], ACT.Ln, bias=eps[:, 0:1])\
                          .then_inc(S["rstd_steps" + n], 1)
                        act.wait_ge(S["rstd_steps" + n], reach("rstd_steps" + n, f, i, b))
                        nc.scalar.activation(rst[:, p, 1, :], rst[:, p, 0, :], ACT.Exp, scale=-0.5)\
                          .then_inc(S["rstd" + n], 1)
                    return go

                rstd = rstd_of(mv, rs)

                def relu_of(source, rst, nmt, n=""):
                    def go(i, b):
                        p = b % 2
                        act.wait_ge(S["shift" + n], reach("shift" + n, f, i, b))
                        if k == "in":
                            act.wait_ge(S["transposed"], freed("transposed", f, i, b, BODY))
                        else:
                            act.wait_ge(stored[b], slot_done(STORES, f, i - 1))
                        if k == "conv":
                            act.wait_ge(S["h_transposed"], freed("h_transposed", f, i, b, BODY))
                        dest = O2 if k == "in" else O1
                        for c in range(QUAD):
                            ins = nc.scalar.activation(dest[:, QUAD * b + c, :], source[:, QUAD * b + c, :], ACT.Relu,
                                                       bias=nmt[:, p, c:c + 1], scale=rst[:, p, 1, c:c + 1])
                        ins.then_inc(S["h_ready"], 1)
                    return go

                relu = relu_of(L2 if k == "in" else O2, rs, nm)

                def h_copy(i, b):
                    copy(XV[:, b % 2, :], bank[:, 5, :],
                         [(S["h_transposed"], reach("h_transposed", f, i, b)),
                          (S["qa_product"], freed("qa_product", f, i, b, 2))], S["ht_ready"])

                def exp_of(h):
                    def go(i, b):
                        act.wait_ge(S[f"gaps{h}"], reach(f"gaps{h}", f, i, b))
                        back = f"back_steps{h}"
                        act.wait_ge(S[back], freed(back, f, i, b, 1))
                        if h == 1:
                            act.wait_ge(S["state_ready"], freed("state_ready", f, i, b, 1))
                        nc.scalar.activation(exps[:, h, :, :], gaps[:, h, :, :], ACT.Exp).then_inc(S[f"exps{h}"], 1)
                    return go

                def self_exp(i, b):
                    act.wait_ge(S["self_gaps"], reach("self_gaps", f, i, b))
                    nc.scalar.activation(sexp[:, b % 2, :, :], sgap[:, b % 2, :, :], ACT.Exp)\
                      .then_inc(S["self_exps"], 1)

                def squares(i, b):
                    p = b % 2
                    act.wait_ge(S["sage_biased"], reach("sage_biased", f, i, b))
                    for c in range(QUAD):
                        if c:
                            act.wait_ge(S["sage_squares"], reach("sage_squares", f, i, b, c))
                        nc.scalar.activation(sq[:, :], sage[:, p, c, :], ACT.Square,
                                             accum_out=ss[:, p, 0, c:c + 1]).then_inc(S["sage_squares"], 1)

                def norm(i, b):
                    p = b % 2
                    act.wait_ge(S["sage_floor"], reach("sage_floor", f, i, b))
                    nc.scalar.activation(ss[:, p, 1, :], ss[:, p, 1, :], ACT.Ln, scale=float(2 ** 20))\
                      .then_inc(S["sage_log"], 1)
                    act.wait_ge(S["sage_log"], reach("sage_log", f, i, b))
                    nc.scalar.activation(ss[:, p, 2, :], ss[:, p, 1, :], ACT.Exp, scale=-0.5, bias=lnb[:, 0:1])\
                      .then_inc(S["sage_norm"], 1)

                def part_copies(i, b):
                    for n in range(3):
                        copy(XV[:, n, :], bank[:, 5 + n % 2, :],
                             [(S["parts_transposed"], reach("parts_transposed", f, i, b, n + 1)),
                              (S["fused"], freed("fused", f, i, b, 1))], S["parts_ready"])

                def normed(i, b):
                    p = b % 2
                    act.wait_ge(S["shift"], reach("shift", f, i, b, 1))
                    for c in range(QUAD):
                        ins = nc.scalar.activation(zn[:, p, c, :], yv[:, p, c, :], ACT.Identity,
                                                   bias=nm[:, p, c:c + 1], scale=rs[:, p, 1, c:c + 1])
                    ins.then_inc(S["normed"], 1)

                if k == "in":
                    run(act, f, [(rstd, 0), (relu, 1), (copies, 2)])
                elif k in ("gcn", "sage1", "sage2"):
                    run(act, f, [(copies, 0)])
                elif k == "gcn_out":
                    run(act, f, [(rstd, 0), (relu, 1)])
                elif k == "conv":
                    run(act, f, [(copies, 0), (rstd, 1), (relu, 2), (h_copy, 3)])
                elif k == "attend":
                    run(act, f, [(copies, 0), (exp_of(0), 1), (exp_of(1), 1)])
                    act.wait_ge(s_cgap, 1)
                    nc.scalar.activation(cm, cm, ACT.Exp).then_inc(s_act, 1)
                    act.wait_ge(s_cgap, 2)
                    nc.scalar.activation(mc[:, 2:4, :], mc[:, 2:4, :], ACT.Exp).then_inc(s_act, 1)
                elif k == "fuse":
                    def tail(i, b):
                        normed(i, b)
                        rstd_of(mv2, rs2, "2")(i, b)
                        relu_of(O2, rs2, nm2, "2")(i, b)

                    run(act, f, [(copies, 0), (self_exp, 1), (squares, 1), (norm, 2), (part_copies, 2), (rstd, 3),
                                 (tail, 4)])

        @block.vector
        def _(dve):
            V = nc.vector
            steps = [0]

            def prep(ins):
                steps[0] += 1
                ins.then_inc(s_prepd, 1)
                dve.wait_ge(s_prepd, steps[0])

            dve.wait_ge(s_const, 16 * (len(consts) + 2))
            prep(V.tensor_scalar(blk[:, 0, :], hmask[:, :], attc[:, 0:1], None, ALU.mult))
            prep(V.tensor_scalar(blk[:, 1, :], hmask[:, :], attc[:, 1:2], None, ALU.mult))
            prep(V.tensor_scalar(blk[:, 3, :], hmask[:, :], attc[:, 2:3], None, ALU.mult))
            prep(V.tensor_tensor(blk[:, 2, :], blk[:, 0, :], blk[:, 1, :], ALU.add))
            assert steps[0] == BLK
            prep(V.memset(G[:, :, :], 0.0))
            V.memset(ST[:, :, :], 0.0).then_inc(s_zero, 1)
            prep(V.tensor_copy(dst[:, :], dst_i[:, 0:COLS]))
            prep(V.memset(same[:, 0:1], 0.0))
            prep(V.tensor_tensor(same[:, 1:COLS], dst[:, 1:COLS], dst[:, 0:COLS - 1], ALU.is_equal))
            prep(V.tensor_scalar(gapneg[:, :], same[:, :], 1.0, -NEG, ALU.subtract, ALU.mult))
            quot, hi, lo, flag, _ = t_f
            prep(V.tensor_scalar(quot, dst[:, :], 1.0 / COLS, None, ALU.mult))
            prep(V.tensor_copy(t_i, quot))
            prep(V.tensor_copy(hi, t_i))
            prep(V.scalar_tensor_tensor(out=lo, in0=hi, scalar=-float(COLS), in1=dst[:, :], op0=ALU.mult, op1=ALU.add))
            prep(V.tensor_scalar(flag, lo, 0.0, None, ALU.is_lt))
            prep(V.tensor_tensor(hi, hi, flag, ALU.subtract))
            prep(V.tensor_scalar(flag, lo, float(COLS), None, ALU.is_ge))
            prep(V.tensor_tensor(hi, hi, flag, ALU.add))
            prep(V.scalar_tensor_tensor(out=lo, in0=hi, scalar=-float(COLS), in1=dst[:, :], op0=ALU.mult, op1=ALU.add))

            def onehots(col, c):
                V.tensor_scalar(oh_hi[:, c, :], iota[:, 0:P], hi[:, col:col + 1] if isinstance(col, int)
                                else hi[:, bass.ds(col, 1)], None, ALU.is_equal).then_inc(s_onehot, 1)
                V.tensor_scalar(oh_lo[:, c, :], iota[:, :], lo[:, col:col + 1] if isinstance(col, int)
                                else lo[:, bass.ds(col, 1)], None, ALU.is_equal).then_inc(s_onehot, 1)

            for c in range(16):
                onehots(c, c)
            with dve.Fori(1, COLS // 16) as i:
                for c in range(16):
                    dve.wait_ge(s_hist, (i - 1) * 16 + c + 2)
                    onehots(i * 16 + c, c)
            dve.wait_ge(s_hist, COLS + 2)
            deg, deg1, run_, t3, _ = t_f
            prep(V.tensor_copy(deg, bank[:, 0, 0:COLS]))
            prep(V.tensor_scalar(deg1, deg, 1.0, None, ALU.add))
            assert steps[0] == DEG
            prep(V.tensor_scalar(t3, deg, 1.0, None, ALU.max))
            prep(V.reciprocal(invdeg[:, :], t3))
            prep(V.tensor_scalar(has[:, :], deg, 0.0, None, ALU.is_gt))
            prep(V.memset(t3, 1.0))
            prep(V.tensor_tensor_scan(run_, t3, deg, 0.0, ALU.mult, ALU.add))
            assert steps[0] == TOTALS
            dve.wait_ge(s_prep, 9)
            prep(V.tensor_copy(t3[:, 0:1], bank[:, 5, 0:1]))
            prep(V.tensor_scalar(run_, run_, t3[:, 0:1], -1.0, ALU.add, ALU.add))
            prep(V.tensor_scalar(run_, run_, emptyrow[:, 0:1], None, ALU.subtract))
            prep(V.tensor_tensor(run_, run_, has[:, :], ALU.mult))
            prep(V.tensor_scalar(last_i[:, 0:COLS], run_, emptyrow[:, 0:1], None, ALU.add))
            prep(V.tensor_scalar(XT[:, 0, 0:P], ident[:, :], dst[:, 0:1], None, ALU.mult))
            prep(V.tensor_scalar(XT[:, 0, P:2 * P], ident[:, :], dst[:, COLS - 1:COLS], None, ALU.mult))
            assert steps[0] == DIAG
            dve.wait_ge(s_prep, 11)
            prep(V.scalar_tensor_tensor(out=carry_mask[:, :], in0=bank[:, 6, 0:P], scalar=dst[:, COLS - 1:COLS],
                                        in1=upper[:, :], op0=ALU.is_equal, op1=ALU.mult))
            prep(V.scalar_tensor_tensor(out=carry_maskT[:, :], in0=bank[:, 6, P:2 * P], scalar=dst[:, 0:1],
                                        in1=lower[:, :], op0=ALU.is_equal, op1=ALU.mult))
            prep(V.tensor_scalar(deg, dst[:, :], dst[:, 0:1], None, ALU.is_equal))
            prep(V.tensor_reduce(t3[:, 1:2], deg, AX.X, ALU.add))
            prep(V.tensor_scalar(first_end[:, :], t3[:, 1:2], firstrow[:, 0:1], None, ALU.add))
            prep(V.tensor_copy(WE[:, 0:D], mat("gat_w")))
            prep(V.tensor_copy(WE[:, D:2 * D], mat("wv")))
            prep(V.tensor_copy(WE[:, 2 * D:3 * D], mat("wk")))
            prep(V.tensor_copy(WE[:, 3 * D:PROJ], bank[:, 1, 0:HEADS]))
            scale = HC ** -0.5
            prep(V.tensor_scalar(WQA[:, 0:D], mat("wq"), scale, None, ALU.mult))
            prep(V.tensor_copy(WQA[:, D:D + HEADS], bank[:, 1, 16:16 + HEADS]))
            prep(V.tensor_scalar(WQA[:, D + HEADS:QA], bank[:, 1, 48:48 + HEADS], scale, None, ALU.mult))
            prep(V.tensor_scalar(BQA[:, 0:D], vec("bq"), scale, None, ALU.mult))
            prep(V.memset(BQA[:, D:D + HEADS], 0.0))
            prep(V.tensor_scalar(BQA[:, D + HEADS:QA], bank[:, 1, 64:64 + HEADS], scale, None, ALU.mult))
            prep(V.tensor_copy(WSELF[:, 0:D], mat("gat_w")))
            prep(V.tensor_copy(WSELF[:, D:D + HEADS], bank[:, 1, 32:32 + HEADS]))
            prep(V.tensor_copy(WS3[:, :], bank[:, 2, 0:D]))
            prep(V.tensor_tensor(c0[:, :], bank[:, 3, 0:D], vec("fus_b"), ALU.add))
            prep(V.tensor_copy(c1[:, :], bank[:, 4, 0:D]))
            prep(V.tensor_tensor(bsum[:, 0, :], vec("bn1"), vec("bs1"), ALU.add))
            prep(V.tensor_tensor(bsum[:, 1, :], vec("bn2"), vec("bs2"), ALU.add))
            assert steps[0] == SETUP_END
            dve.wait_ge(s_pool, 9)

            carries = 0
            carry_products = 0
            local = [0]

            def did(ins):
                local[0] += 1
                ins.then_inc(s_dve, 1)
                dve.wait_ge(s_dve, local[0])

            for f in range(len(PHASES)):
                k, what = PHASES[f]
                index = src_i if k in ("edge", "attend") else last_i

                def stage_indices(i, b):
                    dve.wait_ge(gathered[b], slot_done(GATHERS, f, i))
                    copy_indices(i + 1, b)

                def copy_indices(i, b):
                    w = bass.ds(STEP * i + QUAD * b, QUAD)
                    t = slice(QUAD * b, QUAD * (b + 1))
                    V.tensor_scalar(stage[:, t], index[:, w], 0, None, ALU.add).then_inc(S["idx"], 1)
                    if k == "attend":
                        V.tensor_scalar(stage2[:, t], dst_i[:, w], 0, None, ALU.add).then_inc(S["idx2"], 1)

                if k != "in":
                    dve.wait_ge(S["idx"], before("idx", f))
                    for b in range(BODY):
                        copy_indices(0, b)

                def product_bank(b):
                    return bank[:, 4 if k in ("conv", "fuse") else 4 + b % 2, :].rearrange("p (c f) -> p c f", c=QUAD)

                def stats(i, b, source, mvt, bstt, n=""):
                    p = b % 2
                    user = "normed" if k == "fuse" and not n else "h_ready"
                    dve.wait_ge(S[user], freed(user, f, i, b, 2))
                    for c in range(QUAD):
                        V.bn_stats(bstt[:, p, c, :], source[:, c, :]).then_inc(S["norm_steps" + n], 1)
                    dve.wait_ge(S["norm_steps" + n], reach("norm_steps" + n, f, i, b, QUAD))
                    dve.sem_inc(s_dvew, 1)
                    for c in range(QUAD):
                        ins = V.bn_aggr(mvt[:, p, c, :], bstt[:, p, c, :])
                    ins.then_inc(S["stats" + n], 1)

                def shift(i, b, mvt=mv, rst=rs, nmt=nm, n=""):
                    p = b % 2
                    dve.wait_ge(S["rstd" + n], reach("rstd" + n, f, i, b))
                    V.scalar_tensor_tensor(out=nmt[:, p, :], in0=mvt[:, p, :, 1 - 1], scalar=-1.0, in1=rst[:, p, 1, :],
                                           op0=ALU.mult, op1=ALU.mult).then_inc(S["shift" + n], 1)

                def sums_of(i, b):
                    stage_indices(i, b)
                    for c in range(QUAD):
                        t = QUAD * b + c
                        dve.wait_ge(S["summed"], reach("summed", f, i, b, c))
                        V.scalar_tensor_tensor(out=G[:, t, :], in0=G[:, prior_tiles(b, c), :],
                                               scalar=same[:, bass.ds(STEP * i + t, 1)], in1=G[:, t, :],
                                               op0=ALU.mult, op1=ALU.add).then_inc(S["summed"], 1)

                def in_stats(i, b):
                    dve.wait_ge(loaded[b], slot_done(LOADS, f, i))
                    stats(i, b, quad(L2, b), mv, bst)

                def aggregate(i, b):
                    stage_indices(i, b)
                    g = quad(G, b)
                    if k in ("gcn", "gcn_out"):
                        dve.wait_ge(loaded[b], slot_done(LOADS, f, i))
                        V.tensor_tensor(g, g, quad(L1, b), ALU.add).then_inc(S["agg_steps"], 1)
                        dve.wait_ge(S["agg_steps"], reach("agg_steps", f, i, b, 1))
                        ins = V.tensor_tensor(g, g, per_col(dinv, i, b), ALU.mult)
                        if k == "gcn":
                            ins.then_inc(S["agg_ready"], 1)
                            return
                        ins.then_inc(S["agg_steps"], 1)
                        dve.wait_ge(S["agg_steps"], reach("agg_steps", f, i, b, 2))
                        dve.wait_ge(stored[b], slot_done(STORES, f, i - 1))
                        V.tensor_tensor(quad(O2, b), g, quad(L2, b), ALU.add).then_inc(S["x_ready"], 1)
                        dve.wait_ge(S["x_ready"], reach("x_ready", f, i, b))
                        stats(i, b, quad(O2, b), mv, bst)
                    elif k in ("sage1", "sage2"):
                        V.tensor_tensor(g, g, per_col(invdeg, i, b), ALU.mult).then_inc(S["agg_ready"], 1)
                    elif k == "fuse":
                        x = quad(ST, b)[:, :, X_:X_ + D]
                        V.tensor_tensor(x, x, per_col(invdeg, i, b), ALU.mult).then_inc(S["agg_ready"], 1)

                def post(i, b):
                    o = quad(O1, b)
                    bias = {"in": lambda: vec("b0"), "gcn": lambda: vec(f"b{what}"), "sage1": lambda: bsum[:, 0, :],
                            "sage2": lambda: bsum[:, 1, :]}[k]()
                    dve.wait_ge(S["product"], reach("product", f, i, b))
                    dve.wait_ge(stored[b], slot_done(STORES, f, i - 1))
                    V.tensor_tensor(o, product_bank(b), over_quad(bias), ALU.add).then_inc(S["biased"], 1)
                    dve.wait_ge(S["biased"], reach("biased", f, i, b))
                    if k in ("in", "gcn"):
                        ins = V.scalar_tensor_tensor(out=o, in0=o, scalar=0.0, in1=per_col(dinv, i, b),
                                                     op0=ALU.max, op1=ALU.mult)
                    elif k == "sage1":
                        ins = V.tensor_scalar(o, o, 0.0, None, ALU.max)
                    else:
                        dve.wait_ge(loaded[b], slot_done(LOADS, f, i))
                        ins = V.tensor_tensor(o, o, quad(L2, b), ALU.add)
                    ins.then_inc(S["out_ready"], 1)

                def conv_x(i, b):
                    dve.wait_ge(S["product"], reach("product", f, i, b))
                    dve.wait_ge(loaded[b], slot_done(LOADS, f, i))
                    dve.wait_ge(stored[b], slot_done(STORES, f, i - 1))
                    V.tensor_tensor(quad(O2, b), product_bank(b), quad(L2, b), ALU.add).then_inc(S["x_ready"], 1)
                    dve.wait_ge(S["x_ready"], reach("x_ready", f, i, b))
                    stats(i, b, quad(O2, b), mv, bst)

                wide = bank[:, 6:8, :].rearrange("p a (t c) -> p (a t) c", t=2)

                def conv_qa(i, b):
                    dve.wait_ge(S["qa_product"], reach("qa_product", f, i, b))
                    dve.wait_ge(stored[b], slot_done(STORES, f, i - 1))
                    V.tensor_tensor(quad(QG, b), wide[:, :, 0:QA], over_quad(BQA[:, :]), ALU.add)\
                     .then_inc(S["qa_ready"], 1)

                def heads(t):
                    return t.rearrange("p c (h e) -> p c h e", e=HC)

                def front(i, b, h):
                    fs = f"front_steps{h}"
                    t0 = QUAD * b + 2 * h
                    pair = slice(t0, t0 + 2)
                    pj = bank[:, 2 + 2 * h:4 + 2 * h, :]

                    def after(n):
                        dve.wait_ge(S[fs], reach(fs, f, i, b, n))

                    dve.wait_ge(S[f"proj{h}"], reach(f"proj{h}", f, i, b))
                    if h == 0:
                        dve.wait_ge(stored[b], slot_done(STORES, f, i - 1))
                    V.tensor_tensor(prod[:, h], pj[:, :, 2 * D:3 * D], QG[:, pair, 0:D], ALU.mult).then_inc(S[fs], 1)
                    V.tensor_tensor(asum[:, h], pj[:, :, 3 * D:PROJ], QG[:, pair, D:D + HEADS], ALU.add)\
                     .then_inc(S[fs], 1)
                    after(1)
                    V.tensor_reduce(red[:, h], heads(prod[:, h]), AX.X, ALU.add).then_inc(S[fs], 1)
                    after(2)
                    V.scalar_tensor_tensor(out=lg[:, h, :, 0:HEADS], in0=asum[:, h], scalar=0.2, in1=asum[:, h],
                                           op0=ALU.mult, op1=ALU.max).then_inc(S[fs], 1)
                    after(3)
                    V.tensor_tensor(lg[:, h, :, HEADS:], red[:, h], QG[:, pair, D + HEADS:QA], ALU.add)\
                     .then_inc(S[fs], 1)
                    after(5)
                    if h == 1:
                        dve.wait_ge(S["front_steps0"], reach("front_steps0", f, i, b, 7))
                    else:
                        dve.wait_ge(S["front_steps1"], reach("front_steps1", f, i, b, 0))
                    for c in range(2):
                        V.scalar_tensor_tensor(out=ST[:, t0 + c, M_:S_], in0=ST[:, (t0 + c - 1) % STEP, M_:S_],
                                               scalar=gapneg[:, bass.ds(STEP * i + t0 + c, 1)], in1=lg[:, h, c, :],
                                               op0=ALU.add, op1=ALU.max).then_inc(S[fs], 1)
                        after(6 + c)
                    dve.wait_ge(S[f"exps{h}"], freed(f"exps{h}", f, i, b, 1))
                    V.tensor_tensor(gaps[:, h, :, 2 * HEADS:], lg[:, h], ST[:, pair, M_:S_], ALU.subtract)
                    for c in range(2):
                        ins = V.scalar_tensor_tensor(
                            out=gaps[:, h, c, 0:2 * HEADS], in0=ST[:, (t0 + c - 1) % STEP, M_:S_],
                            scalar=gapneg[:, bass.ds(STEP * i + t0 + c, 1)], in1=ST[:, t0 + c, M_:S_],
                            op0=ALU.add, op1=ALU.subtract)
                    ins.then_inc(S[f"gaps{h}"], 1)

                def back(i, b, h):
                    bs = f"back_steps{h}"
                    t0 = QUAD * b + 2 * h
                    pj = bank[:, 2 + 2 * h:4 + 2 * h, :]

                    def after(n):
                        dve.wait_ge(S[bs], reach(bs, f, i, b, n))

                    if h == 1:
                        dve.wait_ge(S["back_steps0"], reach("back_steps0", f, i, b, 10))
                    else:
                        dve.wait_ge(S["state_ready"], reach("state_ready", f, i, b, 0))
                    dve.wait_ge(S[f"exps{h}"], reach(f"exps{h}", f, i, b))
                    V.tensor_tensor(heads(tmp[:, :, :]), heads(pj[:, :, 0:2 * D]),
                                    exps[:, h, :, 2 * HEADS:].unsqueeze(3).to_broadcast([P, 2, 2 * HEADS, HC]),
                                    ALU.mult).then_inc(S[f"proj_used{h}"], 1)
                    for c in range(2):
                        t, before_t = t0 + c, (t0 + c - 1) % STEP
                        r = exps[:, h, c, 0:2 * HEADS]
                        R = ST[:, t, 0:2 * D].rearrange("p (h e) -> p h e", e=HC)
                        Rb = ST[:, before_t, 0:2 * D].rearrange("p (h e) -> p h e", e=HC)
                        if c:
                            after(4)
                        V.tensor_tensor(R, Rb, r.unsqueeze(2).to_broadcast([P, 2 * HEADS, HC]), ALU.mult)\
                         .then_inc(S[bs], 1)
                        if c:
                            after(5)
                        V.tensor_tensor(ST[:, t, S_:SW], ST[:, before_t, S_:SW], r, ALU.mult).then_inc(S[bs], 1)
                        V.scalar_tensor_tensor(out=ST[:, t, X_:M_], in0=ST[:, before_t, X_:M_],
                                               scalar=same[:, bass.ds(STEP * i + t, 1)], in1=G[:, t, :],
                                               op0=ALU.mult, op1=ALU.add).then_inc(S[bs], 1)
                        if not c:
                            dve.wait_ge(S[f"proj_used{h}"], reach(f"proj_used{h}", f, i, b))
                        after(5 * c + 1)
                        V.tensor_tensor(ST[:, t, 0:2 * D], ST[:, t, 0:2 * D], tmp[:, c, :], ALU.add)\
                         .then_inc(S[bs], 1)
                        after(5 * c + 2)
                        V.tensor_tensor(ST[:, t, S_:SW], ST[:, t, S_:SW], exps[:, h, c, 2 * HEADS:], ALU.add)\
                         .then_inc(S["state_ready" if (h, c) == (1, 1) else bs], 1)

                def attend_pairs(i, b):
                    front(i, b, 0)
                    front(i, b, 1)
                    back(i, b, 0)
                    back(i, b, 1)

                H = bank[:, 2:4, :].rearrange("p a (t c) -> p (a t) c", t=2)

                def self_logits(i, b):
                    s = quad(ST, b)

                    def after(n):
                        dve.wait_ge(S["self_steps"], reach("self_steps", f, i, b, n))

                    dve.wait_ge(S["self_product"], reach("self_product", f, i, b))
                    V.tensor_scalar(slog[:, :, :], H[:, :, D:D + HEADS], 0.2, None, ALU.mult)\
                     .then_inc(S["self_steps"], 1)
                    after(1)
                    V.tensor_tensor(slog[:, :, :], slog[:, :, :], H[:, :, D:D + HEADS], ALU.max)\
                     .then_inc(S["self_steps"], 1)
                    after(2)
                    V.tensor_tensor(sm[:, :, :], slog[:, :, :], s[:, :, M_:M_ + HEADS], ALU.max)\
                     .then_inc(S["self_steps"], 1)
                    after(3)
                    dve.wait_ge(S["sage_ready"], freed("sage_ready", f, i, b, 2))
                    V.tensor_tensor(sgap[:, b % 2, :, 0:HEADS], s[:, :, M_:M_ + HEADS], sm[:, :, :], ALU.subtract)
                    V.tensor_tensor(sgap[:, b % 2, :, HEADS:], slog[:, :, :], sm[:, :, :], ALU.subtract)\
                     .then_inc(S["self_gaps"], 1)

                def sage_bias(i, b):
                    dve.wait_ge(S["product"], reach("product", f, i, b))
                    dve.wait_ge(S["parts_transposed"], freed("parts_transposed", f, i, b, 2))
                    V.tensor_tensor(sage[:, b % 2, :, :], product_bank(b), over_quad(vec("sage_bl")), ALU.add)\
                     .then_inc(S["sage_biased"], 1)

                def floor(i, b):
                    p = b % 2
                    dve.wait_ge(S["sage_squares"], reach("sage_squares", f, i, b, QUAD))
                    V.tensor_scalar(ss[:, p, 1, :], ss[:, p, 0, :], 1e-24, None, ALU.max).then_inc(S["sage_floor"], 1)

                def blend(i, b):
                    s, e = quad(ST, b), sexp[:, b % 2, :, :]

                    def after(n):
                        dve.wait_ge(S["blend_steps"], reach("blend_steps", f, i, b, n))

                    def step(ins):
                        ins.then_inc(S["blend_steps"], 1)

                    def by_head(t):
                        return t.unsqueeze(3).to_broadcast([P, QUAD, HEADS, HC])

                    dve.wait_ge(S["self_exps"], reach("self_exps", f, i, b))
                    step(V.tensor_tensor(zz[:, :, 0:HEADS], s[:, :, S_:S_ + HEADS], e[:, :, 0:HEADS], ALU.mult))
                    step(V.tensor_copy(zz[:, :, HEADS:], s[:, :, S_ + HEADS:SW]))
                    after(1)
                    step(V.tensor_tensor(zz[:, :, 0:HEADS], zz[:, :, 0:HEADS], e[:, :, HEADS:], ALU.add))
                    after(3)
                    step(V.tensor_scalar(zz[:, :, :], zz[:, :, :], 1e-16, None, ALU.max))
                    after(4)
                    step(V.reciprocal(zz[:, :, :], zz[:, :, :]))
                    after(5)
                    e2 = e.rearrange("p c (g h) -> p c g h", g=2)
                    step(V.tensor_tensor(e2, e2, zz[:, :, 0:HEADS].unsqueeze(2).to_broadcast([P, QUAD, 2, HEADS]),
                                         ALU.mult))
                    tr = heads(s[:, :, D:2 * D])
                    V.tensor_tensor(tr, tr, by_head(zz[:, :, HEADS:]), ALU.mult).then_inc(S["tr_ready"], 1)
                    after(6)
                    gat = heads(s[:, :, 0:D])
                    step(V.tensor_tensor(gat, gat, by_head(e[:, :, 0:HEADS]), ALU.mult))
                    V.tensor_tensor(heads(hself[:, :, :]), heads(H[:, :, 0:D]), by_head(e[:, :, HEADS:]), ALU.mult)\
                     .then_inc(S["self_used"], 1)
                    dve.wait_ge(S["self_used"], reach("self_used", f, i, b))
                    after(7)
                    V.tensor_tensor(s[:, :, 0:D], s[:, :, 0:D], hself[:, :, :], ALU.add).then_inc(S["gat_ready"], 1)

                def sage_scale(i, b):
                    p = b % 2
                    dve.wait_ge(S["sage_norm"], reach("sage_norm", f, i, b))
                    V.tensor_tensor(sage[:, p, :, :], sage[:, p, :, :],
                                    ss[:, p, 2, :].unsqueeze(2).to_broadcast([P, QUAD, D]), ALU.mult)\
                     .then_inc(S["sage_ready"], 1)

                def fused_stats(i, b):
                    p = b % 2
                    dve.wait_ge(S["fused"], reach("fused", f, i, b))
                    dve.wait_ge(S["normed"], freed("normed", f, i, b, 2))
                    V.tensor_tensor(yv[:, p, :, :], bank[:, 7, :].rearrange("p (c f) -> p c f", c=QUAD),
                                    over_quad(c0[:, :]), ALU.add).then_inc(S["fused_used"], 1)
                    dve.wait_ge(S["fused_used"], reach("fused_used", f, i, b))
                    for c in range(QUAD):
                        V.scalar_tensor_tensor(out=yv[:, p, c, :], in0=c1[:, :],
                                               scalar=has[:, bass.ds(STEP * i + QUAD * b + c, 1)],
                                               in1=yv[:, p, c, :], op0=ALU.mult, op1=ALU.add)\
                         .then_inc(S["fuse_steps"], 1)
                    dve.wait_ge(S["fuse_steps"], reach("fuse_steps", f, i, b, QUAD))
                    stats(i, b, yv[:, p, :, :], mv, bst)

                def fused_x(i, b):
                    p = b % 2
                    z = zn[:, p, :, :]
                    shift(i, b)
                    dve.wait_ge(S["normed"], reach("normed", f, i, b))
                    V.tensor_tensor(z, z, over_quad(vec("ln_g")), ALU.mult).then_inc(S["x3_steps"], 1)
                    dve.wait_ge(S["x3_steps"], reach("x3_steps", f, i, b, 1))
                    V.tensor_tensor(z, z, over_quad(vec("ln_b")), ALU.add).then_inc(S["x3_steps"], 1)
                    dve.wait_ge(S["x3_steps"], reach("x3_steps", f, i, b, 2))
                    dve.wait_ge(stored[b], slot_done(STORES, f, i - 1))
                    dve.wait_ge(loaded[b], slot_done(LOADS, f, i))
                    V.tensor_tensor(quad(O2, b), z, quad(L2, b), ALU.add).then_inc(S["x_ready"], 1)
                    dve.wait_ge(S["x_ready"], reach("x_ready", f, i, b))
                    stats(i, b, quad(O2, b), mv2, bst2, "2")
                    shift(i, b, mv2, rs2, nm2, "2")

                if k == "in":
                    run(dve, f, [(in_stats, 0), (shift, 1), (post, 3)])
                elif k == "edge":
                    run(dve, f, [(sums_of, 0)])
                    carries += 1
                    carry_products += 1
                    if carries > 1:
                        dve.wait_ge(s_carry_d, 16 * (carries - 1))
                    dve.wait_ge(s_carry_p, carry_products)
                    V.tensor_copy(carry[:, :], bank[:, 0, 0:D]).then_inc(s_carry_v, 1)
                elif k in ("gcn", "sage1", "sage2"):
                    run(dve, f, [(aggregate, 0), (post, 2)])
                elif k == "gcn_out":
                    run(dve, f, [(aggregate, 0), (shift, 1)])
                elif k == "conv":
                    run(dve, f, [(stage_indices, 0), (conv_x, 1), (shift, 2), (conv_qa, 4)])
                elif k == "fuse":
                    run(dve, f, [(aggregate, 0), (self_logits, 1), (sage_bias, 1), (floor, 2), (blend, 2),
                                 (sage_scale, 2), (fused_stats, 3), (fused_x, 4)])
                elif k == "attend":
                    run(dve, f, [(stage_indices, 0), (attend_pairs, 1)])
                    carries += 1
                    HH = 2 * HEADS
                    end = ST[:, STEP - 1, :]
                    dve.wait_ge(S["state_ready"], before("state_ready", f + 1))
                    did(V.tensor_tensor(rsv[:, :, 0:HC], end[:, 0:2 * D].rearrange("p (h e) -> p h e", e=HC),
                                        end[:, 0:2 * D].rearrange("p (h e) -> p h e", e=HC), ALU.max))
                    did(V.tensor_copy(rsv[:, :, HC], end[:, S_:SW]))
                    did(V.tensor_scalar(XT[:, 0, 0:P], carry_maskT[:, :], 1.0, -NEG, ALU.subtract, ALU.mult))
                    V.tensor_tensor(cm, ident[:, :].unsqueeze(1).to_broadcast([P, HH, P]),
                                    end[:, M_:S_].unsqueeze(2).to_broadcast([P, HH, P]), ALU.mult).then_inc(s_acarry, 1)
                    spread = bank[:, 0:4, :].rearrange("p a (t q) -> p (a t) q", t=4)
                    dve.wait_ge(s_carry_p, carry_products + 1)
                    did(V.tensor_tensor(cm, spread, XT[:, 0, 0:P].unsqueeze(1).to_broadcast([P, HH, P]), ALU.add))
                    did(V.tensor_reduce(mc[:, 0, :], cm, AX.X, ALU.max))
                    V.tensor_tensor(cm, cm, mc[:, 0, :].unsqueeze(2).to_broadcast([P, HH, P]), ALU.subtract)\
                     .then_inc(s_cgap, 1)
                    dve.wait_ge(s_act, 1)
                    V.tensor_tensor(cm, cm, carry_maskT[:, :].unsqueeze(1).to_broadcast([P, HH, P]), ALU.mult)\
                     .then_inc(s_acarry, 1)
                    dve.wait_ge(s_carry_p, carry_products + 2)
                    V.tensor_copy(cmT, spread).then_inc(s_acarry, 1)
                    dve.wait_ge(s_fixg, 16)
                    m1, ga, gb, sc = mc[:, 1, :], mc[:, 2, :], mc[:, 3, :], mc[:, 4, :]
                    did(V.tensor_tensor(m1, mc[:, 0, :], fixrow[:, M_:S_], ALU.max))
                    did(V.tensor_tensor(ga, mc[:, 0, :], m1, ALU.subtract))
                    V.tensor_tensor(gb, fixrow[:, M_:S_], m1, ALU.subtract).then_inc(s_cgap, 1)
                    dve.wait_ge(s_act, 2)
                    dve.wait_ge(s_carry_p, carry_products + 3)
                    carry_products += 3
                    rc = bank[:, 4, 0:HH * (HC + 1)].rearrange("p (h e) -> p h e", e=HC + 1)
                    fr = fixrow[:, 0:2 * D].rearrange("p (h e) -> p h e", e=HC)
                    ft = fixtmp[:, 0:2 * D].rearrange("p (h e) -> p h e", e=HC)
                    did(V.tensor_tensor(ft, rc[:, :, 0:HC], ga.unsqueeze(2).to_broadcast([P, HH, HC]), ALU.mult))
                    did(V.tensor_tensor(fr, fr, gb.unsqueeze(2).to_broadcast([P, HH, HC]), ALU.mult))
                    did(V.tensor_tensor(fixrow[:, 0:2 * D], fixrow[:, 0:2 * D], fixtmp[:, 0:2 * D], ALU.add))
                    did(V.tensor_tensor(sc, rc[:, :, HC], ga, ALU.mult))
                    did(V.tensor_tensor(fixrow[:, S_:SW], fixrow[:, S_:SW], gb, ALU.mult))
                    did(V.tensor_tensor(fixrow[:, S_:SW], fixrow[:, S_:SW], sc, ALU.add))
                    did(V.tensor_tensor(fixrow[:, X_:M_], fixrow[:, X_:M_], bank[:, 5, 0:D], ALU.add))
                    V.tensor_copy(fixrow[:, M_:S_], m1).then_inc(s_carry_v, 1)


def kernel(**inputs):
    import concourse.bacc as bacc
    from concourse.bass_utils import run_bass_kernel_spmd

    x = {k: np.asarray(v) for k, v in inputs.items()}

    def rows(v):
        return np.broadcast_to(v[None, :], (P, D))

    def column(v):
        return np.broadcast_to(v.reshape(-1)[:, None], (P, D))

    def padded(v, fill):
        return np.concatenate([v, np.full((P * COLS - v.shape[0],), fill, v.dtype)]).reshape(P, COLS)

    g = {k[len("L2_gnn_"):]: v for k, v in x.items() if k.startswith("L2_gnn_")}
    fus = g["fus_w"]
    mats = dict(W0=x["L0_gnn_W0"], W1=x["L0_gnn_W1"], W2=x["L0_gnn_W2"], L1_W=x["L1_gnn_W"],
                L1_Wself=x["L1_gnn_W_self"], gat_w=g["gat_w"], gat_wT=g["gat_w"].T, sage_wl=g["sage_wl"],
                sage_wr=g["sage_wr"], wq=g["tr_wq"], wqT=g["tr_wq"].T, wk=g["tr_wk"], wv=g["tr_wv"],
                wskipT=g["tr_wskip"].T, F1=fus[0:D], F2=fus[D:2 * D], F3=fus[2 * D:3 * D],
                Wn1T=x["L3_gnn_W_neigh1"].T, Ws1T=x["L3_gnn_W_self1"].T, Wn2T=x["L3_gnn_W_neigh2"].T,
                Ws2T=x["L3_gnn_W_self2"].T, gat_b_col=column(g["gat_b"]), bskip_col=column(g["tr_bskip"]),
                bv_col=column(g["tr_bv"]), bq_col=column(g["tr_bq"]))
    vecs = dict(b0=x["L0_gnn_b0"], b1=x["L0_gnn_b1"], b2=x["L0_gnn_b2"], sage_bl=g["sage_bl"], bq=g["tr_bq"],
                fus_b=g["fus_b"], ln_g=g["ln_g"], ln_b=g["ln_b"], bn1=x["L3_gnn_b_neigh1"],
                bs1=x["L3_gnn_b_self1"], bn2=x["L3_gnn_b_neigh2"], bs2=x["L3_gnn_b_self2"])
    part = np.arange(P)
    arrays = {
        "x": np.concatenate([x["x"], np.zeros((ROWS - N, D), x["x"].dtype)]),
        "src": padded(x["src"], 0), "dst": padded(x["dst"], N),
        "mats": np.stack([mats[n] for n in MATS], axis=1), "vecs": np.stack([rows(vecs[n]) for n in VECS], axis=1),
        "attc": np.stack([g["gat_att_src"].reshape(-1), g["gat_att_dst"].reshape(-1), g["tr_bk"]], axis=1),
        "ident": np.eye(P, dtype=np.float32),
        "upper": np.triu(np.ones((P, P), np.float32), 1), "lower": np.tril(np.ones((P, P), np.float32), -1),
        "hmask": (part[:, None] // HC == np.arange(HEADS)[None, :]).astype(np.float32),
        "iota": np.tile(np.arange(COLS, dtype=np.float16), (P, 1)),
        "emptyrow": (ROWS + part[:, None]).astype(np.float32),
        "firstrow": (part[:, None] * COLS - 1).astype(np.float32),
    }
    nc = bacc.Bacc("TRN2", target_bir_lowering=False, num_devices=1)
    args, feed = {}, {}
    for name, arr in arrays.items():
        arr = np.ascontiguousarray(arr)
        feed["in_" + name] = arr
        args[name] = nc.dram_tensor("in_" + name, arr.shape, mybir.dt.from_np(arr.dtype), kind="ExternalInput").ap()
    out = nc.dram_tensor("out_0", (ROWS, D), mybir.dt.float32, kind="ExternalOutput").ap()
    gnn_kernel(nc, args, out)
    r = run_bass_kernel_spmd(nc, [feed], core_ids=[0])
    return r.results[0]["out_0"][0:N]
```

```python
from contextlib import ExitStack, contextmanager

import numpy as np

import concourse.bass as bass
from concourse import mybir

P = 128
D = 128
N = 50000
E = 50000
HEADS = 8
HC = D // HEADS
QUAD = 4
BODY = 4
COLS = 392
NQ = COLS // QUAD
TURNS = NQ // BODY
STEP = QUAD * BODY
END_TILE = (COLS - 1) % STEP
ROWS = P * COLS
QA = D + 2 * HEADS
SW = 3 * D + 4 * HEADS
R_, X_, M_, S_ = 0, 2 * D, 3 * D, 3 * D + 2 * HEADS
PROJ = 3 * D + HEADS
NEG = -1.0e30
EPS = 1e-5

MATS = ["W0", "W1", "W2", "L1_W", "L1_Wself", "gat_w", "gat_wT", "sage_wl", "sage_wr", "wq", "wqT", "wk",
        "wv", "wskipT", "F1", "F2", "F3", "Wn1T", "Ws1T", "Wn2T", "Ws2T", "gat_b_col", "bskip_col",
        "bq_col"]
VECS = ["b0", "b1", "b2", "sage_bl", "bq", "fus_b", "ln_g", "ln_b", "bv", "bn1", "bs1", "bn2", "bs2"]

PHASES = [("in", None), ("edge", "g0"), ("gcn", 1), ("edge", "g1"), ("gcn", 2), ("edge", "g2"), ("gcn_out", None),
          ("edge", "h1"), ("conv", None), ("attend", "h2"), ("fuse", None), ("edge", "h3"), ("sage1", None),
          ("edge", "h4"), ("sage2", None)]

COUNTS = {
    "idx": dict(edge=1, gcn=1, gcn_out=1, conv=1, attend=1, fuse=1, sage1=1, sage2=1),
    "idx2": dict(attend=1),
    "summed": dict(edge=4),
    "agg_steps": dict(gcn=1, gcn_out=1),
    "norm_steps": {"in": 4, "gcn_out": 4, "conv": 4, "fuse": 4}, "norm_steps2": dict(fuse=4),
    "stats2": dict(fuse=1), "rstd2": dict(fuse=1), "shift2": dict(fuse=1), "rstd_steps2": dict(fuse=1),
    "front_steps0": dict(attend=7), "front_steps1": dict(attend=7),
    "back_steps0": dict(attend=10), "back_steps1": dict(attend=9),
    "self_steps": dict(fuse=3), "blend_steps": dict(fuse=7), "x3_steps": dict(fuse=1),
    "rstd_steps": {"in": 1, "gcn_out": 1, "conv": 1, "fuse": 1}, "sage_log": dict(fuse=1),
    "agg_ready": dict(gcn=1, fuse=1, sage1=1, sage2=1),
    "transposed": {"in": 1, "gcn": 1, "conv": 1, "attend": 1, "fuse": 1, "sage1": 1, "sage2": 1},
    "own_transposed": dict(conv=1, fuse=1, sage1=1, sage2=1),
    "xt_ready": {"in": 1, "gcn": 1, "conv": 1, "attend": 1, "fuse": 1, "sage1": 1, "sage2": 1},
    "xu_ready": dict(conv=1, fuse=1, sage1=1, sage2=1),
    "product": {"in": 1, "gcn": 1, "conv": 1, "fuse": 1, "sage1": 1, "sage2": 1},
    "biased": {"in": 1, "gcn": 1, "sage1": 1, "sage2": 1},
    "out_ready": {"in": 1, "gcn": 1, "sage1": 1, "sage2": 1},
    "x_ready": dict(gcn_out=1, conv=1, fuse=1),
    "stats": {"in": 1, "gcn_out": 1, "conv": 1, "fuse": 1},
    "rstd": {"in": 1, "gcn_out": 1, "conv": 1, "fuse": 1},
    "shift": {"in": 1, "gcn_out": 1, "conv": 1, "fuse": 1},
    "h_ready": {"in": 1, "gcn_out": 1, "conv": 1, "fuse": 1},
    "h_transposed": dict(conv=1),
    "ht_ready": dict(conv=1),
    "qa_product": dict(conv=1),
    "qa_ready": dict(conv=1),
    "proj0": dict(attend=1), "proj1": dict(attend=1),
    "gaps0": dict(attend=1), "gaps1": dict(attend=1),
    "exps0": dict(attend=1), "exps1": dict(attend=1),
    "proj_used0": dict(attend=1), "proj_used1": dict(attend=1),
    "state_ready": dict(attend=1),
    "based": dict(conv=1), "own_h": dict(fuse=1),
    "self_used": dict(fuse=1),
    "self_gaps": dict(fuse=1), "self_exps": dict(fuse=1),
    "sage_biased": dict(fuse=1), "sage_squares": dict(fuse=4), "sage_floor": dict(fuse=1), "sage_norm": dict(fuse=1),
    "gat_ready": dict(fuse=1), "tr_ready": dict(fuse=1), "sage_ready": dict(fuse=1),
    "parts_transposed": dict(fuse=3), "parts_ready": dict(fuse=3),
    "fused": dict(fuse=1), "normed": dict(fuse=1),
}
GATHERS = dict(edge=64, gcn=64, gcn_out=64, conv=64, attend=128, fuse=64, sage1=64, sage2=64)
LOADS = dict(gcn=16, gcn_out=16, conv=16, fuse=16, sage1=16, sage2=16)
RES_LOADS = {"in": 16, "gcn_out": 16, "conv": 16, "fuse": 16, "sage2": 16}
STORES = dict(
    table={"in": 16, "edge": 16, "gcn": 16, "gcn_out": 16, "conv": 16, "attend": 16, "fuse": 16, "sage1": 16,
           "sage2": 16},
    residual=dict(gcn_out=16, conv=16, fuse=16),
    qa=dict(conv=16))
CREDIT = 10 * BODY


def before(name, f):
    c = COUNTS[name]
    extra = BODY if name in ("idx", "idx2") else 0
    return CREDIT + sum(c[k] * (NQ + 0) + extra for k, _ in PHASES[:f] if k in c)


def before_slot(table, f, b):
    quads = len(range(b, NQ, BODY))
    return (16 if table in STORES.values() else 0) + quads * sum(table.get(k, 0) for k, _ in PHASES[:f])


def gnn_kernel(nc, a, out):
    f32, f16, i32 = mybir.dt.float32, mybir.dt.float16, mybir.dt.int32
    ALU, ACT, AX = mybir.AluOpType, mybir.ActivationFunctionType, mybir.AxisListType
    ctx = ExitStack()

    def sb(name, shape, dt=f32):
        return ctx.enter_context(nc.sbuf_tensor(name, shape, dt))

    def sem(name):
        return ctx.enter_context(nc.semaphore(name))

    def dram(name, rows, width):
        return nc.dram_tensor(name, (rows, width), f32).ap()

    with ctx:
        tab = {n: dram("tab_" + n, ROWS, D) for n in ("g0", "g1", "g2", "h1", "h2", "h3", "h4")}
        tab_qa = dram("tab_qa", ROWS, QA)
        res = {n: dram("res_" + n, ROWS, D) for n in ("x1", "x2", "x3")}
        sums = dram("sums", ROWS + P, D)
        states = dram("states", ROWS + P, SW)

        def cols(t):
            return t[0:ROWS, :].rearrange("(p c) f -> p c f", c=COLS)

        mats = sb("mats", [P, len(MATS), D])
        vecs = sb("vecs", [P, len(VECS), D])
        ident = sb("ident", [P, P])
        upper = sb("upper", [P, P])
        lower = sb("lower", [P, P])
        hmask = sb("hmask", [P, HEADS])
        attc = sb("attc", [P, 3])
        ones = sb("ones", [P, P])
        zero16 = sb("zero16", [P, P], f16)
        iota = sb("iota", [P, COLS], f16)
        emptyrow = sb("emptyrow", [P, 1])
        firstrow = sb("firstrow", [P, 1])
        eps = sb("eps", [P, 1])
        src_i = sb("src_i", [P, COLS + STEP], i32)
        dst_i = sb("dst_i", [P, COLS + STEP], i32)
        last_i = sb("last_i", [P, COLS + STEP], i32)
        dst = sb("dst", [P, COLS])
        same = sb("same", [P, COLS])
        gapneg = sb("gapneg", [P, COLS])
        dinv = sb("dinv", [P, COLS])
        invdeg = sb("invdeg", [P, COLS])
        has = sb("has", [P, COLS])
        stage = sb("stage", [P, STEP], i32)
        stage2 = sb("stage2", [P, STEP], i32)
        carry_mask = sb("carry_mask", [P, P])
        carry_maskT = sb("carry_maskT", [P, P])
        first_end = sb("first_end", [P, 1], i32)
        carry = sb("carry", [P, D])

        G = sb("G", [P, STEP, D])
        L1 = sb("L1", [P, STEP, D])
        L2 = sb("L2", [P, STEP, D])
        O1 = sb("O1", [P, STEP, D])
        O2 = sb("O2", [P, STEP, D])
        ST = sb("ST", [P, STEP, SW])
        QG = sb("QG", [P, STEP, QA])
        XT = sb("XT", [P, 2, QUAD * D])
        XU = sb("XU", [P, BODY, QUAD * D])
        XV = sb("XV", [P, 3, QUAD * D])
        bst = sb("bst", [P, 2, QUAD, 6])
        mv = sb("mv", [P, 2, QUAD, 2])
        rs = sb("rs", [P, 2, 2, QUAD])
        nm = sb("nm", [P, 2, QUAD])
        bst2 = sb("bst2", [P, 2, QUAD, 6])
        mv2 = sb("mv2", [P, 2, QUAD, 2])
        rs2 = sb("rs2", [P, 2, 2, QUAD])
        nm2 = sb("nm2", [P, 2, QUAD])
        WE = sb("WE", [P, PROJ])
        WQA = sb("WQA", [P, QA])
        BQA = sb("BQA", [P, QA])
        WSELF = sb("WSELF", [P, D + HEADS])
        WS3 = sb("WS3", [P, D])
        c0 = sb("c0", [P, D])
        row0 = sb("row0", [P, P])
        bsum = sb("bsum", [P, 2, D])
        blk = sb("blk", [P, 4, HEADS])
        oh_hi = sb("oh_hi", [P, 16, P], f16)
        oh_lo = sb("oh_lo", [P, 16, COLS], f16)
        prod = sb("prod", [P, 2, 2, D])
        red = sb("red", [P, 2, 2, HEADS])
        asum = sb("asum", [P, 2, 2, HEADS])
        lg = sb("lg", [P, 2, 2, 2 * HEADS])
        gaps = sb("gaps", [P, 2, 2, 4 * HEADS])
        exps = sb("exps", [P, 2, 2, 4 * HEADS])
        tmp = sb("tmp", [P, 2, 2 * D])
        sage = sb("sage", [P, 2, QUAD, D])
        hself = sb("hself", [P, QUAD, D])
        zn = sb("zn", [P, 2, QUAD, D])
        sq = sb("sq", [P, D])
        ss = sb("ss", [P, 2, 3, QUAD])
        sgap = sb("sgap", [P, 2, QUAD, 2 * HEADS])
        sexp = sb("sexp", [P, 2, QUAD, 2 * HEADS])
        slog = sb("slog", [P, QUAD, HEADS])
        sm = sb("sm", [P, QUAD, HEADS])
        zz = sb("zz", [P, QUAD, 2 * HEADS])
        lnb = sb("lnb", [P, 1])

        t_f = [L1[:, :, :].rearrange("p c f -> p (c f)")[:, k * COLS:(k + 1) * COLS] for k in range(5)]
        t_i = QG[:, :, :].rearrange("p c f -> p (c f)")[:, 0:COLS].bitcast(i32)
        cm = L1[:, :, :].rearrange("p c f -> p (c f)")[:, 0:2 * HEADS * P].rearrange("p (h q) -> p h q", h=2 * HEADS)
        cmT = L2[:, :, :].rearrange("p c f -> p (c f)")[:, 0:2 * HEADS * P].rearrange("p (h q) -> p h q", h=2 * HEADS)
        rsv = O1[:, :, :].rearrange("p c f -> p (c f)")[:, 0:2 * HEADS * (HC + 1)].rearrange(
            "p (h e) -> p h e", h=2 * HEADS)
        fixrow = O2[:, :, :].rearrange("p c f -> p (c f)")[:, 0:SW]
        fixtmp = O2[:, :, :].rearrange("p c f -> p (c f)")[:, 512:512 + SW]
        mc = O2[:, :, :].rearrange("p c f -> p (c f)")[:, 1024:1024 + 6 * 16].rearrange("p (k h) -> p k h", k=6)

        bank = ctx.enter_context(nc.psum_tensor("bank", [P, 8, 512], f32))

        wide34 = bank[:, 3:5, :].rearrange("p a (t c) -> p (a t) c", t=2)
        wide67 = bank[:, 6:8, :].rearrange("p a (t c) -> p (a t) c", t=2)

        def key_bank(h):
            return bank[:, 2 + h, 0:512].rearrange("p (c f) -> p c f", c=2)[:, :, 0:D + HEADS]

        def value_bank(b, h):
            return bank[:, 4 + 2 * (b % 2) + h, :].rearrange("p (c f) -> p c f", c=2)

        S = {n: sem(n) for n in COUNTS}
        gathered = [sem(f"gathered{b}") for b in range(BODY)]
        loaded = [sem(f"own_loaded{b}") for b in range(BODY)]
        res_loaded = [sem(f"residual_loaded{b}") for b in range(BODY)]
        stored = {n: [sem(f"{n}_stored{b}") for b in range(BODY)] for n in STORES}
        s_const = sem("constants")
        s_pool = sem("pool_setup")
        s_poolw = sem("pool_waited")
        s_dvew = sem("vector_waited")
        s_spw = sem("sync_waited")
        s_actw = sem("scalar_waited")
        s_zero = sem("zero_rows")
        s_onehot = sem("onehot")
        s_hist = sem("histogram")
        s_prep = sem("setup_product")
        s_prepd = sem("setup_vector")
        s_dve = sem("vector_step")
        s_act = sem("scalar_step")
        s_carry_p = sem("carry_product")
        s_carry_v = sem("carry_vector")
        s_carry_d = sem("carry_stored")
        s_fixg = sem("fix_gathered")
        s_acarry = sem("carry_weights")
        s_cgap = sem("carry_gaps")
        BLK, DEG, TOTALS, DIAG, SETUP_END = 4, 20, 25, 32, 53

        def mat(name):
            return mats[:, MATS.index(name), :]

        def vec(name):
            return vecs[:, VECS.index(name), :]

        def over_quad(row):
            return row.unsqueeze(1).to_broadcast([P, QUAD, row.shape[-1]])

        def quad(t, b):
            return t[:, QUAD * b:QUAD * (b + 1), :]

        def per_col(t, i, b):
            return t[:, bass.ds(STEP * i + QUAD * b, QUAD)].unsqueeze(2).to_broadcast([P, QUAD, D])

        def reach(name, f, i, b, part=1):
            c = COUNTS[name][PHASES[f][0]]
            return before(name, f) + (i * BODY + b) * c + part

        def freed(name, f, i, b, ring):
            c = COUNTS[name][PHASES[f][0]]
            return before(name, f) + (i * BODY + b - ring + 1) * c

        def slot_done(table, f, i, b):
            return before_slot(table, f, b) + table[PHASES[f][0]] * (i + 1)

        def all_stored(eng, f):
            for name in STORES:
                for b in range(BODY):
                    eng.wait_ge(stored[name][b], before_slot(STORES[name], f, b))

        def slot_stored(eng, name, f, i, b):
            eng.wait_ge(stored[name][b], slot_done(STORES[name], f, i - 1, b))

        def run(eng, stages):
            deepest = max(lag for _, lag in stages)
            peeled = max(1, -(-deepest // BODY))
            for s in range(peeled * BODY):
                for fn, lag in stages:
                    if s >= lag:
                        fn((s - lag) // BODY, (s - lag) % BODY)
            with eng.Fori(peeled, TURNS) as i:
                for s in range(BODY):
                    for fn, lag in stages:
                        fn(i + (s - lag) // BODY, (s - lag) % BODY)
            for s in range(deepest + NQ % BODY):
                for fn, lag in stages:
                    if s < lag + NQ % BODY:
                        fn(TURNS + (s - lag) // BODY, (s - lag) % BODY)

        consts = [(mats, "mats"), (vecs, "vecs"), (ident, "ident"), (upper, "upper"), (lower, "lower"),
                  (hmask, "hmask"), (attc, "attc"), (iota, "iota"), (emptyrow, "emptyrow"), (firstrow, "firstrow"), (row0, "row0")]

        def kind(f):
            return PHASES[f][0]

        def prior_tiles(b, k):
            return (QUAD * b + k - 1) % STEP

        block = ctx.enter_context(nc.Block())

        @block.sync
        def _(sp):
            for s in S.values():
                sp.sem_inc(s, CREDIT)
            for t, name in consts:
                sp.dma_start(t[:], a[name]).then_inc(s_const, 16)
            sp.dma_start(src_i[:, 0:COLS], a["src"]).then_inc(s_const, 16)
            sp.dma_start(dst_i[:, 0:COLS], a["dst"]).then_inc(s_const, 16)
            sp.wait_ge(s_zero, 1)
            slots = [x for name in STORES for x in stored[name]]
            part = P // (len(slots) // 2)
            for n, x in enumerate(slots):
                t, d = ((G, sums), (ST, states))[n % 2]
                of = slice(n // 2 * part, (n // 2 + 1) * part if n // 2 < len(slots) // 2 - 1 else P)
                sp.dma_start(d[ROWS + of.start:ROWS + of.stop, :], t[of, 0, :]).then_inc(x, 16)

            for f in range(len(PHASES)):
                k, what = PHASES[f]
                all_stored(sp, f)
                if k == "fuse":
                    sp.wait_ge(s_carry_d, 16 * sum(kk in ("edge", "attend") for kk, _ in PHASES[:f]))
                own = {"gcn": tab.get(f"g{(what or 0) - 1}" if k == "gcn" else ""), "gcn_out": tab["g2"],
                       "conv": tab["h1"], "fuse": tab["h2"], "sage1": tab["h3"], "sage2": tab["h4"]}.get(k)
                residual = {"in": a["x"], "gcn_out": a["x"], "conv": res["x1"], "fuse": res["x2"],
                            "sage2": res["x3"]}.get(k)
                own_reader = {"gcn": "agg_ready", "gcn_out": "x_ready"}.get(k, "own_transposed")
                residual_reader = {"in": "h_ready", "sage2": "out_ready"}.get(k, "x_ready")
                stores = {"in": [("table", O1, tab["g0"], "out_ready", 4)],
                          "edge": [("table", G, sums, "summed", 0)],
                          "gcn": [("table", O1, tab.get(f"g{what}"), "out_ready", 2)],
                          "gcn_out": [("table", O1, tab["h1"], "h_ready", 1), ("residual", O2, res["x1"], "x_ready", 0)],
                          "conv": [("qa", QG, tab_qa, "qa_ready", 4), ("table", O1, tab["h2"], "h_ready", 2),
                                   ("residual", ST[:, :, 0:D], res["x2"], "based", 1)],
                          "attend": [("table", ST, states, "state_ready", 1)],
                          "fuse": [("table", O1, tab["h3"], "h_ready", 5), ("residual", O2, res["x3"], "x_ready", 4)],
                          "sage1": [("table", O1, tab["h4"], "out_ready", 2)],
                          "sage2": [("table", O1, out, "out_ready", 2)]}[k]

                def load(t, d, reader, sems, i, b):
                    sp.wait_ge(S[reader], freed(reader, f, i, b, BODY))
                    sp.sem_inc(s_spw, 1)
                    sp.dma_start(quad(t, b), cols(d)[:, bass.ds(STEP * i + QUAD * b, QUAD), :])\
                      .then_inc(sems[b], 16)

                def load_own(i, b):
                    load(L1, own, own_reader, loaded, i, b)

                def load_residual(i, b):
                    load(L2, residual, residual_reader, res_loaded, i, b)

                def store_of(name, t, d, maker):
                    def go(i, b):
                        sp.wait_ge(S[maker], reach(maker, f, i, b, COUNTS[maker][k]))
                        sp.sem_inc(s_spw, 1)
                        sp.dma_start(cols(d)[:, bass.ds(STEP * i + QUAD * b, QUAD), :], quad(t, b))\
                          .then_inc(stored[name][b], 16)
                    return go

                run(sp, [(load_own, 0)] * (own is not None)
                    + [(load_residual, 2 if k == "fuse" else 0)] * (residual is not None)
                    + [(store_of(*spec), lag + 2) for *spec, lag in stores])
            all_stored(sp, len(PHASES))

        @block.gpsimd
        def _(pool):
            for t, val in ((ones, 1.0), (eps, EPS), (zero16, 0.0), (lnb, 10.0 * float(np.log(2.0)))):
                pool.memset(t[:], val).then_inc(s_pool, 1)
            pool.memset(src_i[:, COLS:], 0).then_inc(s_pool, 1)
            pool.memset(dst_i[:, COLS:], 0).then_inc(s_pool, 1)
            pool.memset(last_i[:, COLS:], 0).then_inc(s_pool, 1)
            pool.wait_ge(s_prepd, DEG)
            pool.wait_ge(s_pool, 7)
            pool.memset(t_f[4], -0.5).then_inc(s_pool, 1)
            pool.wait_ge(s_pool, 8)
            pool.tensor_tensor(dinv[:, :], t_f[1], t_f[4], ALU.pow).then_inc(s_pool, 1)

            def gather(dest, table, index):
                return pool.indirect_dma_start(
                    out=dest, out_offset=None, in_=table, in_offset=bass.IndirectOffsetOnAxis(ap=index, axis=0))

            waits = 0
            carries = 0
            for f in range(len(PHASES)):
                k, what = PHASES[f]
                if k == "in":
                    continue
                all_stored(pool, f)
                if k not in ("edge", "attend"):
                    pool.wait_ge(s_carry_d, 16 * carries)
                readers = {"edge": ["summed"], "gcn": ["transposed"], "gcn_out": ["x_ready"],
                           "conv": ["transposed"], "attend": ["state_ready"], "fuse": ["parts_transposed"],
                           "sage1": ["transposed"], "sage2": ["transposed"]}[k]

                def step(i, b):
                    pool.wait_ge(S["idx"], reach("idx", f, i, b))
                    if k == "attend":
                        pool.wait_ge(S["idx2"], reach("idx2", f, i, b))
                    for r in readers:
                        ring = BODY - 1 if k == "edge" else BODY
                        pool.wait_ge(S[r], freed(r, f, i, b, ring))
                    if k == "edge":
                        slot_stored(pool, "table", f, i, b)
                    pool.sem_inc(s_poolw, 1)
                    for c in range(QUAD):
                        t = QUAD * b + c
                        if k in ("edge", "attend"):
                            gather(G[:, t, :], tab[what], stage[:, t:t + 1]).then_inc(gathered[b], 16)
                        elif k == "fuse":
                            gather(ST[:, t, :], states, stage[:, t:t + 1]).then_inc(gathered[b], 16)
                        else:
                            gather(G[:, t, :], sums, stage[:, t:t + 1]).then_inc(gathered[b], 16)
                        if k == "attend":
                            gather(QG[:, t, :], tab_qa, stage2[:, t:t + 1]).then_inc(gathered[b], 16)

                run(pool, [(step, 0)])
                if k == "edge":
                    carries += 1
                    all_stored(pool, f + 1)
                    pool.wait_ge(s_carry_v, carries)
                    pool.indirect_dma_start(
                        out=sums, out_offset=bass.IndirectOffsetOnAxis(ap=first_end[:, 0:1], axis=0),
                        in_=carry[:, :], in_offset=None, compute_op=ALU.add).then_inc(s_carry_d, 16)
                if k == "attend":
                    carries += 1
                    all_stored(pool, f + 1)
                    gather(fixrow, states, first_end[:, 0:1]).then_inc(s_fixg, 16)
                    pool.wait_ge(s_carry_v, carries)
                    pool.indirect_dma_start(
                        out=states, out_offset=bass.IndirectOffsetOnAxis(ap=first_end[:, 0:1], axis=0),
                        in_=fixrow, in_offset=None).then_inc(s_carry_d, 16)

        @block.tensor
        def _(pe):
            prep = [0]

            def product(out_, lhsT, rhs, start=True, stop=True):
                return nc.tensor.matmul(out_, lhsT, rhs, start=start, stop=stop)

            pe.wait_ge(s_const, 16 * (len(consts) + 2))
            pe.wait_ge(s_pool, 4)
            product(bank[:, 0, 0:COLS], zero16[:, :], iota[:, 0:COLS], True, False).then_inc(s_hist, 1)
            with pe.Fori(0, COLS // 16) as i:
                for c in range(16):
                    pe.wait_ge(s_onehot, i * 32 + 2 * c + 2)
                    product(bank[:, 0, 0:COLS], oh_hi[:, c, :], oh_lo[:, c, :], False, False).then_inc(s_hist, 1)
            for c in range(COLS % 16):
                pe.wait_ge(s_onehot, 2 * (COLS - COLS % 16 + c + 1))
                product(bank[:, 0, 0:COLS], oh_hi[:, c, :], oh_lo[:, c, :], False, False).then_inc(s_hist, 1)
            product(bank[:, 0, 0:COLS], zero16[:, :], iota[:, 0:COLS], False, True).then_inc(s_hist, 1)

            def prep_product(*args):
                product(*args).then_inc(s_prep, 1)

            pe.wait_ge(s_prepd, BLK)
            prep_product(bank[:, 1, 0:HEADS], mat("gat_wT"), blk[:, 0, :])
            prep_product(bank[:, 1, 16:16 + HEADS], mat("gat_wT"), blk[:, 1, :])
            prep_product(bank[:, 1, 32:32 + HEADS], mat("gat_wT"), blk[:, 2, :])
            prep_product(bank[:, 1, 48:48 + HEADS], mat("wqT"), blk[:, 3, :])
            prep_product(bank[:, 1, 64:64 + HEADS], mat("bq_col"), blk[:, 3, :])
            prep_product(bank[:, 2, 0:D], mat("wskipT"), mat("F3"))
            product(bank[:, 3, 0:D], mat("gat_b_col"), mat("F1"), True, False)
            prep_product(bank[:, 3, 0:D], mat("bskip_col"), mat("F3"), False, True)
            pe.wait_ge(s_prepd, TOTALS)
            prep_product(bank[:, 5, 0:1], upper[:, :], t_f[2][:, COLS - 1:COLS])
            pe.wait_ge(s_prepd, DIAG)
            prep_product(bank[:, 6, 0:P], ones[:, :], XT[:, 0, 0:P])
            prep_product(bank[:, 6, P:2 * P], ones[:, :], XT[:, 0, P:2 * P])
            pe.wait_ge(s_prepd, SETUP_END)

            carries = 0
            for f in range(len(PHASES)):
                k, what = PHASES[f]

                if k == "edge":
                    carries += 1
                    pe.wait_ge(S["summed"], before("summed", f + 1))
                    product(bank[:, 0, 0:D], carry_mask[:, :], G[:, END_TILE, :]).then_inc(s_carry_p, 1)
                    pe.wait_ge(s_carry_v, carries)
                    continue

                def transposes(dest, tile, signal):
                    for c in range(QUAD):
                        ins = nc.tensor.transpose(dest[:, c * D:(c + 1) * D], tile(c), ident[:, :])
                    ins.then_inc(signal, 1)

                def first(i, b):
                    p = b % 2
                    if k == "in":
                        pe.wait_ge(S["h_ready"], reach("h_ready", f, i, b))
                    elif "agg_ready" in COUNTS and k in COUNTS["agg_ready"]:
                        pe.wait_ge(S["agg_ready"], reach("agg_ready", f, i, b))
                    else:
                        pe.wait_ge(gathered[b], slot_done(GATHERS, f, i, b))
                    pe.wait_ge(S["xt_ready"], freed("xt_ready", f, i, b, 1 if k in ("fuse", "conv") else 2))
                    source = {"in": lambda c: O2[:, QUAD * b + c, :],
                              "fuse": lambda c: ST[:, QUAD * b + c, X_:X_ + D]}.get(k, lambda c: G[:, QUAD * b + c, :])
                    transposes(bank[:, 0 if k in ("fuse", "conv") else p, :], source, S["transposed"])
                    if k in ("conv", "sage1", "sage2", "fuse"):
                        pe.wait_ge(loaded[b], slot_done(LOADS, f, i, b))
                        pe.wait_ge(S["xu_ready"], freed("xu_ready", f, i, b, 1 if k in ("fuse", "conv") else 2))
                        transposes(bank[:, 1 if k in ("fuse", "conv") else 2 + p, :], lambda c: L1[:, QUAD * b + c, :],
                                   S["own_transposed"])

                def second(i, b):
                    p = b % 2
                    pe.wait_ge(S["xt_ready"], reach("xt_ready", f, i, b))
                    two = k in ("conv", "sage1", "sage2")
                    if two:
                        pe.wait_ge(S["xu_ready"], reach("xu_ready", f, i, b))
                    user = "x_ready" if k == "conv" else "biased"
                    pe.wait_ge(S[user], freed(user, f, i, b, 2))
                    w1, w2 = {"in": ("W0", None), "gcn": (f"W{what}", None), "conv": ("L1_W", "L1_Wself"),
                              "sage1": ("Wn1T", "Ws1T"), "sage2": ("Wn2T", "Ws2T")}[k]
                    o = bank[:, 4 + p, :]
                    for c in range(QUAD):
                        w = slice(c * D, (c + 1) * D)
                        ins = product(o[:, w], XT[:, p, w], mat(w1), True, not two)
                        if two:
                            ins = product(o[:, w], XU[:, b, w], mat(w2), False, True)
                    ins.then_inc(S["product"], 1)

                def h_transpose(i, b):
                    pe.wait_ge(S["h_ready"], reach("h_ready", f, i, b))
                    pe.wait_ge(S["ht_ready"], freed("ht_ready", f, i, b, 1))
                    transposes(bank[:, 2, :], lambda c: O1[:, QUAD * b + c, :], S["h_transposed"])

                def h_product(i, b):
                    pe.wait_ge(S["ht_ready"], reach("ht_ready", f, i, b))
                    pe.wait_ge(S["qa_ready"], freed("qa_ready", f, i, b, 1))
                    for c in range(QUAD):
                        ins = product(bank[:, 6 + c // 2, 256 * (c % 2):256 * (c % 2) + QA],
                                      XV[:, b % 2, c * D:(c + 1) * D], WQA[:, :])
                    ins.then_inc(S["qa_product"], 1)

                def project(i, b):
                    pe.wait_ge(S["xt_ready"], reach("xt_ready", f, i, b))
                    for h in range(2):
                        keys, used = f"front_steps{h}", f"proj_used{h}"
                        pe.wait_ge(S[keys], freed(keys, f, i, b, 1))
                        pe.wait_ge(S[used], freed(used, f, i, b, 2))
                        for c in (2 * h, 2 * h + 1):
                            x, kb, vb = XT[:, b % 2, c * D:(c + 1) * D], key_bank(h), value_bank(b, h)
                            product(kb[:, c % 2, :], x, WE[:, 2 * D:PROJ])
                            product(vb[:, c % 2, :], x, WE[:, 0:2 * D], True, False)
                            ins = product(vb[:, c % 2, D:2 * D], row0[:, :], vec("bv"), False, True)
                        ins.then_inc(S[f"proj{h}"], 1)

                def logits_and_sage(i, b):
                    pe.wait_ge(S["xt_ready"], reach("xt_ready", f, i, b))
                    pe.wait_ge(S["xu_ready"], reach("xu_ready", f, i, b))
                    pe.wait_ge(S["self_gaps"], freed("self_gaps", f, i, b, 1))
                    pe.wait_ge(S["sage_biased"], freed("sage_biased", f, i, b, 1))
                    for c in range(QUAD):
                        w, o = slice(c * D, (c + 1) * D), wide34[:, c, :]
                        product(o[:, 0:D + HEADS], XU[:, b, w], WSELF[:, :], True, False)
                        ins = product(o[:, 0:D], XT[:, b % 2, w], mat("sage_wl"), False, True)
                    ins.then_inc(S["product"], 1)

                def own_h(i, b):
                    pe.wait_ge(S["self_used"], freed("self_used", f, i, b, 1))
                    for c in range(QUAD):
                        w = slice(c * D, (c + 1) * D)
                        ins = product(bank[:, 2, w], XU[:, b, w], mat("gat_w"))
                    ins.then_inc(S["own_h"], 1)

                def gat_and_tr(i, b):
                    for n, ready in enumerate(("gat_ready", "tr_ready")):
                        pe.wait_ge(S[ready], reach(ready, f, i, b))
                        pe.wait_ge(S["parts_ready"], freed("parts_ready", f, i, b, 1))
                        transposes(bank[:, 5 + n, :], lambda c: ST[:, QUAD * b + c, n * D:(n + 1) * D],
                                   S["parts_transposed"])

                def sage_part(i, b):
                    pe.wait_ge(S["sage_ready"], reach("sage_ready", f, i, b))
                    pe.wait_ge(S["parts_ready"], reach("parts_ready", f, i, b, 1))
                    transposes(bank[:, 5, :], lambda c: sage[:, b % 2, c, :], S["parts_transposed"])

                def fuse_product(i, b):
                    pe.wait_ge(S["parts_ready"], reach("parts_ready", f, i, b, 3))
                    pe.wait_ge(S["normed"], freed("normed", f, i, b, 1))
                    for c in range(QUAD):
                        w = slice(c * D, (c + 1) * D)
                        product(bank[:, 7, w], row0[:, :], c0[:, :], True, False)
                        product(bank[:, 7, w], XU[:, b, w], WS3[:, :], False, False)
                        product(bank[:, 7, w], XV[:, 0, w], mat("F1"), False, False)
                        product(bank[:, 7, w], XV[:, 1, w], mat("F3"), False, False)
                        ins = product(bank[:, 7, w], XV[:, 2, w], mat("F2"), False, True)
                    ins.then_inc(S["fused"], 1)

                if k == "in":
                    run(pe, [(second, 3), (first, 2)])
                elif k in ("gcn", "sage1", "sage2"):
                    run(pe, [(second, 1), (first, 0)])
                elif k == "conv":
                    run(pe, [(second, 1), (h_transpose, 3), (h_product, 4), (first, 0)])
                elif k == "attend":
                    run(pe, [(project, 1), (first, 0)])
                    carries += 1
                    pe.wait_ge(s_acarry, 1)
                    for n in range(4):
                        ins = product(bank[:, n, :], ones[:, :],
                                      cm[:, 4 * n:4 * n + 4, :].rearrange("p h q -> p (h q)"))
                    ins.then_inc(s_carry_p, 1)
                    pe.wait_ge(s_acarry, 2)
                    for n in range(2 * HEADS):
                        ins = nc.tensor.transpose(bank[:, n // 4, (n % 4) * P:(n % 4 + 1) * P], cm[:, n, :], ident[:, :])
                    ins.then_inc(s_carry_p, 1)
                    pe.wait_ge(s_acarry, 3)
                    for n in range(2 * HEADS):
                        product(bank[:, 4, n * (HC + 1):(n + 1) * (HC + 1)], cmT[:, n, :], rsv[:, n, :])
                    product(bank[:, 5, 0:D], carry_mask[:, :], ST[:, END_TILE, X_:X_ + D]).then_inc(s_carry_p, 1)
                    pe.wait_ge(s_carry_v, carries)
                elif k == "fuse":
                    run(pe, [(logits_and_sage, 1), (fuse_product, 3), (gat_and_tr, 2), (first, 0),
                             (sage_part, 2), (own_h, 1)])

        @block.scalar
        def _(act):
            act.preload_act_table_set("natural_log_exp_and_others")
            act.wait_ge(s_pool, 4)

            for f in range(len(PHASES)):
                k, what = PHASES[f]

                def copy(dest, source, waits, signal):
                    for w in waits:
                        act.wait_ge(*w)
                    nc.scalar.activation(dest, source, ACT.Copy).then_inc(signal, 1)

                def copies(i, b):
                    p = b % 2
                    user = {"attend": "proj1"}.get(k, "product")
                    copy(XT[:, p, :], bank[:, 0 if k in ("fuse", "conv") else p, :],
                         [(S["transposed"], reach("transposed", f, i, b)), (S[user], freed(user, f, i, b, 2))],
                         S["xt_ready"])
                    if k in ("conv", "sage1", "sage2", "fuse"):
                        user = {"fuse": "fused"}.get(k, "product")
                        copy(XU[:, b, :], bank[:, 1 if k in ("fuse", "conv") else 2 + p, :],
                             [(S["own_transposed"], reach("own_transposed", f, i, b)),
                              (S[user], freed(user, f, i, b, BODY))], S["xu_ready"])

                def rstd_of(mvt, rst, n=""):
                    def go(i, b):
                        p = b % 2
                        act.wait_ge(S["stats" + n], reach("stats" + n, f, i, b))
                        nc.scalar.activation(rst[:, p, 0, :], mvt[:, p, :, 1], ACT.Ln, bias=eps[:, 0:1])\
                          .then_inc(S["rstd_steps" + n], 1)
                        act.wait_ge(S["rstd_steps" + n], reach("rstd_steps" + n, f, i, b))
                        nc.scalar.activation(rst[:, p, 1, :], rst[:, p, 0, :], ACT.Exp, scale=-0.5)\
                          .then_inc(S["rstd" + n], 1)
                    return go

                rstd = rstd_of(mv, rs)

                def relu_of(source, rst, nmt, n=""):
                    def go(i, b):
                        p = b % 2
                        act.wait_ge(S["shift" + n], reach("shift" + n, f, i, b))
                        if k == "in":
                            act.wait_ge(S["transposed"], freed("transposed", f, i, b, BODY))
                        else:
                            slot_stored(act, "table", f, i, b)
                        if k == "conv":
                            act.wait_ge(S["h_transposed"], freed("h_transposed", f, i, b, BODY))
                        dest = O2 if k == "in" else O1
                        for c in range(QUAD):
                            ins = nc.scalar.activation(dest[:, QUAD * b + c, :], source[:, QUAD * b + c, :], ACT.Relu,
                                                       bias=nmt[:, p, c:c + 1], scale=rst[:, p, 1, c:c + 1])
                        ins.then_inc(S["h_ready"], 1)
                    return go

                relu = relu_of(L2 if k == "in" else O2, rs, nm)

                def h_copy(i, b):
                    copy(XV[:, b % 2, :], bank[:, 2, :],
                         [(S["h_transposed"], reach("h_transposed", f, i, b)),
                          (S["qa_product"], freed("qa_product", f, i, b, 2))], S["ht_ready"])

                def exp_of(h):
                    def go(i, b):
                        act.wait_ge(S[f"gaps{h}"], reach(f"gaps{h}", f, i, b))
                        back = f"back_steps{h}"
                        act.wait_ge(S[back], freed(back, f, i, b, 1))
                        if h == 1:
                            act.wait_ge(S["state_ready"], freed("state_ready", f, i, b, 1))
                        nc.scalar.activation(exps[:, h, :, :], gaps[:, h, :, :], ACT.Exp).then_inc(S[f"exps{h}"], 1)
                    return go

                def self_exp(i, b):
                    act.wait_ge(S["self_gaps"], reach("self_gaps", f, i, b))
                    nc.scalar.activation(sexp[:, b % 2, :, :], sgap[:, b % 2, :, :], ACT.Exp)\
                      .then_inc(S["self_exps"], 1)

                def squares(i, b):
                    p = b % 2
                    act.wait_ge(S["sage_biased"], reach("sage_biased", f, i, b))
                    for c in range(QUAD):
                        if c:
                            act.wait_ge(S["sage_squares"], reach("sage_squares", f, i, b, c))
                        nc.scalar.activation(sq[:, :], sage[:, p, c, :], ACT.Square,
                                             accum_out=ss[:, p, 0, c:c + 1]).then_inc(S["sage_squares"], 1)

                def norm(i, b):
                    p = b % 2
                    act.wait_ge(S["sage_floor"], reach("sage_floor", f, i, b))
                    nc.scalar.activation(ss[:, p, 1, :], ss[:, p, 1, :], ACT.Ln, scale=float(2 ** 20))\
                      .then_inc(S["sage_log"], 1)
                    act.wait_ge(S["sage_log"], reach("sage_log", f, i, b))
                    nc.scalar.activation(ss[:, p, 2, :], ss[:, p, 1, :], ACT.Exp, scale=-0.5, bias=lnb[:, 0:1])\
                      .then_inc(S["sage_norm"], 1)

                def part_copy(n):
                    def go(i, b):
                        copy(XV[:, n, :], bank[:, 5 + n % 2, :],
                             [(S["parts_transposed"], reach("parts_transposed", f, i, b, n + 1)),
                              (S["fused"], freed("fused", f, i, b, 1))], S["parts_ready"])
                    return go

                def mean(i, b):
                    act.wait_ge(gathered[b], slot_done(GATHERS, f, i, b))
                    act.sem_inc(s_actw, 1)
                    for c in range(QUAD):
                        x = ST[:, QUAD * b + c, X_:X_ + D]
                        ins = nc.scalar.activation(x, x, ACT.Copy,
                                                   scale=invdeg[:, bass.ds(STEP * i + QUAD * b + c, 1)])
                    ins.then_inc(S["agg_ready"], 1)

                def normed(i, b):
                    p = b % 2
                    act.wait_ge(S["shift"], reach("shift", f, i, b))
                    act.wait_ge(S["x_ready"], freed("x_ready", f, i, b, 2))
                    for c in range(QUAD):
                        ins = nc.scalar.activation(zn[:, p, c, :], bank[:, 7, c * D:(c + 1) * D], ACT.Identity,
                                                   bias=nm[:, p, c:c + 1], scale=rs[:, p, 1, c:c + 1])
                    ins.then_inc(S["normed"], 1)

                if k == "in":
                    run(act, [(relu, 1), (copies, 2), (rstd, 0)])
                elif k in ("gcn", "sage1", "sage2"):
                    run(act, [(copies, 0)])
                elif k == "gcn_out":
                    run(act, [(relu, 1), (rstd, 0)])
                elif k == "conv":
                    run(act, [(relu, 2), (h_copy, 3), (copies, 0), (rstd, 1)])
                elif k == "attend":
                    run(act, [(exp_of(0), 1), (exp_of(1), 1), (copies, 0)])
                    act.wait_ge(s_cgap, 1)
                    nc.scalar.activation(cm, cm, ACT.Exp).then_inc(s_act, 1)
                    act.wait_ge(s_cgap, 2)
                    nc.scalar.activation(mc[:, 2:4, :], mc[:, 2:4, :], ACT.Exp).then_inc(s_act, 1)
                elif k == "fuse":
                    run(act, [(normed, 4), (norm, 2), (relu_of(O2, rs2, nm2, "2"), 5), (mean, 0),
                              (part_copy(0), 2), (part_copy(1), 2), (copies, 0), (rstd_of(mv2, rs2, "2"), 4),
                              (part_copy(2), 2), (self_exp, 1), (squares, 1), (rstd, 3)])

        @block.vector
        def _(dve):
            V = nc.vector
            steps = [0]

            def prep(ins):
                steps[0] += 1
                ins.then_inc(s_prepd, 1)
                dve.wait_ge(s_prepd, steps[0])

            dve.wait_ge(s_const, 16 * (len(consts) + 2))
            prep(V.tensor_scalar(blk[:, 0, :], hmask[:, :], attc[:, 0:1], None, ALU.mult))
            prep(V.tensor_scalar(blk[:, 1, :], hmask[:, :], attc[:, 1:2], None, ALU.mult))
            prep(V.tensor_scalar(blk[:, 3, :], hmask[:, :], attc[:, 2:3], None, ALU.mult))
            prep(V.tensor_tensor(blk[:, 2, :], blk[:, 0, :], blk[:, 1, :], ALU.add))
            assert steps[0] == BLK
            prep(V.memset(G[:, :, :], 0.0))
            V.memset(ST[:, :, :], 0.0).then_inc(s_zero, 1)
            prep(V.tensor_copy(dst[:, :], dst_i[:, 0:COLS]))
            prep(V.memset(same[:, 0:1], 0.0))
            prep(V.tensor_tensor(same[:, 1:COLS], dst[:, 1:COLS], dst[:, 0:COLS - 1], ALU.is_equal))
            prep(V.tensor_scalar(gapneg[:, :], same[:, :], 1.0, -NEG, ALU.subtract, ALU.mult))
            quot, hi, lo, flag, _ = t_f
            prep(V.tensor_scalar(quot, dst[:, :], 1.0 / COLS, None, ALU.mult))
            prep(V.tensor_copy(t_i, quot))
            prep(V.tensor_copy(hi, t_i))
            prep(V.scalar_tensor_tensor(out=lo, in0=hi, scalar=-float(COLS), in1=dst[:, :], op0=ALU.mult, op1=ALU.add))
            prep(V.tensor_scalar(flag, lo, 0.0, None, ALU.is_lt))
            prep(V.tensor_tensor(hi, hi, flag, ALU.subtract))
            prep(V.tensor_scalar(flag, lo, float(COLS), None, ALU.is_ge))
            prep(V.tensor_tensor(hi, hi, flag, ALU.add))
            prep(V.scalar_tensor_tensor(out=lo, in0=hi, scalar=-float(COLS), in1=dst[:, :], op0=ALU.mult, op1=ALU.add))

            def onehots(col, c):
                V.tensor_scalar(oh_hi[:, c, :], iota[:, 0:P], hi[:, col:col + 1] if isinstance(col, int)
                                else hi[:, bass.ds(col, 1)], None, ALU.is_equal).then_inc(s_onehot, 1)
                V.tensor_scalar(oh_lo[:, c, :], iota[:, :], lo[:, col:col + 1] if isinstance(col, int)
                                else lo[:, bass.ds(col, 1)], None, ALU.is_equal).then_inc(s_onehot, 1)

            for c in range(16):
                onehots(c, c)
            with dve.Fori(1, COLS // 16) as i:
                for c in range(16):
                    dve.wait_ge(s_hist, (i - 1) * 16 + c + 2)
                    onehots(i * 16 + c, c)
            for c in range(COLS % 16):
                dve.wait_ge(s_hist, COLS - COLS % 16 - 16 + c + 2)
                onehots(COLS - COLS % 16 + c, c)
            dve.wait_ge(s_hist, COLS + 2)
            deg, deg1, run_, t3, _ = t_f
            prep(V.tensor_copy(deg, bank[:, 0, 0:COLS]))
            prep(V.tensor_scalar(deg1, deg, 1.0, None, ALU.add))
            assert steps[0] == DEG
            prep(V.tensor_scalar(t3, deg, 1.0, None, ALU.max))
            prep(V.reciprocal(invdeg[:, :], t3))
            prep(V.tensor_scalar(has[:, :], deg, 0.0, None, ALU.is_gt))
            prep(V.memset(t3, 1.0))
            prep(V.tensor_tensor_scan(run_, t3, deg, 0.0, ALU.mult, ALU.add))
            assert steps[0] == TOTALS
            dve.wait_ge(s_prep, 8)
            prep(V.tensor_copy(t3[:, 0:1], bank[:, 5, 0:1]))
            prep(V.tensor_scalar(run_, run_, t3[:, 0:1], -1.0, ALU.add, ALU.add))
            prep(V.tensor_scalar(run_, run_, emptyrow[:, 0:1], None, ALU.subtract))
            prep(V.tensor_tensor(run_, run_, has[:, :], ALU.mult))
            prep(V.tensor_scalar(last_i[:, 0:COLS], run_, emptyrow[:, 0:1], None, ALU.add))
            prep(V.tensor_scalar(XT[:, 0, 0:P], ident[:, :], dst[:, 0:1], None, ALU.mult))
            prep(V.tensor_scalar(XT[:, 0, P:2 * P], ident[:, :], dst[:, COLS - 1:COLS], None, ALU.mult))
            assert steps[0] == DIAG
            dve.wait_ge(s_prep, 10)
            prep(V.scalar_tensor_tensor(out=carry_mask[:, :], in0=bank[:, 6, 0:P], scalar=dst[:, COLS - 1:COLS],
                                        in1=upper[:, :], op0=ALU.is_equal, op1=ALU.mult))
            prep(V.scalar_tensor_tensor(out=carry_maskT[:, :], in0=bank[:, 6, P:2 * P], scalar=dst[:, 0:1],
                                        in1=lower[:, :], op0=ALU.is_equal, op1=ALU.mult))
            prep(V.tensor_scalar(deg, dst[:, :], dst[:, 0:1], None, ALU.is_equal))
            prep(V.tensor_reduce(t3[:, 1:2], deg, AX.X, ALU.add))
            prep(V.tensor_scalar(first_end[:, :], t3[:, 1:2], firstrow[:, 0:1], None, ALU.add))
            prep(V.tensor_copy(WE[:, 0:D], mat("gat_w")))
            prep(V.tensor_copy(WE[:, D:2 * D], mat("wv")))
            prep(V.tensor_copy(WE[:, 2 * D:3 * D], mat("wk")))
            prep(V.tensor_copy(WE[:, 3 * D:PROJ], bank[:, 1, 0:HEADS]))
            scale = HC ** -0.5
            prep(V.tensor_scalar(WQA[:, 0:D], mat("wq"), scale, None, ALU.mult))
            prep(V.tensor_copy(WQA[:, D:D + HEADS], bank[:, 1, 16:16 + HEADS]))
            prep(V.tensor_scalar(WQA[:, D + HEADS:QA], bank[:, 1, 48:48 + HEADS], scale, None, ALU.mult))
            prep(V.tensor_scalar(BQA[:, 0:D], vec("bq"), scale, None, ALU.mult))
            prep(V.memset(BQA[:, D:D + HEADS], 0.0))
            prep(V.tensor_scalar(BQA[:, D + HEADS:QA], bank[:, 1, 64:64 + HEADS], scale, None, ALU.mult))
            prep(V.tensor_copy(WSELF[:, 0:D], mat("sage_wr")))
            prep(V.tensor_copy(WSELF[:, D:D + HEADS], bank[:, 1, 32:32 + HEADS]))
            prep(V.tensor_copy(WS3[:, :], bank[:, 2, 0:D]))
            prep(V.tensor_tensor(c0[:, :], bank[:, 3, 0:D], vec("fus_b"), ALU.add))
            prep(V.tensor_tensor(bsum[:, 0, :], vec("bn1"), vec("bs1"), ALU.add))
            prep(V.tensor_tensor(bsum[:, 1, :], vec("bn2"), vec("bs2"), ALU.add))
            assert steps[0] == SETUP_END
            dve.wait_ge(s_pool, 9)

            carries = 0
            carry_products = 0
            local = [0]

            def did(ins):
                local[0] += 1
                ins.then_inc(s_dve, 1)
                dve.wait_ge(s_dve, local[0])

            for f in range(len(PHASES)):
                k, what = PHASES[f]
                index = src_i if k in ("edge", "attend") else last_i

                def stage_indices(i, b):
                    dve.wait_ge(gathered[b], slot_done(GATHERS, f, i, b))
                    copy_indices(i + 1, b)

                def copy_indices(i, b):
                    w = bass.ds(STEP * i + QUAD * b, QUAD)
                    t = slice(QUAD * b, QUAD * (b + 1))
                    V.tensor_scalar(stage[:, t], index[:, w], 0, None, ALU.add).then_inc(S["idx"], 1)
                    if k == "attend":
                        V.tensor_scalar(stage2[:, t], dst_i[:, w], 0, None, ALU.add).then_inc(S["idx2"], 1)

                if k != "in":
                    dve.wait_ge(S["idx"], before("idx", f))
                    for b in range(BODY):
                        copy_indices(0, b)

                def product_bank(b):
                    return bank[:, 4 + b % 2, :].rearrange("p (c f) -> p c f", c=QUAD)

                def stats(i, b, source, mvt, bstt, n=""):
                    p = b % 2
                    user = "normed" if k == "fuse" and not n else "h_ready"
                    dve.wait_ge(S[user], freed(user, f, i, b, 2))
                    for c in range(QUAD):
                        V.bn_stats(bstt[:, p, c, :], source[:, c, :]).then_inc(S["norm_steps" + n], 1)
                    dve.wait_ge(S["norm_steps" + n], reach("norm_steps" + n, f, i, b, QUAD))
                    dve.sem_inc(s_dvew, 1)
                    for c in range(QUAD):
                        ins = V.bn_aggr(mvt[:, p, c, :], bstt[:, p, c, :])
                    ins.then_inc(S["stats" + n], 1)

                def shift(i, b, mvt=mv, rst=rs, nmt=nm, n=""):
                    p = b % 2
                    dve.wait_ge(S["rstd" + n], reach("rstd" + n, f, i, b))
                    V.scalar_tensor_tensor(out=nmt[:, p, :], in0=mvt[:, p, :, 1 - 1], scalar=-1.0, in1=rst[:, p, 1, :],
                                           op0=ALU.mult, op1=ALU.mult).then_inc(S["shift" + n], 1)

                def sums_of(i, b):
                    stage_indices(i, b)
                    for c in range(QUAD):
                        t = QUAD * b + c
                        dve.wait_ge(S["summed"], reach("summed", f, i, b, c))
                        V.scalar_tensor_tensor(out=G[:, t, :], in0=G[:, prior_tiles(b, c), :],
                                               scalar=same[:, bass.ds(STEP * i + t, 1)], in1=G[:, t, :],
                                               op0=ALU.mult, op1=ALU.add).then_inc(S["summed"], 1)

                def in_stats(i, b):
                    dve.wait_ge(res_loaded[b], slot_done(RES_LOADS, f, i, b))
                    stats(i, b, quad(L2, b), mv, bst)

                def aggregate(i, b):
                    stage_indices(i, b)
                    g = quad(G, b)
                    if k in ("gcn", "gcn_out"):
                        dve.wait_ge(loaded[b], slot_done(LOADS, f, i, b))
                        V.tensor_tensor(g, g, quad(L1, b), ALU.add).then_inc(S["agg_steps"], 1)
                        dve.wait_ge(S["agg_steps"], reach("agg_steps", f, i, b, 1))
                        if k == "gcn":
                            V.tensor_tensor(g, g, per_col(dinv, i, b), ALU.mult).then_inc(S["agg_ready"], 1)
                            return
                        slot_stored(dve, "residual", f, i, b)
                        dve.wait_ge(S["h_ready"], freed("h_ready", f, i, b, BODY))
                        dve.wait_ge(res_loaded[b], slot_done(RES_LOADS, f, i, b))
                        for c in range(QUAD):
                            t = QUAD * b + c
                            ins = V.scalar_tensor_tensor(out=O2[:, t, :], in0=G[:, t, :],
                                                         scalar=dinv[:, bass.ds(STEP * i + t, 1)], in1=L2[:, t, :],
                                                         op0=ALU.mult, op1=ALU.add)
                        ins.then_inc(S["x_ready"], 1)
                        dve.wait_ge(S["x_ready"], reach("x_ready", f, i, b))
                        stats(i, b, quad(O2, b), mv, bst)
                    elif k in ("sage1", "sage2"):
                        V.tensor_tensor(g, g, per_col(invdeg, i, b), ALU.mult).then_inc(S["agg_ready"], 1)

                def post(i, b):
                    o = quad(O1, b)
                    bias = {"in": lambda: vec("b0"), "gcn": lambda: vec(f"b{what}"), "sage1": lambda: bsum[:, 0, :],
                            "sage2": lambda: bsum[:, 1, :]}[k]()
                    dve.wait_ge(S["product"], reach("product", f, i, b))
                    slot_stored(dve, "table", f, i, b)
                    V.tensor_tensor(o, product_bank(b), over_quad(bias), ALU.add).then_inc(S["biased"], 1)
                    dve.wait_ge(S["biased"], reach("biased", f, i, b))
                    if k in ("in", "gcn"):
                        ins = V.scalar_tensor_tensor(out=o, in0=o, scalar=0.0, in1=per_col(dinv, i, b),
                                                     op0=ALU.max, op1=ALU.mult)
                    elif k == "sage1":
                        ins = V.tensor_scalar(o, o, 0.0, None, ALU.max)
                    else:
                        dve.wait_ge(res_loaded[b], slot_done(RES_LOADS, f, i, b))
                        ins = V.tensor_tensor(o, o, quad(L2, b), ALU.add)
                    ins.then_inc(S["out_ready"], 1)

                def conv_x(i, b):
                    dve.wait_ge(S["product"], reach("product", f, i, b))
                    dve.wait_ge(res_loaded[b], slot_done(RES_LOADS, f, i, b))
                    slot_stored(dve, "residual", f, i, b)
                    dve.wait_ge(S["h_ready"], freed("h_ready", f, i, b, BODY))
                    V.tensor_tensor(quad(O2, b), product_bank(b), quad(L2, b), ALU.add).then_inc(S["x_ready"], 1)
                    dve.wait_ge(S["x_ready"], reach("x_ready", f, i, b))
                    stats(i, b, quad(O2, b), mv, bst)
                    V.tensor_tensor(quad(ST, b)[:, :, 0:D], quad(O2, b), over_quad(vec("ln_b")), ALU.add)\
                     .then_inc(S["based"], 1)

                def conv_qa(i, b):
                    dve.wait_ge(S["qa_product"], reach("qa_product", f, i, b))
                    slot_stored(dve, "qa", f, i, b)
                    V.tensor_tensor(quad(QG, b), wide67[:, :, 0:QA], over_quad(BQA[:, :]), ALU.add)\
                     .then_inc(S["qa_ready"], 1)

                def heads(t):
                    return t.rearrange("p c (h e) -> p c h e", e=HC)

                def attend_pair(h):
                    o, back_lag = 1 - h, 1 - h
                    fs, bs = f"front_steps{h}", f"back_steps{o}"

                    def go(i, b, front=True, back=True):
                        t0 = QUAD * b + 2 * h
                        pair = slice(t0, t0 + 2)
                        pj = key_bank(h)
                        bi, bb = (i, b) if h else ((i, b - 1) if b else (i - 1, BODY - 1))
                        u0 = QUAD * bb + 2 * o
                        pjo = value_bank(bb, o)

                        def after(n):
                            dve.wait_ge(S[fs], reach(fs, f, i, b, n))

                        def after_back(n):
                            dve.wait_ge(S[bs], reach(bs, f, bi, bb, n))

                        def back_state(c, part):
                            t, before_t = u0 + c, (u0 + c - 1) % STEP
                            r = exps[:, o, c, 0:2 * HEADS]
                            if part == "R":
                                if c:
                                    after_back(4)
                                V.tensor_tensor(ST[:, t, 0:2 * D].rearrange("p (h e) -> p h e", e=HC),
                                                ST[:, before_t, 0:2 * D].rearrange("p (h e) -> p h e", e=HC),
                                                r.unsqueeze(2).to_broadcast([P, 2 * HEADS, HC]), ALU.mult)\
                                 .then_inc(S[bs], 1)
                            elif part == "S":
                                if c:
                                    after_back(5)
                                V.tensor_tensor(ST[:, t, S_:SW], ST[:, before_t, S_:SW], r, ALU.mult)\
                                 .then_inc(S[bs], 1)
                            elif part == "X":
                                V.scalar_tensor_tensor(out=ST[:, t, X_:M_], in0=ST[:, before_t, X_:M_],
                                                       scalar=same[:, bass.ds(STEP * bi + t, 1)], in1=G[:, t, :],
                                                       op0=ALU.mult, op1=ALU.add).then_inc(S[bs], 1)
                            elif part == "R+":
                                dve.wait_ge(S[f"proj_used{o}"], reach(f"proj_used{o}", f, bi, bb))
                                after_back(5 * c + 1)
                                V.tensor_tensor(ST[:, t, 0:2 * D], ST[:, t, 0:2 * D], tmp[:, c, :], ALU.add)\
                                 .then_inc(S[bs], 1)
                            else:
                                after_back(5 * c + 2)
                                V.tensor_tensor(ST[:, t, S_:SW], ST[:, t, S_:SW], exps[:, o, c, 2 * HEADS:], ALU.add)\
                                 .then_inc(S["state_ready" if (o, c) == (1, 1) else bs], 1)

                        if front:
                            dve.wait_ge(S[f"proj{h}"], reach(f"proj{h}", f, i, b))
                            V.tensor_tensor(prod[:, h], pj[:, :, 0:D], QG[:, pair, 0:D], ALU.mult)\
                             .then_inc(S[fs], 1)
                            V.tensor_tensor(asum[:, h], pj[:, :, D:D + HEADS], QG[:, pair, D:D + HEADS], ALU.add)\
                             .then_inc(S[fs], 1)
                        if back:
                            if o == 1:
                                dve.wait_ge(S["back_steps0"], reach("back_steps0", f, bi, bb, 10))
                            else:
                                dve.wait_ge(S["state_ready"], reach("state_ready", f, bi, bb, 0))
                            dve.wait_ge(S[f"exps{o}"], reach(f"exps{o}", f, bi, bb))
                            V.tensor_tensor(heads(tmp[:, :, :]), heads(pjo),
                                            exps[:, o, :, 2 * HEADS:].unsqueeze(3).to_broadcast([P, 2, 2 * HEADS, HC]),
                                            ALU.mult).then_inc(S[f"proj_used{o}"], 1)
                        if front:
                            after(1)
                            V.tensor_reduce(red[:, h], heads(prod[:, h]), AX.X, ALU.add).then_inc(S[fs], 1)
                            after(2)
                            V.scalar_tensor_tensor(out=lg[:, h, :, 0:HEADS], in0=asum[:, h], scalar=0.2,
                                                   in1=asum[:, h], op0=ALU.mult, op1=ALU.max).then_inc(S[fs], 1)
                        if back:
                            back_state(0, "R")
                        if front:
                            after(3)
                            V.tensor_tensor(lg[:, h, :, HEADS:], red[:, h], QG[:, pair, D + HEADS:QA], ALU.add)\
                             .then_inc(S[fs], 1)
                        if back:
                            back_state(0, "S")
                            back_state(0, "X")
                        for c in range(2):
                            if front:
                                if c == 0:
                                    after(5)
                                    if h == 0:
                                        slot_stored(dve, "table", f, i, b)
                                    other = f"front_steps{o}"
                                    dve.wait_ge(S[other], reach(other, f, i, b, 7 if h else 0))
                                else:
                                    after(6)
                                V.scalar_tensor_tensor(
                                    out=ST[:, t0 + c, M_:S_], in0=ST[:, (t0 + c - 1) % STEP, M_:S_],
                                    scalar=gapneg[:, bass.ds(STEP * i + t0 + c, 1)], in1=lg[:, h, c, :],
                                    op0=ALU.add, op1=ALU.max).then_inc(S[fs], 1)
                            if back:
                                back_state(0, ("R+", "S+")[c])
                                if c:
                                    back_state(1, "R")
                        if front:
                            after(7)
                            dve.wait_ge(S[f"exps{h}"], freed(f"exps{h}", f, i, b, 1))
                            V.tensor_tensor(gaps[:, h, :, 2 * HEADS:], lg[:, h], ST[:, pair, M_:S_], ALU.subtract)
                            for c in range(2):
                                ins = V.scalar_tensor_tensor(
                                    out=gaps[:, h, c, 0:2 * HEADS], in0=ST[:, (t0 + c - 1) % STEP, M_:S_],
                                    scalar=gapneg[:, bass.ds(STEP * i + t0 + c, 1)], in1=ST[:, t0 + c, M_:S_],
                                    op0=ALU.add, op1=ALU.subtract)
                            ins.then_inc(S[f"gaps{h}"], 1)
                        if back:
                            for part in ("S", "X", "R+", "S+"):
                                back_state(1, part)
                    return go

                attend_first, attend_second = attend_pair(0), attend_pair(1)

                def attend_pairs(i, b):
                    attend_first(i, b, back=not (isinstance(i, int) and (i, b) == (0, 0)))
                    attend_second(i, b)

                H = bank[:, 2, :].rearrange("p (c f) -> p c f", c=QUAD)
                SL = wide34[:, :, D:D + HEADS]

                def self_logits(i, b):
                    s = quad(ST, b)

                    def after(n):
                        dve.wait_ge(S["self_steps"], reach("self_steps", f, i, b, n))

                    dve.wait_ge(S["product"], reach("product", f, i, b))
                    V.tensor_scalar(slog[:, :, :], SL, 0.2, None, ALU.mult)\
                     .then_inc(S["self_steps"], 1)
                    after(1)
                    V.tensor_tensor(slog[:, :, :], slog[:, :, :], SL, ALU.max)\
                     .then_inc(S["self_steps"], 1)
                    after(2)
                    V.tensor_tensor(sm[:, :, :], slog[:, :, :], s[:, :, M_:M_ + HEADS], ALU.max)\
                     .then_inc(S["self_steps"], 1)
                    after(3)
                    dve.wait_ge(S["sage_ready"], freed("sage_ready", f, i, b, 2))
                    V.tensor_tensor(sgap[:, b % 2, :, 0:HEADS], s[:, :, M_:M_ + HEADS], sm[:, :, :], ALU.subtract)
                    V.tensor_tensor(sgap[:, b % 2, :, HEADS:], slog[:, :, :], sm[:, :, :], ALU.subtract)\
                     .then_inc(S["self_gaps"], 1)

                def sage_bias(i, b):
                    dve.wait_ge(S["product"], reach("product", f, i, b))
                    dve.wait_ge(S["parts_transposed"], freed("parts_transposed", f, i, b, 2))
                    V.tensor_tensor(sage[:, b % 2, :, :], wide34[:, :, 0:D], over_quad(vec("sage_bl")), ALU.add)\
                     .then_inc(S["sage_biased"], 1)

                def floor(i, b):
                    p = b % 2
                    dve.wait_ge(S["sage_squares"], reach("sage_squares", f, i, b, QUAD))
                    V.tensor_scalar(ss[:, p, 1, :], ss[:, p, 0, :], 1e-24, None, ALU.max).then_inc(S["sage_floor"], 1)

                def blend(i, b):
                    s, e = quad(ST, b), sexp[:, b % 2, :, :]

                    def after(n):
                        dve.wait_ge(S["blend_steps"], reach("blend_steps", f, i, b, n))

                    def step(ins):
                        ins.then_inc(S["blend_steps"], 1)

                    def by_head(t):
                        return t.unsqueeze(3).to_broadcast([P, QUAD, HEADS, HC])

                    dve.wait_ge(S["self_exps"], reach("self_exps", f, i, b))
                    dve.wait_ge(S["own_h"], reach("own_h", f, i, b))
                    step(V.tensor_tensor(zz[:, :, 0:HEADS], s[:, :, S_:S_ + HEADS], e[:, :, 0:HEADS], ALU.mult))
                    step(V.tensor_copy(zz[:, :, HEADS:], s[:, :, S_ + HEADS:SW]))
                    after(1)
                    step(V.tensor_tensor(zz[:, :, 0:HEADS], zz[:, :, 0:HEADS], e[:, :, HEADS:], ALU.add))
                    after(3)
                    step(V.tensor_scalar(zz[:, :, :], zz[:, :, :], 1e-16, None, ALU.max))
                    after(4)
                    step(V.reciprocal(zz[:, :, :], zz[:, :, :]))
                    after(5)
                    e2 = e.rearrange("p c (g h) -> p c g h", g=2)
                    step(V.tensor_tensor(e2, e2, zz[:, :, 0:HEADS].unsqueeze(2).to_broadcast([P, QUAD, 2, HEADS]),
                                         ALU.mult))
                    tr = heads(s[:, :, D:2 * D])
                    V.tensor_tensor(tr, tr, by_head(zz[:, :, HEADS:]), ALU.mult).then_inc(S["tr_ready"], 1)
                    after(6)
                    gat = heads(s[:, :, 0:D])
                    step(V.tensor_tensor(gat, gat, by_head(e[:, :, 0:HEADS]), ALU.mult))
                    V.tensor_tensor(heads(hself[:, :, :]), heads(H), by_head(e[:, :, HEADS:]), ALU.mult)\
                     .then_inc(S["self_used"], 1)
                    dve.wait_ge(S["self_used"], reach("self_used", f, i, b))
                    after(7)
                    V.tensor_tensor(s[:, :, 0:D], s[:, :, 0:D], hself[:, :, :], ALU.add).then_inc(S["gat_ready"], 1)

                def sage_scale(i, b):
                    p = b % 2
                    dve.wait_ge(S["sage_norm"], reach("sage_norm", f, i, b))
                    V.tensor_tensor(sage[:, p, :, :], sage[:, p, :, :],
                                    ss[:, p, 2, :].unsqueeze(2).to_broadcast([P, QUAD, D]), ALU.mult)\
                     .then_inc(S["sage_ready"], 1)

                def fused_stats(i, b):
                    dve.wait_ge(S["fused"], reach("fused", f, i, b))
                    stats(i, b, bank[:, 7, :].rearrange("p (c f) -> p c f", c=QUAD), mv, bst)

                def fused_x(i, b):
                    p = b % 2
                    z = zn[:, p, :, :]
                    dve.wait_ge(S["normed"], reach("normed", f, i, b))
                    V.tensor_tensor(z, z, over_quad(vec("ln_g")), ALU.mult).then_inc(S["x3_steps"], 1)
                    dve.wait_ge(S["x3_steps"], reach("x3_steps", f, i, b, 1))
                    slot_stored(dve, "residual", f, i, b)
                    dve.wait_ge(res_loaded[b], slot_done(RES_LOADS, f, i, b))
                    V.tensor_tensor(quad(O2, b), z, quad(L2, b), ALU.add).then_inc(S["x_ready"], 1)
                    dve.wait_ge(S["x_ready"], reach("x_ready", f, i, b))
                    stats(i, b, quad(O2, b), mv2, bst2, "2")

                def shift2(i, b):
                    shift(i, b, mv2, rs2, nm2, "2")

                if k == "in":
                    run(dve, [(in_stats, 0), (shift, 1), (post, 4)])
                elif k == "edge":
                    run(dve, [(sums_of, 0)])
                    carries += 1
                    carry_products += 1
                    if carries > 1:
                        dve.wait_ge(s_carry_d, 16 * (carries - 1))
                    dve.wait_ge(s_carry_p, carry_products)
                    V.tensor_copy(carry[:, :], bank[:, 0, 0:D]).then_inc(s_carry_v, 1)
                elif k in ("gcn", "sage1", "sage2"):
                    run(dve, [(post, 2), (aggregate, 0)])
                elif k == "gcn_out":
                    run(dve, [(aggregate, 0), (shift, 1)])
                elif k == "conv":
                    run(dve, [(shift, 2), (conv_x, 1), (conv_qa, 4), (stage_indices, 0)])
                elif k == "fuse":
                    run(dve, [(shift, 4), (shift2, 5), (floor, 2), (blend, 2), (fused_x, 4), (sage_scale, 2),
                              (stage_indices, 0), (self_logits, 1), (sage_bias, 1), (fused_stats, 3)])
                elif k == "attend":
                    run(dve, [(attend_pairs, 1), (stage_indices, 0)])
                    attend_first(NQ // BODY, NQ % BODY, front=False)
                    carries += 1
                    HH = 2 * HEADS
                    end = ST[:, END_TILE, :]
                    dve.wait_ge(S["state_ready"], before("state_ready", f + 1))
                    did(V.tensor_tensor(rsv[:, :, 0:HC], end[:, 0:2 * D].rearrange("p (h e) -> p h e", e=HC),
                                        end[:, 0:2 * D].rearrange("p (h e) -> p h e", e=HC), ALU.max))
                    did(V.tensor_copy(rsv[:, :, HC], end[:, S_:SW]))
                    did(V.tensor_scalar(XT[:, 0, 0:P], carry_maskT[:, :], 1.0, -NEG, ALU.subtract, ALU.mult))
                    V.tensor_tensor(cm, ident[:, :].unsqueeze(1).to_broadcast([P, HH, P]),
                                    end[:, M_:S_].unsqueeze(2).to_broadcast([P, HH, P]), ALU.mult).then_inc(s_acarry, 1)
                    spread = bank[:, 0:4, :].rearrange("p a (t q) -> p (a t) q", t=4)
                    dve.wait_ge(s_carry_p, carry_products + 1)
                    did(V.tensor_tensor(cm, spread, XT[:, 0, 0:P].unsqueeze(1).to_broadcast([P, HH, P]), ALU.add))
                    did(V.tensor_reduce(mc[:, 0, :], cm, AX.X, ALU.max))
                    V.tensor_tensor(cm, cm, mc[:, 0, :].unsqueeze(2).to_broadcast([P, HH, P]), ALU.subtract)\
                     .then_inc(s_cgap, 1)
                    dve.wait_ge(s_act, 1)
                    V.tensor_tensor(cm, cm, carry_maskT[:, :].unsqueeze(1).to_broadcast([P, HH, P]), ALU.mult)\
                     .then_inc(s_acarry, 1)
                    dve.wait_ge(s_carry_p, carry_products + 2)
                    V.tensor_copy(cmT, spread).then_inc(s_acarry, 1)
                    dve.wait_ge(s_fixg, 16)
                    m1, ga, gb, sc = mc[:, 1, :], mc[:, 2, :], mc[:, 3, :], mc[:, 4, :]
                    did(V.tensor_tensor(m1, mc[:, 0, :], fixrow[:, M_:S_], ALU.max))
                    did(V.tensor_tensor(ga, mc[:, 0, :], m1, ALU.subtract))
                    V.tensor_tensor(gb, fixrow[:, M_:S_], m1, ALU.subtract).then_inc(s_cgap, 1)
                    dve.wait_ge(s_act, 2)
                    dve.wait_ge(s_carry_p, carry_products + 3)
                    carry_products += 3
                    rc = bank[:, 4, 0:HH * (HC + 1)].rearrange("p (h e) -> p h e", e=HC + 1)
                    fr = fixrow[:, 0:2 * D].rearrange("p (h e) -> p h e", e=HC)
                    ft = fixtmp[:, 0:2 * D].rearrange("p (h e) -> p h e", e=HC)
                    did(V.tensor_tensor(ft, rc[:, :, 0:HC], ga.unsqueeze(2).to_broadcast([P, HH, HC]), ALU.mult))
                    did(V.tensor_tensor(fr, fr, gb.unsqueeze(2).to_broadcast([P, HH, HC]), ALU.mult))
                    did(V.tensor_tensor(fixrow[:, 0:2 * D], fixrow[:, 0:2 * D], fixtmp[:, 0:2 * D], ALU.add))
                    did(V.tensor_tensor(sc, rc[:, :, HC], ga, ALU.mult))
                    did(V.tensor_tensor(fixrow[:, S_:SW], fixrow[:, S_:SW], gb, ALU.mult))
                    did(V.tensor_tensor(fixrow[:, S_:SW], fixrow[:, S_:SW], sc, ALU.add))
                    did(V.tensor_tensor(fixrow[:, X_:M_], fixrow[:, X_:M_], bank[:, 5, 0:D], ALU.add))
                    V.tensor_copy(fixrow[:, M_:S_], m1).then_inc(s_carry_v, 1)


def kernel(**inputs):
    import concourse.bacc as bacc
    from concourse.bass_utils import run_bass_kernel_spmd

    x = {k: np.asarray(v) for k, v in inputs.items()}

    def rows(v):
        return np.broadcast_to(v[None, :], (P, D))

    def column(v):
        return np.broadcast_to(v.reshape(-1)[:, None], (P, D))

    def padded(v, fill):
        return np.concatenate([v, np.full((P * COLS - v.shape[0],), fill, v.dtype)]).reshape(P, COLS)

    g = {k[len("L2_gnn_"):]: v for k, v in x.items() if k.startswith("L2_gnn_")}
    fus = g["fus_w"]
    mats = dict(W0=x["L0_gnn_W0"], W1=x["L0_gnn_W1"], W2=x["L0_gnn_W2"], L1_W=x["L1_gnn_W"],
                L1_Wself=x["L1_gnn_W_self"], gat_w=g["gat_w"], gat_wT=g["gat_w"].T, sage_wl=g["sage_wl"],
                sage_wr=g["sage_wr"], wq=g["tr_wq"], wqT=g["tr_wq"].T, wk=g["tr_wk"], wv=g["tr_wv"],
                wskipT=g["tr_wskip"].T, F1=fus[0:D], F2=fus[D:2 * D], F3=fus[2 * D:3 * D],
                Wn1T=x["L3_gnn_W_neigh1"].T, Ws1T=x["L3_gnn_W_self1"].T, Wn2T=x["L3_gnn_W_neigh2"].T,
                Ws2T=x["L3_gnn_W_self2"].T, gat_b_col=column(g["gat_b"]), bskip_col=column(g["tr_bskip"]),
                bq_col=column(g["tr_bq"]))
    vecs = dict(b0=x["L0_gnn_b0"], b1=x["L0_gnn_b1"], b2=x["L0_gnn_b2"], sage_bl=g["sage_bl"], bq=g["tr_bq"],
                fus_b=g["fus_b"], ln_g=g["ln_g"], ln_b=g["ln_b"], bv=g["tr_bv"], bn1=x["L3_gnn_b_neigh1"],
                bs1=x["L3_gnn_b_self1"], bn2=x["L3_gnn_b_neigh2"], bs2=x["L3_gnn_b_self2"])
    part = np.arange(P)
    arrays = {
        "x": np.concatenate([x["x"], np.zeros((ROWS - N, D), x["x"].dtype)]),
        "src": padded(x["src"], 0), "dst": padded(x["dst"], N),
        "mats": np.stack([mats[n] for n in MATS], axis=1), "vecs": np.stack([rows(vecs[n]) for n in VECS], axis=1),
        "attc": np.stack([g["gat_att_src"].reshape(-1), g["gat_att_dst"].reshape(-1), g["tr_bk"]], axis=1),
        "row0": (part[:, None] + 0 * part[None, :] == 0).astype(np.float32),
        "ident": np.eye(P, dtype=np.float32),
        "upper": np.triu(np.ones((P, P), np.float32), 1), "lower": np.tril(np.ones((P, P), np.float32), -1),
        "hmask": (part[:, None] // HC == np.arange(HEADS)[None, :]).astype(np.float32),
        "iota": np.tile(np.arange(COLS, dtype=np.float16), (P, 1)),
        "emptyrow": (ROWS + part[:, None]).astype(np.float32),
        "firstrow": (part[:, None] * COLS - 1).astype(np.float32),
    }
    nc = bacc.Bacc("TRN2", target_bir_lowering=False, num_devices=1)
    args, feed = {}, {}
    for name, arr in arrays.items():
        arr = np.ascontiguousarray(arr)
        feed["in_" + name] = arr
        args[name] = nc.dram_tensor("in_" + name, arr.shape, mybir.dt.from_np(arr.dtype), kind="ExternalInput").ap()
    out = nc.dram_tensor("out_0", (ROWS, D), mybir.dt.float32, kind="ExternalOutput").ap()
    gnn_kernel(nc, args, out)
    r = run_bass_kernel_spmd(nc, [feed], core_ids=[0])
    return r.results[0]["out_0"][0:N]
```

```python
from contextlib import ExitStack

import numpy as np

import concourse.bass as bass
from concourse import mybir

P = 128
D = 128
N = 50000
E = 50000
HEADS = 8
HC = D // HEADS
QUAD = 4
BODY = 4
COLS = 392
NQ = COLS // QUAD
TURNS = NQ // BODY
STEP = QUAD * BODY
END_TILE = (COLS - 1) % STEP
ROWS = P * COLS
QA = D + 2 * HEADS
SW = 3 * D + 4 * HEADS
R_, X_, M_, S_ = 0, 2 * D, 3 * D, 3 * D + 2 * HEADS
PROJ = 3 * D + HEADS
NEG = -1.0e30
HI_SHARE = 11
EPS = 1e-5

MATS = ["W0", "W1", "W2", "L1_W", "L1_Wself", "gat_w", "gat_wT", "sage_wl", "sage_wr", "wq", "wqT", "wk",
        "wv", "wskipT", "F1", "F2", "F3", "Wn1T", "Ws1T", "Wn2T", "Ws2T", "gat_b_col", "bskip_col",
        "bq_col"]
VECS = ["b0", "b1", "b2", "sage_bl", "bq", "fus_b", "ln_g", "ln_b", "bv", "bn1", "bs1", "bn2", "bs2"]

PHASES = [("in", None), ("edge", "g0"), ("gcn", 1), ("edge", "g1"), ("gcn", 2), ("edge", "g2"), ("gcn_out", None),
          ("edge", "h1"), ("conv", None), ("attend", "h2"), ("fuse", None), ("edge", "h3"), ("sage1", None),
          ("edge", "h4"), ("sage2", None)]

COUNTS = {
    "idx": dict(edge=1, gcn=1, gcn_out=1, conv=1, attend=1, fuse=1, sage1=1, sage2=1),
    "idx2": dict(attend=1),
    "summed": dict(edge=4),
    "agg_steps": dict(gcn=1, gcn_out=1),
    "norm_steps": {"in": 4, "gcn_out": 4, "conv": 4, "fuse": 4}, "norm_steps2": dict(fuse=4),
    "stats2": dict(fuse=1), "rstd2": dict(fuse=1), "shift2": dict(fuse=1), "rstd_steps2": dict(fuse=1),
    "front_steps0": dict(attend=7), "front_steps1": dict(attend=7),
    "back_steps0": dict(attend=10), "back_steps1": dict(attend=9),
    "self_steps": dict(fuse=3), "blend_steps": dict(fuse=7), "x3_steps": dict(fuse=1),
    "rstd_steps": {"in": 1, "gcn_out": 1, "conv": 1, "fuse": 1}, "sage_log": dict(fuse=1),
    "agg_ready": dict(gcn=1, fuse=1, sage1=1, sage2=1),
    "transposed": {"in": 1, "gcn": 1, "conv": 1, "attend": 1, "fuse": 1, "sage1": 1, "sage2": 1},
    "own_transposed": dict(conv=1, fuse=1, sage1=1, sage2=1),
    "xt_ready": {"in": 1, "gcn": 1, "conv": 1, "attend": 1, "fuse": 1, "sage1": 1, "sage2": 1},
    "xu_ready": dict(conv=1, fuse=1, sage1=1, sage2=1),
    "product": {"in": 1, "gcn": 1, "conv": 1, "fuse": 1, "sage1": 1, "sage2": 1},
    "biased": {"in": 1, "gcn": 1, "sage1": 1, "sage2": 1},
    "out_ready": {"in": 1, "gcn": 1, "sage1": 1, "sage2": 1},
    "x_ready": dict(gcn_out=1, conv=1, fuse=1),
    "stats": {"in": 1, "gcn_out": 1, "conv": 1, "fuse": 1},
    "rstd": {"in": 1, "gcn_out": 1, "conv": 1, "fuse": 1},
    "shift": {"in": 1, "gcn_out": 1, "conv": 1, "fuse": 1},
    "h_ready": {"in": 1, "gcn_out": 1, "conv": 1, "fuse": 1},
    "h_transposed": dict(conv=1),
    "ht_ready": dict(conv=1),
    "qa_product": dict(conv=1),
    "qa_ready": dict(conv=1),
    "proj0": dict(attend=1), "proj1": dict(attend=1),
    "gaps0": dict(attend=1), "gaps1": dict(attend=1),
    "exps0": dict(attend=1), "exps1": dict(attend=1),
    "proj_used0": dict(attend=1), "proj_used1": dict(attend=1),
    "state_ready": dict(attend=1),
    "based": dict(conv=1), "own_h": dict(fuse=1),
    "self_used": dict(fuse=1),
    "self_gaps": dict(fuse=1), "self_exps": dict(fuse=1),
    "sage_biased": dict(fuse=1), "sage_squares": dict(fuse=4), "sage_floor": dict(fuse=1), "sage_norm": dict(fuse=1),
    "gat_ready": dict(fuse=1), "tr_ready": dict(fuse=1), "sage_ready": dict(fuse=1),
    "parts_transposed": dict(fuse=3), "parts_ready": dict(fuse=3),
    "fused": dict(fuse=1), "normed": dict(fuse=1),
}
GATHERS = dict(edge=64, gcn=64, gcn_out=64, conv=64, attend=128, fuse=64, sage1=64, sage2=64)
LOADS = dict(gcn=16, gcn_out=16, conv=16, fuse=16, sage1=16, sage2=16)
RES_LOADS = {"in": 16, "gcn_out": 16, "conv": 16, "fuse": 16, "sage2": 16}
STORES = dict(
    table={"in": 16, "edge": 16, "gcn": 16, "gcn_out": 16, "conv": 16, "attend": 16, "fuse": 16, "sage1": 16,
           "sage2": 16},
    residual=dict(gcn_out=16, conv=16, fuse=16),
    qa=dict(conv=16))
CREDIT = 10 * BODY


def before(name, f):
    c = COUNTS[name]
    extra = BODY if name in ("idx", "idx2") else 0
    return CREDIT + sum(c[k] * NQ + extra for k, _ in PHASES[:f] if k in c)


def before_slot(table, f, b):
    quads = len(range(b, NQ, BODY))
    return (16 if table in STORES.values() else 0) + quads * sum(table.get(k, 0) for k, _ in PHASES[:f])


def gnn_kernel(nc, a, out):
    f32, f16, bf16, i32 = mybir.dt.float32, mybir.dt.float16, mybir.dt.bfloat16, mybir.dt.int32
    ALU, ACT, AX = mybir.AluOpType, mybir.ActivationFunctionType, mybir.AxisListType
    ctx = ExitStack()

    def sb(name, shape, dt=f32):
        return ctx.enter_context(nc.sbuf_tensor(name, shape, dt))

    def sem(name):
        return ctx.enter_context(nc.semaphore(name))

    def dram(name, rows, width):
        return nc.dram_tensor(name, (rows, width), f32).ap()

    with ctx:
        tab = {n: dram("tab_" + n, ROWS, D) for n in ("g0", "g1", "g2", "h1", "h2", "h3", "h4")}
        tab_qa = dram("tab_qa", ROWS, QA)
        res = {n: dram("res_" + n, ROWS, D) for n in ("x1", "x2", "x3")}
        sums = dram("sums", ROWS + P, D)
        states = dram("states", ROWS + P, SW)

        def cols(t):
            return t[0:ROWS, :].rearrange("(p c) f -> p c f", c=COLS)

        mats = sb("mats", [P, len(MATS), D])
        vecs = sb("vecs", [P, len(VECS), D])
        ident = sb("ident", [P, P])
        upper = sb("upper", [P, P])
        lower = sb("lower", [P, P])
        hmask = sb("hmask", [P, HEADS])
        attc = sb("attc", [P, 3])
        ones = sb("ones", [P, P])
        zero16 = sb("zero16", [P, P], f16)
        iota = sb("iota", [P, COLS], f16)
        emptyrow = sb("emptyrow", [P, 1])
        firstrow = sb("firstrow", [P, 1])
        eps = sb("eps", [P, 1])
        src_i = sb("src_i", [P, COLS + STEP], i32)
        dst_i = sb("dst_i", [P, COLS + STEP], i32)
        last_i = sb("last_i", [P, COLS + STEP], i32)
        dst = sb("dst", [P, COLS])
        same = sb("same", [P, COLS])
        gapneg = sb("gapneg", [P, COLS])
        dinv = sb("dinv", [P, COLS])
        invdeg = sb("invdeg", [P, COLS])
        has = sb("has", [P, COLS])
        stage = sb("stage", [P, STEP], i32)
        stage2 = sb("stage2", [P, STEP], i32)
        carry_mask = sb("carry_mask", [P, P])
        carry_maskT = sb("carry_maskT", [P, P])
        first_end = sb("first_end", [P, 1], i32)
        carry = sb("carry", [P, D])

        G = sb("G", [P, STEP, D])
        L1 = sb("L1", [P, STEP, D])
        L2 = sb("L2", [P, STEP, D])
        O1 = sb("O1", [P, STEP, D])
        O2 = sb("O2", [P, STEP, D])
        ST = sb("ST", [P, STEP, SW])
        QG = sb("QG", [P, STEP, QA])
        XT = sb("XT", [P, 2, QUAD * D])
        XU = sb("XU", [P, BODY, QUAD * D])
        XV = sb("XV", [P, 3, QUAD * D])
        bst = sb("bst", [P, 2, QUAD, 6])
        mv = sb("mv", [P, 2, QUAD, 2])
        rs = sb("rs", [P, 2, 2, QUAD])
        nm = sb("nm", [P, 2, QUAD])
        bst2 = sb("bst2", [P, 2, QUAD, 6])
        mv2 = sb("mv2", [P, 2, QUAD, 2])
        rs2 = sb("rs2", [P, 2, 2, QUAD])
        nm2 = sb("nm2", [P, 2, QUAD])
        WE = sb("WE", [P, PROJ])
        WQA = sb("WQA", [P, QA])
        BQA = sb("BQA", [P, QA])
        WSELF = sb("WSELF", [P, D + HEADS])
        WS3 = sb("WS3", [P, D])
        c0 = sb("c0", [P, D])
        c0_rest = sb("c0_rest", [P, D])
        c0_parts = sb("c0_parts", [P, 3, D], bf16)
        c0_rows = sb("c0_rows", [P, D], bf16)
        ones16 = sb("ones16", [P, P], bf16)
        row0 = sb("row0", [P, P])
        bsum = sb("bsum", [P, 2, D])
        blk = sb("blk", [P, 4, HEADS])
        oh_hi = sb("oh_hi", [P, 16, P], f16)
        oh_sq = sb("oh_sq", [P, HI_SHARE, P], f16)
        oh_lo = sb("oh_lo", [P, 16, COLS], f16)
        prod = sb("prod", [P, 2, 2, D])
        red = sb("red", [P, 2, 2, HEADS])
        asum = sb("asum", [P, 2, 2, HEADS])
        lg = sb("lg", [P, 2, 2, 2 * HEADS])
        gaps = sb("gaps", [P, 2, 2, 4 * HEADS])
        exps = sb("exps", [P, 2, 2, 4 * HEADS])
        tmp = sb("tmp", [P, 2, 2 * D])
        sage = sb("sage", [P, 2, QUAD, D])
        hself = sb("hself", [P, QUAD, D])
        zn = sb("zn", [P, 2, QUAD, D])
        sq = sb("sq", [P, D])
        ss = sb("ss", [P, 2, 3, QUAD])
        sgap = sb("sgap", [P, 2, QUAD, 2 * HEADS])
        sexp = sb("sexp", [P, 2, QUAD, 2 * HEADS])
        slog = sb("slog", [P, QUAD, HEADS])
        sm = sb("sm", [P, QUAD, HEADS])
        zz = sb("zz", [P, QUAD, 2 * HEADS])
        lnb = sb("lnb", [P, 1])

        t_f = [L1[:, :, :].rearrange("p c f -> p (c f)")[:, k * COLS:(k + 1) * COLS] for k in range(5)]
        t_i = QG[:, :, :].rearrange("p c f -> p (c f)")[:, 0:COLS].bitcast(i32)
        cm = L1[:, :, :].rearrange("p c f -> p (c f)")[:, 0:2 * HEADS * P].rearrange("p (h q) -> p h q", h=2 * HEADS)
        cmT = L2[:, :, :].rearrange("p c f -> p (c f)")[:, 0:2 * HEADS * P].rearrange("p (h q) -> p h q", h=2 * HEADS)
        rsv = O1[:, :, :].rearrange("p c f -> p (c f)")[:, 0:2 * HEADS * (HC + 1)].rearrange(
            "p (h e) -> p h e", h=2 * HEADS)
        fixrow = O2[:, :, :].rearrange("p c f -> p (c f)")[:, 0:SW]
        fixtmp = O2[:, :, :].rearrange("p c f -> p (c f)")[:, 512:512 + SW]
        mc = O2[:, :, :].rearrange("p c f -> p (c f)")[:, 1024:1024 + 6 * 16].rearrange("p (k h) -> p k h", k=6)

        bank = ctx.enter_context(nc.psum_tensor("bank", [P, 8, 512], f32))

        wide34 = bank[:, 3:5, :].rearrange("p a (t c) -> p (a t) c", t=2)
        wide67 = bank[:, 6:8, :].rearrange("p a (t c) -> p (a t) c", t=2)

        def key_bank(h):
            return bank[:, 2 + h, 0:512].rearrange("p (c f) -> p c f", c=2)[:, :, 0:D + HEADS]

        def value_bank(b, h):
            return bank[:, 4 + 2 * (b % 2) + h, :].rearrange("p (c f) -> p c f", c=2)

        S = {n: sem(n) for n in COUNTS}
        gathered = [sem(f"gathered{b}") for b in range(BODY)]
        loaded = [sem(f"own_loaded{b}") for b in range(BODY)]
        res_loaded = [sem(f"residual_loaded{b}") for b in range(BODY)]
        stored = {n: [sem(f"{n}_stored{b}") for b in range(BODY)] for n in STORES}
        s_const = sem("constants")
        s_pool = sem("pool_setup")
        s_poolw = sem("pool_waited")
        s_dvew = sem("vector_waited")
        s_spw = sem("sync_waited")
        s_actw = sem("scalar_waited")
        s_dinv = sem("degree_scales")
        s_zero = sem("zero_rows")
        s_onehot = sem("onehot")
        s_onehot_hi = sem("onehot_hi")
        s_square = sem("onehot_squares")
        s_hist = sem("histogram")
        s_prep = sem("setup_product")
        s_prepd = sem("setup_vector")
        s_dve = sem("vector_step")
        s_act = sem("scalar_step")
        s_carry_p = sem("carry_product")
        s_carry_v = sem("carry_vector")
        s_carry_d = sem("carry_stored")
        s_fixg = sem("fix_gathered")
        s_acarry = sem("carry_weights")
        s_cgap = sem("carry_gaps")
        BLK, HI_LO, DEG, TOTALS, DIAG, SETUP_END = 4, 19, 21, 26, 33, 65

        def mat(name):
            return mats[:, MATS.index(name), :]

        def vec(name):
            return vecs[:, VECS.index(name), :]

        def over_quad(row):
            return row.unsqueeze(1).to_broadcast([P, QUAD, row.shape[-1]])

        def quad(t, b):
            return t[:, QUAD * b:QUAD * (b + 1), :]

        def per_col(t, i, b):
            return t[:, bass.ds(STEP * i + QUAD * b, QUAD)].unsqueeze(2).to_broadcast([P, QUAD, D])

        def reach(name, f, i, b, part=1):
            c = COUNTS[name][PHASES[f][0]]
            return before(name, f) + (i * BODY + b) * c + part

        def freed(name, f, i, b, ring):
            c = COUNTS[name][PHASES[f][0]]
            return before(name, f) + (i * BODY + b - ring + 1) * c

        def slot_done(table, f, i, b):
            return before_slot(table, f, b) + table[PHASES[f][0]] * (i + 1)

        def all_stored(eng, f):
            for name in STORES:
                for b in range(BODY):
                    eng.wait_ge(stored[name][b], before_slot(STORES[name], f, b))

        def slot_stored(eng, name, f, i, b):
            eng.wait_ge(stored[name][b], slot_done(STORES[name], f, i - 1, b))

        def run(eng, stages):
            deepest = max(lag for _, lag in stages)
            peeled = max(1, -(-deepest // BODY))
            for s in range(peeled * BODY):
                for fn, lag in stages:
                    if s >= lag:
                        fn((s - lag) // BODY, (s - lag) % BODY)
            with eng.Fori(peeled, TURNS) as i:
                for s in range(BODY):
                    for fn, lag in stages:
                        fn(i + (s - lag) // BODY, (s - lag) % BODY)
            for s in range(deepest + NQ % BODY):
                for fn, lag in stages:
                    if s < lag + NQ % BODY:
                        fn(TURNS + (s - lag) // BODY, (s - lag) % BODY)

        consts = [(mats, "mats"), (vecs, "vecs"), (ident, "ident"), (upper, "upper"), (lower, "lower"),
                  (hmask, "hmask"), (attc, "attc"), (iota, "iota"), (emptyrow, "emptyrow"), (firstrow, "firstrow"), (row0, "row0")]

        def kind(f):
            return PHASES[f][0]

        def prior_tiles(b, k):
            return (QUAD * b + k - 1) % STEP

        block = ctx.enter_context(nc.Block())

        @block.sync
        def _(sp):
            for s in S.values():
                sp.sem_inc(s, CREDIT)
            for t, name in consts:
                sp.dma_start(t[:], a[name]).then_inc(s_const, 16)
            sp.dma_start(src_i[:, 0:COLS], a["src"]).then_inc(s_const, 16)
            sp.dma_start(dst_i[:, 0:COLS], a["dst"]).then_inc(s_const, 16)
            sp.wait_ge(s_zero, 1)
            slots = [x for name in STORES for x in stored[name]]
            part = P // (len(slots) // 2)
            for n, x in enumerate(slots):
                t, d = ((G, sums), (ST, states))[n % 2]
                of = slice(n // 2 * part, (n // 2 + 1) * part if n // 2 < len(slots) // 2 - 1 else P)
                sp.dma_start(d[ROWS + of.start:ROWS + of.stop, :], t[of, 0, :]).then_inc(x, 16)

            for f in range(len(PHASES)):
                k, what = PHASES[f]
                all_stored(sp, f)
                if k == "fuse":
                    sp.wait_ge(s_carry_d, 16 * sum(kk in ("edge", "attend") for kk, _ in PHASES[:f]))
                own = {"gcn": tab.get(f"g{(what or 0) - 1}" if k == "gcn" else ""), "gcn_out": tab["g2"],
                       "conv": tab["h1"], "fuse": tab["h2"], "sage1": tab["h3"], "sage2": tab["h4"]}.get(k)
                residual = {"in": a["x"], "gcn_out": a["x"], "conv": res["x1"], "fuse": res["x2"],
                            "sage2": res["x3"]}.get(k)
                own_reader = {"gcn": "agg_ready", "gcn_out": "x_ready"}.get(k, "own_transposed")
                residual_reader = {"in": "h_ready", "sage2": "out_ready"}.get(k, "x_ready")
                stores = {"in": [("table", O1, tab["g0"], "out_ready", 4)],
                          "edge": [("table", G, sums, "summed", 0)],
                          "gcn": [("table", O1, tab.get(f"g{what}"), "out_ready", 2)],
                          "gcn_out": [("table", O1, tab["h1"], "h_ready", 1), ("residual", O2, res["x1"], "x_ready", 0)],
                          "conv": [("qa", QG, tab_qa, "qa_ready", 4), ("table", O1, tab["h2"], "h_ready", 2),
                                   ("residual", ST[:, :, 0:D], res["x2"], "based", 1)],
                          "attend": [("table", ST, states, "state_ready", 1)],
                          "fuse": [("table", O1, tab["h3"], "h_ready", 6), ("residual", O2, res["x3"], "x_ready", 4)],
                          "sage1": [("table", O1, tab["h4"], "out_ready", 2)],
                          "sage2": [("table", O1, out, "out_ready", 2)]}[k]

                def load(t, d, reader, sems, i, b):
                    sp.wait_ge(S[reader], freed(reader, f, i, b, BODY))
                    sp.sem_inc(s_spw, 1)
                    sp.dma_start(quad(t, b), cols(d)[:, bass.ds(STEP * i + QUAD * b, QUAD), :])\
                      .then_inc(sems[b], 16)

                def load_own(i, b):
                    load(L1, own, own_reader, loaded, i, b)

                def load_residual(i, b):
                    load(L2, residual, residual_reader, res_loaded, i, b)

                def store_of(name, t, d, maker):
                    def go(i, b):
                        sp.wait_ge(S[maker], reach(maker, f, i, b, COUNTS[maker][k]))
                        sp.sem_inc(s_spw, 1)
                        sp.dma_start(cols(d)[:, bass.ds(STEP * i + QUAD * b, QUAD), :], quad(t, b))\
                          .then_inc(stored[name][b], 16)
                    return go

                run(sp, [(load_own, 0)] * (own is not None)
                    + [(load_residual, 2 if k == "fuse" else 0)] * (residual is not None)
                    + [(store_of(*spec), lag + 2) for *spec, lag in stores])
            all_stored(sp, len(PHASES))

        @block.gpsimd
        def _(pool):
            for t, val in ((ones, 1.0), (eps, EPS), (zero16, 0.0), (lnb, 10.0 * float(np.log(2.0)))):
                pool.memset(t[:], val).then_inc(s_pool, 1)
            pool.memset(src_i[:, COLS:], 0).then_inc(s_pool, 1)
            pool.memset(dst_i[:, COLS:], 0).then_inc(s_pool, 1)
            pool.memset(last_i[:, COLS:], 0).then_inc(s_pool, 1)
            pool.wait_ge(s_prepd, DEG)
            pool.wait_ge(s_pool, 7)
            pool.wait_ge(s_onehot_hi, -(-COLS // 16))
            pool.memset(t_f[4], -0.5).then_inc(s_pool, 1)
            pool.wait_ge(s_pool, 8)
            with pool.Fori(0, TURNS) as i:
                w = bass.ds(STEP * i, STEP)
                pool.tensor_tensor(dinv[:, w], t_f[1][:, w], t_f[4][:, w], ALU.pow).then_inc(s_dinv, 1)
            w = slice(STEP * TURNS, COLS)
            pool.tensor_tensor(dinv[:, w], t_f[1][:, w], t_f[4][:, w], ALU.pow).then_inc(s_dinv, 1)

            def gather(dest, table, index):
                return pool.indirect_dma_start(
                    out=dest, out_offset=None, in_=table, in_offset=bass.IndirectOffsetOnAxis(ap=index, axis=0))

            carries = 0
            for f in range(len(PHASES)):
                k, what = PHASES[f]
                if k == "in":
                    continue
                all_stored(pool, f)
                if k not in ("edge", "attend"):
                    pool.wait_ge(s_carry_d, 16 * carries)
                readers = {"edge": ["summed"], "gcn": ["transposed"], "gcn_out": ["x_ready"],
                           "conv": ["transposed"], "attend": ["state_ready"], "fuse": ["parts_transposed"],
                           "sage1": ["transposed"], "sage2": ["transposed"]}[k]

                def step(i, b):
                    pool.wait_ge(S["idx"], reach("idx", f, i, b))
                    if k == "attend":
                        pool.wait_ge(S["idx2"], reach("idx2", f, i, b))
                    for r in readers:
                        ring = BODY - 1 if k == "edge" else BODY
                        pool.wait_ge(S[r], freed(r, f, i, b, ring))
                    if k == "edge":
                        slot_stored(pool, "table", f, i, b)
                    pool.sem_inc(s_poolw, 1)
                    for c in range(QUAD):
                        t = QUAD * b + c
                        if k in ("edge", "attend"):
                            gather(G[:, t, :], tab[what], stage[:, t:t + 1]).then_inc(gathered[b], 16)
                        elif k == "fuse":
                            gather(ST[:, t, :], states, stage[:, t:t + 1]).then_inc(gathered[b], 16)
                        else:
                            gather(G[:, t, :], sums, stage[:, t:t + 1]).then_inc(gathered[b], 16)
                        if k == "attend":
                            gather(QG[:, t, :], tab_qa, stage2[:, t:t + 1]).then_inc(gathered[b], 16)

                run(pool, [(step, 0)])
                if k == "edge":
                    carries += 1
                    all_stored(pool, f + 1)
                    pool.wait_ge(s_carry_v, carries)
                    pool.indirect_dma_start(
                        out=sums, out_offset=bass.IndirectOffsetOnAxis(ap=first_end[:, 0:1], axis=0),
                        in_=carry[:, :], in_offset=None, compute_op=ALU.add).then_inc(s_carry_d, 16)
                if k == "attend":
                    carries += 1
                    all_stored(pool, f + 1)
                    gather(fixrow, states, first_end[:, 0:1]).then_inc(s_fixg, 16)
                    pool.wait_ge(s_carry_v, carries)
                    pool.indirect_dma_start(
                        out=states, out_offset=bass.IndirectOffsetOnAxis(ap=first_end[:, 0:1], axis=0),
                        in_=fixrow, in_offset=None).then_inc(s_carry_d, 16)

        @block.tensor
        def _(pe):
            prep = [0]

            def product(out_, lhsT, rhs, start=True, stop=True):
                return nc.tensor.matmul(out_, lhsT, rhs, start=start, stop=stop)

            pe.wait_ge(s_const, 16 * (len(consts) + 2))
            pe.wait_ge(s_pool, 4)
            product(bank[:, 0, 0:COLS], zero16[:, :], iota[:, 0:COLS], True, False).then_inc(s_hist, 1)
            with pe.Fori(0, COLS // 16) as i:
                for c in range(16):
                    if c == 0:
                        pe.wait_ge(s_onehot_hi, i + 1)
                    pe.wait_ge(s_onehot, i * 16 + c + 1)
                    product(bank[:, 0, 0:COLS], oh_hi[:, c, :], oh_lo[:, c, :], False, False).then_inc(s_hist, 1)
            for c in range(COLS % 16):
                if c == 0:
                    pe.wait_ge(s_onehot_hi, COLS // 16 + 1)
                pe.wait_ge(s_onehot, COLS - COLS % 16 + c + 1)
                product(bank[:, 0, 0:COLS], oh_hi[:, c, :], oh_lo[:, c, :], False, False).then_inc(s_hist, 1)
            product(bank[:, 0, 0:COLS], zero16[:, :], iota[:, 0:COLS], False, True).then_inc(s_hist, 1)

            def prep_product(*args):
                product(*args).then_inc(s_prep, 1)

            pe.wait_ge(s_prepd, BLK)
            prep_product(bank[:, 1, 0:HEADS], mat("gat_wT"), blk[:, 0, :])
            prep_product(bank[:, 1, 16:16 + HEADS], mat("gat_wT"), blk[:, 1, :])
            prep_product(bank[:, 1, 32:32 + HEADS], mat("gat_wT"), blk[:, 2, :])
            prep_product(bank[:, 1, 48:48 + HEADS], mat("wqT"), blk[:, 3, :])
            prep_product(bank[:, 1, 64:64 + HEADS], mat("bq_col"), blk[:, 3, :])
            prep_product(bank[:, 2, 0:D], mat("wskipT"), mat("F3"))
            product(bank[:, 3, 0:D], mat("gat_b_col"), mat("F1"), True, False)
            prep_product(bank[:, 3, 0:D], mat("bskip_col"), mat("F3"), False, True)
            pe.wait_ge(s_prepd, TOTALS)
            prep_product(bank[:, 5, 0:1], upper[:, :], t_f[2][:, COLS - 1:COLS])
            pe.wait_ge(s_prepd, DIAG)
            prep_product(bank[:, 6, 0:P], ones[:, :], XT[:, 0, 0:P])
            prep_product(bank[:, 6, P:2 * P], ones[:, :], XT[:, 0, P:2 * P])
            pe.wait_ge(s_prepd, SETUP_END)

            carries = 0
            for f in range(len(PHASES)):
                k, what = PHASES[f]

                if k == "edge":
                    carries += 1
                    pe.wait_ge(S["summed"], before("summed", f + 1))
                    product(bank[:, 0, 0:D], carry_mask[:, :], G[:, END_TILE, :]).then_inc(s_carry_p, 1)
                    pe.wait_ge(s_carry_v, carries)
                    continue

                def transposes(dest, tile, signal):
                    for c in range(QUAD):
                        ins = nc.tensor.transpose(dest[:, c * D:(c + 1) * D], tile(c), ident[:, :])
                    ins.then_inc(signal, 1)

                def first(i, b):
                    p = b % 2
                    if k == "in":
                        pe.wait_ge(S["h_ready"], reach("h_ready", f, i, b))
                    elif k in COUNTS["agg_ready"]:
                        pe.wait_ge(S["agg_ready"], reach("agg_ready", f, i, b))
                    else:
                        pe.wait_ge(gathered[b], slot_done(GATHERS, f, i, b))
                    pe.wait_ge(S["xt_ready"], freed("xt_ready", f, i, b, 1 if k in ("fuse", "conv") else 2))
                    source = {"in": lambda c: O2[:, QUAD * b + c, :],
                              "fuse": lambda c: ST[:, QUAD * b + c, X_:X_ + D]}.get(k, lambda c: G[:, QUAD * b + c, :])
                    transposes(bank[:, 0 if k in ("fuse", "conv") else p, :], source, S["transposed"])
                    if k in ("conv", "sage1", "sage2", "fuse"):
                        pe.wait_ge(loaded[b], slot_done(LOADS, f, i, b))
                        pe.wait_ge(S["xu_ready"], freed("xu_ready", f, i, b, 1 if k in ("fuse", "conv") else 2))
                        transposes(bank[:, 1 if k in ("fuse", "conv") else 2 + p, :], lambda c: L1[:, QUAD * b + c, :],
                                   S["own_transposed"])

                def second(i, b):
                    p = b % 2
                    pe.wait_ge(S["xt_ready"], reach("xt_ready", f, i, b))
                    two = k in ("conv", "sage1", "sage2")
                    if two:
                        pe.wait_ge(S["xu_ready"], reach("xu_ready", f, i, b))
                    user = "x_ready" if k == "conv" else "biased"
                    pe.wait_ge(S[user], freed(user, f, i, b, 2))
                    w1, w2 = {"in": ("W0", None), "gcn": (f"W{what}", None), "conv": ("L1_W", "L1_Wself"),
                              "sage1": ("Wn1T", "Ws1T"), "sage2": ("Wn2T", "Ws2T")}[k]
                    o = bank[:, 4 + p, :]
                    for c in range(QUAD):
                        w = slice(c * D, (c + 1) * D)
                        ins = product(o[:, w], XT[:, p, w], mat(w1), True, not two)
                        if two:
                            ins = product(o[:, w], XU[:, b, w], mat(w2), False, True)
                    ins.then_inc(S["product"], 1)

                def h_transpose(i, b):
                    pe.wait_ge(S["h_ready"], reach("h_ready", f, i, b))
                    pe.wait_ge(S["ht_ready"], freed("ht_ready", f, i, b, 1))
                    transposes(bank[:, 2, :], lambda c: O1[:, QUAD * b + c, :], S["h_transposed"])

                def h_product(i, b):
                    pe.wait_ge(S["ht_ready"], reach("ht_ready", f, i, b))
                    pe.wait_ge(S["qa_ready"], freed("qa_ready", f, i, b, 1))
                    for c in range(QUAD):
                        ins = product(bank[:, 6 + c // 2, 256 * (c % 2):256 * (c % 2) + QA],
                                      XV[:, b % 2, c * D:(c + 1) * D], WQA[:, :])
                    ins.then_inc(S["qa_product"], 1)

                def project(i, b):
                    pe.wait_ge(S["xt_ready"], reach("xt_ready", f, i, b))
                    for h in range(2):
                        keys, used = f"front_steps{h}", f"proj_used{h}"
                        pe.wait_ge(S[keys], freed(keys, f, i, b, 1))
                        pe.wait_ge(S[used], freed(used, f, i, b, 2))
                        for c in (2 * h, 2 * h + 1):
                            x, kb, vb = XT[:, b % 2, c * D:(c + 1) * D], key_bank(h), value_bank(b, h)
                            product(kb[:, c % 2, :], x, WE[:, 2 * D:PROJ])
                            product(vb[:, c % 2, :], x, WE[:, 0:2 * D], True, False)
                            ins = product(vb[:, c % 2, D:2 * D], row0[:, :], vec("bv"), False, True)
                        ins.then_inc(S[f"proj{h}"], 1)

                def logits_and_sage(i, b):
                    pe.wait_ge(S["xt_ready"], reach("xt_ready", f, i, b))
                    pe.wait_ge(S["xu_ready"], reach("xu_ready", f, i, b))
                    pe.wait_ge(S["self_gaps"], freed("self_gaps", f, i, b, 1))
                    pe.wait_ge(S["sage_biased"], freed("sage_biased", f, i, b, 1))
                    for c in range(QUAD):
                        w, o = slice(c * D, (c + 1) * D), wide34[:, c, :]
                        product(o[:, 0:D + HEADS], XU[:, b, w], WSELF[:, :], True, False)
                        ins = product(o[:, 0:D], XT[:, b % 2, w], mat("sage_wl"), False, True)
                    ins.then_inc(S["product"], 1)

                def own_h(i, b):
                    pe.wait_ge(S["self_used"], freed("self_used", f, i, b, 1))
                    for c in range(QUAD):
                        w = slice(c * D, (c + 1) * D)
                        ins = product(bank[:, 2, w], XU[:, b, w], mat("gat_w"))
                    ins.then_inc(S["own_h"], 1)

                def gat_and_tr(i, b):
                    for n, ready in enumerate(("gat_ready", "tr_ready")):
                        pe.wait_ge(S[ready], reach(ready, f, i, b))
                        pe.wait_ge(S["parts_ready"], freed("parts_ready", f, i, b, 1))
                        transposes(bank[:, 5 + n, :], lambda c: ST[:, QUAD * b + c, n * D:(n + 1) * D],
                                   S["parts_transposed"])

                def sage_part(i, b):
                    pe.wait_ge(S["sage_ready"], reach("sage_ready", f, i, b))
                    pe.wait_ge(S["parts_ready"], reach("parts_ready", f, i, b, 1))
                    transposes(bank[:, 5, :], lambda c: sage[:, b % 2, c, :], S["parts_transposed"])

                def fuse_product(i, b):
                    pe.wait_ge(S["parts_ready"], reach("parts_ready", f, i, b, 3))
                    pe.wait_ge(S["normed"], freed("normed", f, i, b, 1))
                    for c in range(QUAD):
                        w = slice(c * D, (c + 1) * D)
                        product(bank[:, 7, w], ones16[:, :], c0_rows[:, :], True, False)
                        product(bank[:, 7, w], XU[:, b, w], WS3[:, :], False, False)
                        product(bank[:, 7, w], XV[:, 0, w], mat("F1"), False, False)
                        product(bank[:, 7, w], XV[:, 1, w], mat("F3"), False, False)
                        ins = product(bank[:, 7, w], XV[:, 2, w], mat("F2"), False, True)
                    ins.then_inc(S["fused"], 1)

                if k == "in":
                    run(pe, [(first, 3), (second, 4)])
                elif k in ("gcn", "sage1", "sage2"):
                    run(pe, [(second, 1), (first, 0)])
                elif k == "conv":
                    run(pe, [(second, 1), (h_transpose, 3), (first, 0), (h_product, 4)])
                elif k == "attend":
                    run(pe, [(project, 1), (first, 0)])
                    carries += 1
                    pe.wait_ge(s_acarry, 1)
                    for n in range(4):
                        ins = product(bank[:, n, :], ones[:, :],
                                      cm[:, 4 * n:4 * n + 4, :].rearrange("p h q -> p (h q)"))
                    ins.then_inc(s_carry_p, 1)
                    pe.wait_ge(s_acarry, 2)
                    for n in range(2 * HEADS):
                        ins = nc.tensor.transpose(bank[:, n // 4, (n % 4) * P:(n % 4 + 1) * P], cm[:, n, :], ident[:, :])
                    ins.then_inc(s_carry_p, 1)
                    pe.wait_ge(s_acarry, 3)
                    for n in range(2 * HEADS):
                        product(bank[:, 4, n * (HC + 1):(n + 1) * (HC + 1)], cmT[:, n, :], rsv[:, n, :])
                    product(bank[:, 5, 0:D], carry_mask[:, :], ST[:, END_TILE, X_:X_ + D]).then_inc(s_carry_p, 1)
                    pe.wait_ge(s_carry_v, carries)
                elif k == "fuse":
                    run(pe, [(fuse_product, 3), (first, 0), (gat_and_tr, 2), (sage_part, 2), (logits_and_sage, 0),
                             (own_h, 1)])

        @block.scalar
        def _(act):
            act.preload_act_table_set("natural_log_exp_and_others")
            act.wait_ge(s_pool, 4)
            act.wait_ge(s_prepd, HI_LO)

            def onehots_hi(i, count, products=None):
                if products is not None:
                    act.wait_ge(s_onehot_hi, i)
                for c in range(count):
                    ins = nc.scalar.activation(oh_sq[:, c, :], iota[:, 0:P], ACT.Square,
                                               bias=t_f[4][:, bass.ds(i * 16 + c, 1)])
                ins.then_inc(s_square, 1)
                act.wait_ge(s_square, i + 1)
                if products is not None:
                    act.wait_ge(s_hist, products)
                nc.scalar.activation(oh_hi[:, 0:count, :], oh_sq[:, 0:count, :], ACT.Relu, bias=ones[:, 0:1],
                                     scale=-1.0).then_inc(s_onehot_hi, 1)

            onehots_hi(0, HI_SHARE)
            with act.Fori(1, COLS // 16) as i:
                onehots_hi(i, HI_SHARE, (i - 1) * 16 + HI_SHARE + 1)
            if COLS % 16:
                last = min(HI_SHARE, COLS % 16)
                onehots_hi(COLS // 16, last, COLS - COLS % 16 - 16 + last + 1)

            for f in range(len(PHASES)):
                k, what = PHASES[f]

                def copy(dest, source, waits, signal):
                    for w in waits:
                        act.wait_ge(*w)
                    nc.scalar.activation(dest, source, ACT.Copy).then_inc(signal, 1)

                def copies(i, b):
                    p = b % 2
                    user = {"attend": "proj1"}.get(k, "product")
                    copy(XT[:, p, :], bank[:, 0 if k in ("fuse", "conv") else p, :],
                         [(S["transposed"], reach("transposed", f, i, b)), (S[user], freed(user, f, i, b, 2))],
                         S["xt_ready"])
                    if k in ("conv", "sage1", "sage2", "fuse"):
                        user = {"fuse": "fused"}.get(k, "product")
                        copy(XU[:, b, :], bank[:, 1 if k in ("fuse", "conv") else 2 + p, :],
                             [(S["own_transposed"], reach("own_transposed", f, i, b)),
                              (S[user], freed(user, f, i, b, BODY))], S["xu_ready"])

                def rstd_of(mvt, rst, n=""):
                    def log(i, b):
                        act.wait_ge(S["stats" + n], reach("stats" + n, f, i, b))
                        nc.scalar.activation(rst[:, b % 2, 0, :], mvt[:, b % 2, :, 1], ACT.Ln, bias=eps[:, 0:1])\
                          .then_inc(S["rstd_steps" + n], 1)

                    def exp(i, b):
                        act.wait_ge(S["rstd_steps" + n], reach("rstd_steps" + n, f, i, b))
                        nc.scalar.activation(rst[:, b % 2, 1, :], rst[:, b % 2, 0, :], ACT.Exp, scale=-0.5)\
                          .then_inc(S["rstd" + n], 1)
                    return log, exp

                rstd_log, rstd = rstd_of(mv, rs)
                rstd2_log, rstd2 = rstd_of(mv2, rs2, "2")

                def relu_of(source, rst, nmt, n=""):
                    def go(i, b):
                        p = b % 2
                        act.wait_ge(S["shift" + n], reach("shift" + n, f, i, b))
                        if k == "in":
                            act.wait_ge(S["transposed"], freed("transposed", f, i, b, BODY))
                        else:
                            slot_stored(act, "table", f, i, b)
                        if k == "conv":
                            act.wait_ge(S["h_transposed"], freed("h_transposed", f, i, b, BODY))
                        dest = O2 if k == "in" else O1
                        for c in range(QUAD):
                            ins = nc.scalar.activation(dest[:, QUAD * b + c, :], source[:, QUAD * b + c, :], ACT.Relu,
                                                       bias=nmt[:, p, c:c + 1], scale=rst[:, p, 1, c:c + 1])
                        ins.then_inc(S["h_ready"], 1)
                    return go

                relu = relu_of(L2 if k == "in" else O2, rs, nm)

                def h_copy(i, b):
                    copy(XV[:, b % 2, :], bank[:, 2, :],
                         [(S["h_transposed"], reach("h_transposed", f, i, b)),
                          (S["qa_product"], freed("qa_product", f, i, b, 2))], S["ht_ready"])

                def exp_of(h):
                    def go(i, b):
                        act.wait_ge(S[f"gaps{h}"], reach(f"gaps{h}", f, i, b))
                        back = f"back_steps{h}"
                        act.wait_ge(S[back], freed(back, f, i, b, 1))
                        if h == 1:
                            act.wait_ge(S["state_ready"], freed("state_ready", f, i, b, 1))
                        nc.scalar.activation(exps[:, h, :, :], gaps[:, h, :, :], ACT.Exp).then_inc(S[f"exps{h}"], 1)
                    return go

                def self_exp(i, b):
                    act.wait_ge(S["self_gaps"], reach("self_gaps", f, i, b))
                    nc.scalar.activation(sexp[:, b % 2, :, :], sgap[:, b % 2, :, :], ACT.Exp)\
                      .then_inc(S["self_exps"], 1)

                def squares(i, b):
                    p = b % 2
                    act.wait_ge(S["sage_biased"], reach("sage_biased", f, i, b))
                    for c in range(QUAD):
                        if c:
                            act.wait_ge(S["sage_squares"], reach("sage_squares", f, i, b, c))
                        nc.scalar.activation(sq[:, :], sage[:, p, c, :], ACT.Square,
                                             accum_out=ss[:, p, 0, c:c + 1]).then_inc(S["sage_squares"], 1)

                def norm_log(i, b):
                    p = b % 2
                    act.wait_ge(S["sage_floor"], reach("sage_floor", f, i, b))
                    nc.scalar.activation(ss[:, p, 1, :], ss[:, p, 1, :], ACT.Ln, scale=float(2 ** 20))\
                      .then_inc(S["sage_log"], 1)

                def norm(i, b):
                    p = b % 2
                    act.wait_ge(S["sage_log"], reach("sage_log", f, i, b))
                    nc.scalar.activation(ss[:, p, 2, :], ss[:, p, 1, :], ACT.Exp, scale=-0.5, bias=lnb[:, 0:1])\
                      .then_inc(S["sage_norm"], 1)

                def part_copy(n):
                    def go(i, b):
                        copy(XV[:, n, :], bank[:, 5 + n % 2, :],
                             [(S["parts_transposed"], reach("parts_transposed", f, i, b, n + 1)),
                              (S["fused"], freed("fused", f, i, b, 1))], S["parts_ready"])
                    return go

                def mean(i, b):
                    act.wait_ge(gathered[b], slot_done(GATHERS, f, i, b))
                    act.sem_inc(s_actw, 1)
                    for c in range(QUAD):
                        x = ST[:, QUAD * b + c, X_:X_ + D]
                        ins = nc.scalar.activation(x, x, ACT.Copy,
                                                   scale=invdeg[:, bass.ds(STEP * i + QUAD * b + c, 1)])
                    ins.then_inc(S["agg_ready"], 1)

                def normed(i, b):
                    p = b % 2
                    act.wait_ge(S["shift"], reach("shift", f, i, b))
                    act.wait_ge(S["x_ready"], freed("x_ready", f, i, b, 2))
                    for c in range(QUAD):
                        ins = nc.scalar.activation(zn[:, p, c, :], bank[:, 7, c * D:(c + 1) * D], ACT.Identity,
                                                   bias=nm[:, p, c:c + 1], scale=rs[:, p, 1, c:c + 1])
                    ins.then_inc(S["normed"], 1)

                if k == "in":
                    run(act, [(copies, 3), (relu, 1), (rstd_log, 0), (rstd, 0)])
                elif k in ("gcn", "sage1", "sage2"):
                    run(act, [(copies, 0)])
                elif k == "gcn_out":
                    run(act, [(relu, 1), (rstd_log, 0), (rstd, 0)])
                elif k == "conv":
                    run(act, [(copies, 0), (relu, 2), (h_copy, 3), (rstd_log, 1), (rstd, 1)])
                elif k == "attend":
                    run(act, [(exp_of(0), 1), (copies, 0), (exp_of(1), 1)])
                    act.wait_ge(s_cgap, 1)
                    nc.scalar.activation(cm, cm, ACT.Exp).then_inc(s_act, 1)
                    act.wait_ge(s_cgap, 2)
                    nc.scalar.activation(mc[:, 2:4, :], mc[:, 2:4, :], ACT.Exp).then_inc(s_act, 1)
                elif k == "fuse":
                    run(act, [(part_copy(2), 3), (normed, 4), (norm_log, 2), (norm, 2), (relu_of(O2, rs2, nm2, "2"), 6),
                              (mean, 0), (squares, 1), (copies, 0), (part_copy(0), 2), (rstd2_log, 5),
                              (rstd_log, 3), (rstd2, 5), (self_exp, 1), (part_copy(1), 2), (rstd, 3)])

        @block.vector
        def _(dve):
            V = nc.vector
            steps = [0]

            def prep(ins):
                steps[0] += 1
                ins.then_inc(s_prepd, 1)
                dve.wait_ge(s_prepd, steps[0])

            dve.wait_ge(s_const, 16 * (len(consts) + 2))
            prep(V.tensor_scalar(blk[:, 0, :], hmask[:, :], attc[:, 0:1], None, ALU.mult))
            prep(V.tensor_scalar(blk[:, 1, :], hmask[:, :], attc[:, 1:2], None, ALU.mult))
            prep(V.tensor_scalar(blk[:, 3, :], hmask[:, :], attc[:, 2:3], None, ALU.mult))
            prep(V.tensor_tensor(blk[:, 2, :], blk[:, 0, :], blk[:, 1, :], ALU.add))
            assert steps[0] == BLK
            prep(V.memset(G[:, :, :], 0.0))
            V.memset(ST[:, :, :], 0.0).then_inc(s_zero, 1)
            prep(V.tensor_copy(dst[:, :], dst_i[:, 0:COLS]))
            prep(V.memset(same[:, 0:1], 0.0))
            prep(V.tensor_tensor(same[:, 1:COLS], dst[:, 1:COLS], dst[:, 0:COLS - 1], ALU.is_equal))
            prep(V.tensor_scalar(gapneg[:, :], same[:, :], 1.0, -NEG, ALU.subtract, ALU.mult))
            quot, hi, lo, flag, hi_neg = t_f
            prep(V.tensor_scalar(quot, dst[:, :], 1.0 / COLS, None, ALU.mult))
            prep(V.tensor_copy(t_i, quot))
            prep(V.tensor_copy(hi, t_i))
            prep(V.scalar_tensor_tensor(out=lo, in0=hi, scalar=-float(COLS), in1=dst[:, :], op0=ALU.mult, op1=ALU.add))
            prep(V.tensor_scalar(flag, lo, 0.0, None, ALU.is_lt))
            prep(V.tensor_tensor(hi, hi, flag, ALU.subtract))
            prep(V.tensor_scalar(flag, lo, float(COLS), None, ALU.is_ge))
            prep(V.tensor_tensor(hi, hi, flag, ALU.add))
            prep(V.scalar_tensor_tensor(out=lo, in0=hi, scalar=-float(COLS), in1=dst[:, :], op0=ALU.mult, op1=ALU.add))

            prep(V.tensor_scalar(hi_neg, hi, -1.0, None, ALU.mult))
            assert steps[0] == HI_LO

            def onehot(col, c):
                if c >= HI_SHARE:
                    V.tensor_scalar(oh_hi[:, c, :], iota[:, 0:P], hi[:, bass.ds(col, 1)], None, ALU.is_equal)
                V.tensor_scalar(oh_lo[:, c, :], iota[:, :], lo[:, bass.ds(col, 1)], None, ALU.is_equal)\
                 .then_inc(s_onehot, 1)

            for c in range(16):
                onehot(c, c)
            with dve.Fori(1, COLS // 16) as i:
                for c in range(16):
                    dve.wait_ge(s_hist, (i - 1) * 16 + c + 2)
                    onehot(i * 16 + c, c)
            for c in range(COLS % 16):
                dve.wait_ge(s_hist, COLS - COLS % 16 - 16 + c + 2)
                onehot(COLS - COLS % 16 + c, c)
            dve.wait_ge(s_hist, COLS + 2)
            deg, deg1, run_, t3, _ = t_f
            prep(V.tensor_copy(deg, bank[:, 0, 0:COLS]))
            prep(V.tensor_scalar(deg1, deg, 1.0, None, ALU.add))
            assert steps[0] == DEG
            prep(V.tensor_scalar(t3, deg, 1.0, None, ALU.max))
            prep(V.reciprocal(invdeg[:, :], t3))
            prep(V.tensor_scalar(has[:, :], deg, 0.0, None, ALU.is_gt))
            prep(V.memset(t3, 1.0))
            prep(V.tensor_tensor_scan(run_, t3, deg, 0.0, ALU.mult, ALU.add))
            assert steps[0] == TOTALS
            dve.wait_ge(s_prep, 8)
            prep(V.tensor_copy(t3[:, 0:1], bank[:, 5, 0:1]))
            prep(V.tensor_scalar(run_, run_, t3[:, 0:1], -1.0, ALU.add, ALU.add))
            prep(V.tensor_scalar(run_, run_, emptyrow[:, 0:1], None, ALU.subtract))
            prep(V.tensor_tensor(run_, run_, has[:, :], ALU.mult))
            prep(V.tensor_scalar(last_i[:, 0:COLS], run_, emptyrow[:, 0:1], None, ALU.add))
            prep(V.tensor_scalar(XT[:, 0, 0:P], ident[:, :], dst[:, 0:1], None, ALU.mult))
            prep(V.tensor_scalar(XT[:, 0, P:2 * P], ident[:, :], dst[:, COLS - 1:COLS], None, ALU.mult))
            assert steps[0] == DIAG
            dve.wait_ge(s_prep, 10)
            prep(V.scalar_tensor_tensor(out=carry_mask[:, :], in0=bank[:, 6, 0:P], scalar=dst[:, COLS - 1:COLS],
                                        in1=upper[:, :], op0=ALU.is_equal, op1=ALU.mult))
            prep(V.scalar_tensor_tensor(out=carry_maskT[:, :], in0=bank[:, 6, P:2 * P], scalar=dst[:, 0:1],
                                        in1=lower[:, :], op0=ALU.is_equal, op1=ALU.mult))
            prep(V.tensor_scalar(deg, dst[:, :], dst[:, 0:1], None, ALU.is_equal))
            prep(V.tensor_reduce(t3[:, 1:2], deg, AX.X, ALU.add))
            prep(V.tensor_scalar(first_end[:, :], t3[:, 1:2], firstrow[:, 0:1], None, ALU.add))
            prep(V.tensor_copy(WE[:, 0:D], mat("gat_w")))
            prep(V.tensor_copy(WE[:, D:2 * D], mat("wv")))
            prep(V.tensor_copy(WE[:, 2 * D:3 * D], mat("wk")))
            prep(V.tensor_copy(WE[:, 3 * D:PROJ], bank[:, 1, 0:HEADS]))
            scale = HC ** -0.5
            prep(V.tensor_scalar(WQA[:, 0:D], mat("wq"), scale, None, ALU.mult))
            prep(V.tensor_copy(WQA[:, D:D + HEADS], bank[:, 1, 16:16 + HEADS]))
            prep(V.tensor_scalar(WQA[:, D + HEADS:QA], bank[:, 1, 48:48 + HEADS], scale, None, ALU.mult))
            prep(V.tensor_scalar(BQA[:, 0:D], vec("bq"), scale, None, ALU.mult))
            prep(V.memset(BQA[:, D:D + HEADS], 0.0))
            prep(V.tensor_scalar(BQA[:, D + HEADS:QA], bank[:, 1, 64:64 + HEADS], scale, None, ALU.mult))
            prep(V.tensor_copy(WSELF[:, 0:D], mat("sage_wr")))
            prep(V.tensor_copy(WSELF[:, D:D + HEADS], bank[:, 1, 32:32 + HEADS]))
            prep(V.tensor_copy(WS3[:, :], bank[:, 2, 0:D]))
            prep(V.tensor_tensor(c0[:, :], bank[:, 3, 0:D], vec("fus_b"), ALU.add))
            prep(V.memset(ones16[:, :], 1.0))
            prep(V.tensor_copy(c0_rest[:, :], c0[:, :]))
            for n in range(3):
                prep(V.tensor_copy(c0_parts[:, n, :], c0_rest[:, :]))
                prep(V.tensor_tensor(c0_rest[:, :], c0_rest[:, :], c0_parts[:, n, :], ALU.subtract))
            prep(V.tensor_scalar(c0_rows[:, :], c0_parts[:, 0, :], ident[:, 0:1], None, ALU.mult))
            for n in (1, 2):
                prep(V.scalar_tensor_tensor(out=c0_rows[:, :], in0=c0_parts[:, n, :], scalar=ident[:, n:n + 1],
                                            in1=c0_rows[:, :], op0=ALU.mult, op1=ALU.add))
            prep(V.tensor_tensor(bsum[:, 0, :], vec("bn1"), vec("bs1"), ALU.add))
            prep(V.tensor_tensor(bsum[:, 1, :], vec("bn2"), vec("bs2"), ALU.add))
            assert steps[0] == SETUP_END

            carries = 0
            carry_products = 0
            local = [0]

            def did(ins):
                local[0] += 1
                ins.then_inc(s_dve, 1)
                dve.wait_ge(s_dve, local[0])

            for f in range(len(PHASES)):
                k, what = PHASES[f]
                index = src_i if k in ("edge", "attend") else last_i

                def stage_indices(i, b):
                    dve.wait_ge(gathered[b], slot_done(GATHERS, f, i, b))
                    copy_indices(i + 1, b)

                def copy_indices(i, b):
                    w = bass.ds(STEP * i + QUAD * b, QUAD)
                    t = slice(QUAD * b, QUAD * (b + 1))
                    V.tensor_scalar(stage[:, t], index[:, w], 0, None, ALU.add).then_inc(S["idx"], 1)
                    if k == "attend":
                        V.tensor_scalar(stage2[:, t], dst_i[:, w], 0, None, ALU.add).then_inc(S["idx2"], 1)

                if k != "in":
                    dve.wait_ge(S["idx"], before("idx", f))
                    for b in range(BODY):
                        copy_indices(0, b)

                def product_bank(b):
                    return bank[:, 4 + b % 2, :].rearrange("p (c f) -> p c f", c=QUAD)

                def sample(i, b, source, bstt, n=""):
                    user = "normed" if k == "fuse" and not n else "h_ready"
                    dve.wait_ge(S[user], freed(user, f, i, b, 2))
                    for c in range(QUAD):
                        V.bn_stats(bstt[:, b % 2, c, :], source[:, c, :]).then_inc(S["norm_steps" + n], 1)

                def moments(i, b, mvt, bstt, n=""):
                    dve.wait_ge(S["norm_steps" + n], reach("norm_steps" + n, f, i, b, QUAD))
                    dve.sem_inc(s_dvew, 1)
                    for c in range(QUAD):
                        ins = V.bn_aggr(mvt[:, b % 2, c, :], bstt[:, b % 2, c, :])
                    ins.then_inc(S["stats" + n], 1)

                def stats(i, b, source):
                    sample(i, b, source, bst)
                    moments(i, b, mv, bst)

                def shift(i, b, mvt=mv, rst=rs, nmt=nm, n=""):
                    p = b % 2
                    dve.wait_ge(S["rstd" + n], reach("rstd" + n, f, i, b))
                    V.scalar_tensor_tensor(out=nmt[:, p, :], in0=mvt[:, p, :, 0], scalar=-1.0, in1=rst[:, p, 1, :],
                                           op0=ALU.mult, op1=ALU.mult).then_inc(S["shift" + n], 1)

                def sums_of(i, b):
                    stage_indices(i, b)
                    for c in range(QUAD):
                        t = QUAD * b + c
                        dve.wait_ge(S["summed"], reach("summed", f, i, b, c))
                        V.scalar_tensor_tensor(out=G[:, t, :], in0=G[:, prior_tiles(b, c), :],
                                               scalar=same[:, bass.ds(STEP * i + t, 1)], in1=G[:, t, :],
                                               op0=ALU.mult, op1=ALU.add).then_inc(S["summed"], 1)

                def in_sample(i, b):
                    dve.wait_ge(res_loaded[b], slot_done(RES_LOADS, f, i, b))
                    sample(i, b, quad(L2, b), bst)

                def in_moments(i, b):
                    moments(i, b, mv, bst)

                def aggregate(i, b):
                    stage_indices(i, b)
                    g = quad(G, b)
                    if k in ("gcn", "gcn_out"):
                        dve.wait_ge(loaded[b], slot_done(LOADS, f, i, b))
                        V.tensor_tensor(g, g, quad(L1, b), ALU.add).then_inc(S["agg_steps"], 1)
                        dve.wait_ge(S["agg_steps"], reach("agg_steps", f, i, b, 1))
                        if k == "gcn":
                            V.tensor_tensor(g, g, per_col(dinv, i, b), ALU.mult).then_inc(S["agg_ready"], 1)
                            return
                        slot_stored(dve, "residual", f, i, b)
                        dve.wait_ge(S["h_ready"], freed("h_ready", f, i, b, BODY))
                        dve.wait_ge(res_loaded[b], slot_done(RES_LOADS, f, i, b))
                        for c in range(QUAD):
                            t = QUAD * b + c
                            ins = V.scalar_tensor_tensor(out=O2[:, t, :], in0=G[:, t, :],
                                                         scalar=dinv[:, bass.ds(STEP * i + t, 1)], in1=L2[:, t, :],
                                                         op0=ALU.mult, op1=ALU.add)
                        ins.then_inc(S["x_ready"], 1)
                        dve.wait_ge(S["x_ready"], reach("x_ready", f, i, b))
                        stats(i, b, quad(O2, b))
                    elif k in ("sage1", "sage2"):
                        V.tensor_tensor(g, g, per_col(invdeg, i, b), ALU.mult).then_inc(S["agg_ready"], 1)

                def post_bias(i, b):
                    bias = {"in": lambda: vec("b0"), "gcn": lambda: vec(f"b{what}"), "sage1": lambda: bsum[:, 0, :],
                            "sage2": lambda: bsum[:, 1, :]}[k]()
                    dve.wait_ge(S["product"], reach("product", f, i, b))
                    slot_stored(dve, "table", f, i, b)
                    V.tensor_tensor(quad(O1, b), product_bank(b), over_quad(bias), ALU.add).then_inc(S["biased"], 1)

                def post_scale(i, b):
                    o = quad(O1, b)
                    dve.wait_ge(S["biased"], reach("biased", f, i, b))
                    if k in ("in", "gcn"):
                        if k == "in":
                            dve.wait_ge(s_dinv, i + 1)
                        ins = V.scalar_tensor_tensor(out=o, in0=o, scalar=0.0, in1=per_col(dinv, i, b),
                                                     op0=ALU.max, op1=ALU.mult)
                    elif k == "sage1":
                        ins = V.tensor_scalar(o, o, 0.0, None, ALU.max)
                    else:
                        dve.wait_ge(res_loaded[b], slot_done(RES_LOADS, f, i, b))
                        ins = V.tensor_tensor(o, o, quad(L2, b), ALU.add)
                    ins.then_inc(S["out_ready"], 1)

                def conv_x(i, b):
                    dve.wait_ge(S["product"], reach("product", f, i, b))
                    dve.wait_ge(res_loaded[b], slot_done(RES_LOADS, f, i, b))
                    slot_stored(dve, "residual", f, i, b)
                    dve.wait_ge(S["h_ready"], freed("h_ready", f, i, b, BODY))
                    V.tensor_tensor(quad(O2, b), product_bank(b), quad(L2, b), ALU.add).then_inc(S["x_ready"], 1)
                    dve.wait_ge(S["x_ready"], reach("x_ready", f, i, b))
                    stats(i, b, quad(O2, b))
                    V.tensor_tensor(quad(ST, b)[:, :, 0:D], quad(O2, b), over_quad(vec("ln_b")), ALU.add)\
                     .then_inc(S["based"], 1)

                def conv_qa(i, b):
                    dve.wait_ge(S["qa_product"], reach("qa_product", f, i, b))
                    slot_stored(dve, "qa", f, i, b)
                    V.tensor_tensor(quad(QG, b), wide67[:, :, 0:QA], over_quad(BQA[:, :]), ALU.add)\
                     .then_inc(S["qa_ready"], 1)

                def heads(t):
                    return t.rearrange("p c (h e) -> p c h e", e=HC)

                def attend_pair(h):
                    o = 1 - h
                    fs, bs = f"front_steps{h}", f"back_steps{o}"

                    def go(i, b, front=True, back=True):
                        t0 = QUAD * b + 2 * h
                        pair = slice(t0, t0 + 2)
                        pj = key_bank(h)
                        bi, bb = (i, b) if h else ((i, b - 1) if b else (i - 1, BODY - 1))
                        u0 = QUAD * bb + 2 * o
                        pjo = value_bank(bb, o)

                        def after(n):
                            dve.wait_ge(S[fs], reach(fs, f, i, b, n))

                        def after_back(n):
                            dve.wait_ge(S[bs], reach(bs, f, bi, bb, n))

                        def back_state(c, part):
                            t, before_t = u0 + c, (u0 + c - 1) % STEP
                            r = exps[:, o, c, 0:2 * HEADS]
                            if part == "R":
                                if c:
                                    after_back(4)
                                V.tensor_tensor(ST[:, t, 0:2 * D].rearrange("p (h e) -> p h e", e=HC),
                                                ST[:, before_t, 0:2 * D].rearrange("p (h e) -> p h e", e=HC),
                                                r.unsqueeze(2).to_broadcast([P, 2 * HEADS, HC]), ALU.mult)\
                                 .then_inc(S[bs], 1)
                            elif part == "S":
                                if c:
                                    after_back(5)
                                V.tensor_tensor(ST[:, t, S_:SW], ST[:, before_t, S_:SW], r, ALU.mult)\
                                 .then_inc(S[bs], 1)
                            elif part == "X":
                                V.scalar_tensor_tensor(out=ST[:, t, X_:M_], in0=ST[:, before_t, X_:M_],
                                                       scalar=same[:, bass.ds(STEP * bi + t, 1)], in1=G[:, t, :],
                                                       op0=ALU.mult, op1=ALU.add).then_inc(S[bs], 1)
                            elif part == "R+":
                                dve.wait_ge(S[f"proj_used{o}"], reach(f"proj_used{o}", f, bi, bb))
                                after_back(5 * c + 1)
                                V.tensor_tensor(ST[:, t, 0:2 * D], ST[:, t, 0:2 * D], tmp[:, c, :], ALU.add)\
                                 .then_inc(S[bs], 1)
                            else:
                                after_back(5 * c + 2)
                                V.tensor_tensor(ST[:, t, S_:SW], ST[:, t, S_:SW], exps[:, o, c, 2 * HEADS:], ALU.add)\
                                 .then_inc(S["state_ready" if (o, c) == (1, 1) else bs], 1)

                        if front:
                            dve.wait_ge(S[f"proj{h}"], reach(f"proj{h}", f, i, b))
                            V.tensor_tensor(prod[:, h], pj[:, :, 0:D], QG[:, pair, 0:D], ALU.mult)\
                             .then_inc(S[fs], 1)
                            V.tensor_tensor(asum[:, h], pj[:, :, D:D + HEADS], QG[:, pair, D:D + HEADS], ALU.add)\
                             .then_inc(S[fs], 1)
                        if back:
                            if o == 1:
                                dve.wait_ge(S["back_steps0"], reach("back_steps0", f, bi, bb, 10))
                            else:
                                dve.wait_ge(S["state_ready"], reach("state_ready", f, bi, bb, 0))
                            dve.wait_ge(S[f"exps{o}"], reach(f"exps{o}", f, bi, bb))
                            V.tensor_tensor(heads(tmp[:, :, :]), heads(pjo),
                                            exps[:, o, :, 2 * HEADS:].unsqueeze(3).to_broadcast([P, 2, 2 * HEADS, HC]),
                                            ALU.mult).then_inc(S[f"proj_used{o}"], 1)
                        if front:
                            after(1)
                            V.tensor_reduce(red[:, h], heads(prod[:, h]), AX.X, ALU.add).then_inc(S[fs], 1)
                            after(2)
                            V.scalar_tensor_tensor(out=lg[:, h, :, 0:HEADS], in0=asum[:, h], scalar=0.2,
                                                   in1=asum[:, h], op0=ALU.mult, op1=ALU.max).then_inc(S[fs], 1)
                        if back:
                            back_state(0, "R")
                        if front:
                            after(3)
                            V.tensor_tensor(lg[:, h, :, HEADS:], red[:, h], QG[:, pair, D + HEADS:QA], ALU.add)\
                             .then_inc(S[fs], 1)
                        if back:
                            back_state(0, "S")
                            back_state(0, "X")
                        for c in range(2):
                            if front:
                                if c == 0:
                                    after(5)
                                    if h == 0:
                                        slot_stored(dve, "table", f, i, b)
                                    other = f"front_steps{o}"
                                    dve.wait_ge(S[other], reach(other, f, i, b, 7 if h else 0))
                                else:
                                    after(6)
                                V.scalar_tensor_tensor(
                                    out=ST[:, t0 + c, M_:S_], in0=ST[:, (t0 + c - 1) % STEP, M_:S_],
                                    scalar=gapneg[:, bass.ds(STEP * i + t0 + c, 1)], in1=lg[:, h, c, :],
                                    op0=ALU.add, op1=ALU.max).then_inc(S[fs], 1)
                            if back:
                                back_state(0, ("R+", "S+")[c])
                                if c:
                                    back_state(1, "R")
                        if front:
                            after(7)
                            dve.wait_ge(S[f"exps{h}"], freed(f"exps{h}", f, i, b, 1))
                            V.tensor_tensor(gaps[:, h, :, 2 * HEADS:], lg[:, h], ST[:, pair, M_:S_], ALU.subtract)
                            for c in range(2):
                                ins = V.scalar_tensor_tensor(
                                    out=gaps[:, h, c, 0:2 * HEADS], in0=ST[:, (t0 + c - 1) % STEP, M_:S_],
                                    scalar=gapneg[:, bass.ds(STEP * i + t0 + c, 1)], in1=ST[:, t0 + c, M_:S_],
                                    op0=ALU.add, op1=ALU.subtract)
                            ins.then_inc(S[f"gaps{h}"], 1)
                        if back:
                            for part in ("S", "X", "R+", "S+"):
                                back_state(1, part)
                    return go

                attend_first, attend_second = attend_pair(0), attend_pair(1)

                def attend_pairs(i, b):
                    attend_first(i, b, back=not (isinstance(i, int) and (i, b) == (0, 0)))
                    attend_second(i, b)

                H = bank[:, 2, :].rearrange("p (c f) -> p c f", c=QUAD)
                SL = wide34[:, :, D:D + HEADS]
                FUSED = bank[:, 7, :].rearrange("p (c f) -> p c f", c=QUAD)

                def self_step(i, b, n, ins):
                    dve.wait_ge(S["self_steps"], reach("self_steps", f, i, b, n))
                    ins().then_inc(S["self_steps"], 1)

                def self_leak(i, b):
                    dve.wait_ge(S["product"], reach("product", f, i, b))
                    V.tensor_scalar(slog[:, :, :], SL, 0.2, None, ALU.mult).then_inc(S["self_steps"], 1)

                def self_logit(i, b):
                    self_step(i, b, 1, lambda: V.tensor_tensor(slog[:, :, :], slog[:, :, :], SL, ALU.max))

                def self_max(i, b):
                    self_step(i, b, 2, lambda: V.tensor_tensor(sm[:, :, :], slog[:, :, :],
                                                               quad(ST, b)[:, :, M_:M_ + HEADS], ALU.max))

                def self_gap(i, b):
                    dve.wait_ge(S["self_steps"], reach("self_steps", f, i, b, 3))
                    dve.wait_ge(S["sage_ready"], freed("sage_ready", f, i, b, 2))
                    V.tensor_tensor(sgap[:, b % 2, :, 0:HEADS], quad(ST, b)[:, :, M_:M_ + HEADS], sm[:, :, :],
                                    ALU.subtract)
                    V.tensor_tensor(sgap[:, b % 2, :, HEADS:], slog[:, :, :], sm[:, :, :], ALU.subtract)\
                     .then_inc(S["self_gaps"], 1)

                def sage_bias(i, b):
                    dve.wait_ge(S["product"], reach("product", f, i, b))
                    dve.wait_ge(S["parts_transposed"], freed("parts_transposed", f, i, b, 2))
                    V.tensor_tensor(sage[:, b % 2, :, :], wide34[:, :, 0:D], over_quad(vec("sage_bl")), ALU.add)\
                     .then_inc(S["sage_biased"], 1)

                def floor(i, b):
                    p = b % 2
                    dve.wait_ge(S["sage_squares"], reach("sage_squares", f, i, b, QUAD))
                    V.tensor_scalar(ss[:, p, 1, :], ss[:, p, 0, :], 1e-24, None, ALU.max).then_inc(S["sage_floor"], 1)

                def blend_step(i, b, n, ins):
                    if n:
                        dve.wait_ge(S["blend_steps"], reach("blend_steps", f, i, b, n))
                    ins().then_inc(S["blend_steps"], 1)

                def by_head(t):
                    return t.unsqueeze(3).to_broadcast([P, QUAD, HEADS, HC])

                def sum_scale(i, b):
                    dve.wait_ge(S["self_exps"], reach("self_exps", f, i, b))
                    blend_step(i, b, 0, lambda: V.tensor_tensor(zz[:, :, 0:HEADS], quad(ST, b)[:, :, S_:S_ + HEADS],
                                                                sexp[:, b % 2, :, 0:HEADS], ALU.mult))
                    blend_step(i, b, 0, lambda: V.tensor_copy(zz[:, :, HEADS:], quad(ST, b)[:, :, S_ + HEADS:SW]))

                def sum_self(i, b):
                    blend_step(i, b, 1, lambda: V.tensor_tensor(zz[:, :, 0:HEADS], zz[:, :, 0:HEADS],
                                                                sexp[:, b % 2, :, HEADS:], ALU.add))

                def sum_floor(i, b):
                    blend_step(i, b, 3, lambda: V.tensor_scalar(zz[:, :, :], zz[:, :, :], 1e-16, None, ALU.max))

                def sum_inverse(i, b):
                    blend_step(i, b, 4, lambda: V.reciprocal(zz[:, :, :], zz[:, :, :]))

                def self_weights(i, b):
                    e = sexp[:, b % 2, :, :].rearrange("p c (g h) -> p c g h", g=2)
                    blend_step(i, b, 5, lambda: V.tensor_tensor(
                        e, e, zz[:, :, 0:HEADS].unsqueeze(2).to_broadcast([P, QUAD, 2, HEADS]), ALU.mult))

                def tr_divide(i, b):
                    dve.wait_ge(S["blend_steps"], reach("blend_steps", f, i, b, 5))
                    tr = heads(quad(ST, b)[:, :, D:2 * D])
                    V.tensor_tensor(tr, tr, by_head(zz[:, :, HEADS:]), ALU.mult).then_inc(S["tr_ready"], 1)

                def gat_divide(i, b):
                    gat = heads(quad(ST, b)[:, :, 0:D])
                    blend_step(i, b, 6, lambda: V.tensor_tensor(gat, gat, by_head(sexp[:, b % 2, :, 0:HEADS]),
                                                                ALU.mult))

                def own_weighted(i, b):
                    dve.wait_ge(S["own_h"], reach("own_h", f, i, b))
                    dve.wait_ge(S["blend_steps"], reach("blend_steps", f, i, b, 6))
                    V.tensor_tensor(heads(hself[:, :, :]), heads(H), by_head(sexp[:, b % 2, :, HEADS:]), ALU.mult)\
                     .then_inc(S["self_used"], 1)

                def gat_add(i, b):
                    dve.wait_ge(S["self_used"], reach("self_used", f, i, b))
                    dve.wait_ge(S["blend_steps"], reach("blend_steps", f, i, b, 7))
                    gat = quad(ST, b)[:, :, 0:D]
                    V.tensor_tensor(gat, gat, hself[:, :, :], ALU.add).then_inc(S["gat_ready"], 1)

                def sage_scale(i, b):
                    p = b % 2
                    dve.wait_ge(S["sage_norm"], reach("sage_norm", f, i, b))
                    V.tensor_tensor(sage[:, p, :, :], sage[:, p, :, :],
                                    ss[:, p, 2, :].unsqueeze(2).to_broadcast([P, QUAD, D]), ALU.mult)\
                     .then_inc(S["sage_ready"], 1)

                def fused_sample(i, b):
                    dve.wait_ge(S["fused"], reach("fused", f, i, b))
                    sample(i, b, FUSED, bst)

                def fused_moments(i, b):
                    moments(i, b, mv, bst)

                def fused_gain(i, b):
                    z = zn[:, b % 2, :, :]
                    dve.wait_ge(S["normed"], reach("normed", f, i, b))
                    V.tensor_tensor(z, z, over_quad(vec("ln_g")), ALU.mult).then_inc(S["x3_steps"], 1)

                def fused_x(i, b):
                    dve.wait_ge(S["x3_steps"], reach("x3_steps", f, i, b, 1))
                    slot_stored(dve, "residual", f, i, b)
                    dve.wait_ge(res_loaded[b], slot_done(RES_LOADS, f, i, b))
                    V.tensor_tensor(quad(O2, b), zn[:, b % 2, :, :], quad(L2, b), ALU.add).then_inc(S["x_ready"], 1)

                def x_sample(i, b):
                    dve.wait_ge(S["x_ready"], reach("x_ready", f, i, b))
                    sample(i, b, quad(O2, b), bst2, "2")

                def x_moments(i, b):
                    moments(i, b, mv2, bst2, "2")

                def shift2(i, b):
                    shift(i, b, mv2, rs2, nm2, "2")

                if k == "in":
                    run(dve, [(shift, 1), (in_sample, 0), (post_scale, 4), (in_moments, 0), (post_bias, 3)])
                elif k == "edge":
                    run(dve, [(sums_of, 0)])
                    carries += 1
                    carry_products += 1
                    if carries > 1:
                        dve.wait_ge(s_carry_d, 16 * (carries - 1))
                    dve.wait_ge(s_carry_p, carry_products)
                    V.tensor_copy(carry[:, :], bank[:, 0, 0:D]).then_inc(s_carry_v, 1)
                elif k in ("gcn", "sage1", "sage2"):
                    run(dve, [(post_bias, 2), (post_scale, 2), (aggregate, 0)])
                elif k == "gcn_out":
                    run(dve, [(aggregate, 0), (shift, 1)])
                elif k == "conv":
                    run(dve, [(stage_indices, 0), (shift, 2), (conv_x, 1), (conv_qa, 4)])
                elif k == "fuse":
                    run(dve, [(sum_scale, 2), (shift, 4), (sum_self, 2), (stage_indices, 0), (sum_floor, 2),
                              (shift2, 6), (sum_inverse, 2), (sage_bias, 1), (self_weights, 2), (self_leak, 1),
                              (tr_divide, 2), (gat_divide, 2), (self_logit, 1), (fused_gain, 4), (self_max, 1),
                              (own_weighted, 2), (sage_scale, 2), (self_gap, 1), (gat_add, 2), (fused_sample, 3),
                              (fused_x, 4), (fused_moments, 3), (x_sample, 4), (floor, 1), (x_moments, 4)])
                elif k == "attend":
                    run(dve, [(attend_pairs, 1), (stage_indices, 0)])
                    attend_first(NQ // BODY, NQ % BODY, front=False)
                    carries += 1
                    HH = 2 * HEADS
                    end = ST[:, END_TILE, :]
                    dve.wait_ge(S["state_ready"], before("state_ready", f + 1))
                    did(V.tensor_tensor(rsv[:, :, 0:HC], end[:, 0:2 * D].rearrange("p (h e) -> p h e", e=HC),
                                        end[:, 0:2 * D].rearrange("p (h e) -> p h e", e=HC), ALU.max))
                    did(V.tensor_copy(rsv[:, :, HC], end[:, S_:SW]))
                    did(V.tensor_scalar(XT[:, 0, 0:P], carry_maskT[:, :], 1.0, -NEG, ALU.subtract, ALU.mult))
                    V.tensor_tensor(cm, ident[:, :].unsqueeze(1).to_broadcast([P, HH, P]),
                                    end[:, M_:S_].unsqueeze(2).to_broadcast([P, HH, P]), ALU.mult).then_inc(s_acarry, 1)
                    spread = bank[:, 0:4, :].rearrange("p a (t q) -> p (a t) q", t=4)
                    dve.wait_ge(s_carry_p, carry_products + 1)
                    did(V.tensor_tensor(cm, spread, XT[:, 0, 0:P].unsqueeze(1).to_broadcast([P, HH, P]), ALU.add))
                    did(V.tensor_reduce(mc[:, 0, :], cm, AX.X, ALU.max))
                    V.tensor_tensor(cm, cm, mc[:, 0, :].unsqueeze(2).to_broadcast([P, HH, P]), ALU.subtract)\
                     .then_inc(s_cgap, 1)
                    dve.wait_ge(s_act, 1)
                    V.tensor_tensor(cm, cm, carry_maskT[:, :].unsqueeze(1).to_broadcast([P, HH, P]), ALU.mult)\
                     .then_inc(s_acarry, 1)
                    dve.wait_ge(s_carry_p, carry_products + 2)
                    V.tensor_copy(cmT, spread).then_inc(s_acarry, 1)
                    dve.wait_ge(s_fixg, 16)
                    m1, ga, gb, sc = mc[:, 1, :], mc[:, 2, :], mc[:, 3, :], mc[:, 4, :]
                    did(V.tensor_tensor(m1, mc[:, 0, :], fixrow[:, M_:S_], ALU.max))
                    did(V.tensor_tensor(ga, mc[:, 0, :], m1, ALU.subtract))
                    V.tensor_tensor(gb, fixrow[:, M_:S_], m1, ALU.subtract).then_inc(s_cgap, 1)
                    dve.wait_ge(s_act, 2)
                    dve.wait_ge(s_carry_p, carry_products + 3)
                    carry_products += 3
                    rc = bank[:, 4, 0:HH * (HC + 1)].rearrange("p (h e) -> p h e", e=HC + 1)
                    fr = fixrow[:, 0:2 * D].rearrange("p (h e) -> p h e", e=HC)
                    ft = fixtmp[:, 0:2 * D].rearrange("p (h e) -> p h e", e=HC)
                    did(V.tensor_tensor(ft, rc[:, :, 0:HC], ga.unsqueeze(2).to_broadcast([P, HH, HC]), ALU.mult))
                    did(V.tensor_tensor(fr, fr, gb.unsqueeze(2).to_broadcast([P, HH, HC]), ALU.mult))
                    did(V.tensor_tensor(fixrow[:, 0:2 * D], fixrow[:, 0:2 * D], fixtmp[:, 0:2 * D], ALU.add))
                    did(V.tensor_tensor(sc, rc[:, :, HC], ga, ALU.mult))
                    did(V.tensor_tensor(fixrow[:, S_:SW], fixrow[:, S_:SW], gb, ALU.mult))
                    did(V.tensor_tensor(fixrow[:, S_:SW], fixrow[:, S_:SW], sc, ALU.add))
                    did(V.tensor_tensor(fixrow[:, X_:M_], fixrow[:, X_:M_], bank[:, 5, 0:D], ALU.add))
                    V.tensor_copy(fixrow[:, M_:S_], m1).then_inc(s_carry_v, 1)


def kernel(**inputs):
    import concourse.bacc as bacc
    from concourse.bass_utils import run_bass_kernel_spmd

    x = {k: np.asarray(v) for k, v in inputs.items()}

    def rows(v):
        return np.broadcast_to(v[None, :], (P, D))

    def column(v):
        return np.broadcast_to(v.reshape(-1)[:, None], (P, D))

    def padded(v, fill):
        return np.concatenate([v, np.full((P * COLS - v.shape[0],), fill, v.dtype)]).reshape(P, COLS)

    g = {k[len("L2_gnn_"):]: v for k, v in x.items() if k.startswith("L2_gnn_")}
    fus = g["fus_w"]
    mats = dict(W0=x["L0_gnn_W0"], W1=x["L0_gnn_W1"], W2=x["L0_gnn_W2"], L1_W=x["L1_gnn_W"],
                L1_Wself=x["L1_gnn_W_self"], gat_w=g["gat_w"], gat_wT=g["gat_w"].T, sage_wl=g["sage_wl"],
                sage_wr=g["sage_wr"], wq=g["tr_wq"], wqT=g["tr_wq"].T, wk=g["tr_wk"], wv=g["tr_wv"],
                wskipT=g["tr_wskip"].T, F1=fus[0:D], F2=fus[D:2 * D], F3=fus[2 * D:3 * D],
                Wn1T=x["L3_gnn_W_neigh1"].T, Ws1T=x["L3_gnn_W_self1"].T, Wn2T=x["L3_gnn_W_neigh2"].T,
                Ws2T=x["L3_gnn_W_self2"].T, gat_b_col=column(g["gat_b"]), bskip_col=column(g["tr_bskip"]),
                bq_col=column(g["tr_bq"]))
    vecs = dict(b0=x["L0_gnn_b0"], b1=x["L0_gnn_b1"], b2=x["L0_gnn_b2"], sage_bl=g["sage_bl"], bq=g["tr_bq"],
                fus_b=g["fus_b"], ln_g=g["ln_g"], ln_b=g["ln_b"], bv=g["tr_bv"], bn1=x["L3_gnn_b_neigh1"],
                bs1=x["L3_gnn_b_self1"], bn2=x["L3_gnn_b_neigh2"], bs2=x["L3_gnn_b_self2"])
    part = np.arange(P)
    arrays = {
        "x": np.concatenate([x["x"], np.zeros((ROWS - N, D), x["x"].dtype)]),
        "src": padded(x["src"], 0), "dst": padded(x["dst"], N),
        "mats": np.stack([mats[n] for n in MATS], axis=1), "vecs": np.stack([rows(vecs[n]) for n in VECS], axis=1),
        "attc": np.stack([g["gat_att_src"].reshape(-1), g["gat_att_dst"].reshape(-1), g["tr_bk"]], axis=1),
        "row0": (part[:, None] + 0 * part[None, :] == 0).astype(np.float32),
        "ident": np.eye(P, dtype=np.float32),
        "upper": np.triu(np.ones((P, P), np.float32), 1), "lower": np.tril(np.ones((P, P), np.float32), -1),
        "hmask": (part[:, None] // HC == np.arange(HEADS)[None, :]).astype(np.float32),
        "iota": np.tile(np.arange(COLS, dtype=np.float16), (P, 1)),
        "emptyrow": (ROWS + part[:, None]).astype(np.float32),
        "firstrow": (part[:, None] * COLS - 1).astype(np.float32),
    }
    nc = bacc.Bacc("TRN2", target_bir_lowering=False, num_devices=1)
    args, feed = {}, {}
    for name, arr in arrays.items():
        arr = np.ascontiguousarray(arr)
        feed["in_" + name] = arr
        args[name] = nc.dram_tensor("in_" + name, arr.shape, mybir.dt.from_np(arr.dtype), kind="ExternalInput").ap()
    out = nc.dram_tensor("out_0", (ROWS, D), mybir.dt.float32, kind="ExternalOutput").ap()
    gnn_kernel(nc, args, out)
    r = run_bass_kernel_spmd(nc, [feed], core_ids=[0])
    return r.results[0]["out_0"][0:N]
```
